# Optimizing a Trainium2 kernel written in Bass

```python
import numpy as np
import jax
import jax.numpy as jnp

def _softmax(x, axis=-1):
    return jax.nn.softmax(x, axis=axis)

def _gelu(x):
    return jax.nn.gelu(x, approximate=True)

def _silu(x):
    return jax.nn.silu(x)

def _sigmoid(x):
    return jax.nn.sigmoid(x)

def _layernorm(x, axis=-1, eps=1e-05):
    m = jnp.mean(x, axis=axis, keepdims=True)
    v = jnp.var(x, axis=axis, keepdims=True)
    return (x - m) / jnp.sqrt(v + eps)

def _scatter_add(tgt, idx, src, axis=0):
    return tgt.at[idx].add(src)

def _segment_sum(src, seg, n):
    return jax.ops.segment_sum(src, seg, n)
kernel_name = 'mk_gnn_resnorm_d4_gnn_r16_c5928b'

def setup_inputs(seed: int=0):
    np.random.seed(seed)
    _w = jnp.asarray

    def _rec_inputs():
        import jax
        import jax.numpy as jnp
        _gk = jax.random.key(seed)
        x = -0.000202 + 1 * jax.random.normal(jax.random.fold_in(_gk, 1), (3125, 64), jnp.float32)
        src = jax.random.randint(jax.random.fold_in(_gk, 2), (100000,), 0, 3125, jnp.int32)
        dst = jax.random.randint(jax.random.fold_in(_gk, 3), (100000,), 0, 3125, jnp.int32)
        _o = jnp.argsort(dst, stable=True)
        src = src[_o]
        dst = dst[_o]
        edge_attr_128 = 2.93046e-05 + 1.00006 * jax.random.normal(jax.random.fold_in(_gk, 12), (100000, 128), jnp.float32)
        edge_attr_64 = -2.25437e-05 + 0.999858 * jax.random.normal(jax.random.fold_in(_gk, 13), (100000, 64), jnp.float32)
        edge_type_32 = jax.random.randint(jax.random.fold_in(_gk, 15), (100000,), 0, 32, jnp.int32)
        return (x, src, dst, edge_attr_128, edge_attr_64, edge_type_32)
    x, src, dst, edge_attr_128, edge_attr_64, edge_type_32 = _rec_inputs()

    def _L0_gnn_setup():
        import jax, jax.numpy as jnp
        import numpy as np
        NEG_SLOPE = 0.01
        N, E, D, R = (6250, 62500, 64, 32)
        key = jax.random.key(seed)
        ks = jax.random.split(key, 8)
        return {'nfeat': jax.random.normal(ks[0], (N, D), dtype=jnp.float32), 'efeat': jax.random.normal(ks[1], (E, D), dtype=jnp.float32), 'src': jax.random.randint(ks[2], (E,), 0, N, dtype=jnp.int32), 'dst': jax.random.randint(ks[3], (E,), 0, N, dtype=jnp.int32), 'etype': jax.random.randint(ks[4], (E,), 0, R, dtype=jnp.int32), 'relation_weight': jax.random.normal(ks[5], (R, D, D), dtype=jnp.float32) * 0.05, 'res_w1': jax.random.normal(ks[6], (D, D), dtype=jnp.float32) * 0.05, 'res_w2': jax.random.normal(ks[7], (D, D), dtype=jnp.float32) * 0.05}
    _L0_gnn_all = _L0_gnn_setup()
    _L0_gnn_in = {k: v for k, v in _L0_gnn_all.items() if k in ('relation_weight', 'res_w1', 'res_w2')}
    del _L0_gnn_all

    def _L1_gnn_setup():
        import jax, jax.numpy as jnp
        import numpy as np
        N_NODES = 6250

        def _gcn_norm(row, col, n_nodes, dtype):
            ones = jnp.ones(row.shape[0], dtype=dtype)
            deg = jax.ops.segment_sum(ones, col, num_segments=n_nodes)
            dinv = jnp.where(deg > 0, jax.lax.rsqrt(jnp.where(deg > 0, deg, 1.0)), 0.0)
            return dinv[row] * dinv[col]
        key = jax.random.key(seed)
        k1, k2 = jax.random.split(key)
        x = jax.random.normal(k1, (N_NODES, 64), dtype=jnp.float32)
        edge_index = jax.random.randint(k2, (2, 100000), 0, N_NODES, dtype=jnp.int64)
        return {'x': x, 'edge_index': edge_index, 'num_steps': 4}
    _L1_gnn_all = _L1_gnn_setup()
    _L1_gnn_in = {k: v for k, v in _L1_gnn_all.items() if k in ()}
    del _L1_gnn_all

    def _L2_gnn_setup():
        import jax, jax.numpy as jnp
        import numpy as np
        N_NODES = 2500
        N_EDGES = 40000
        CH = 64
        DIM = 128
        Z = 2 * CH + DIM
        key = jax.random.key(seed)
        ks = jax.random.split(key, 7)
        x = jax.random.normal(ks[0], (N_NODES, CH), dtype=jnp.float32)
        edge_index = jax.random.randint(ks[1], (2, N_EDGES), 0, N_NODES, dtype=jnp.int32)
        edge_attr = jax.random.normal(ks[2], (N_EDGES, DIM), dtype=jnp.float32)
        W_f = jax.random.normal(ks[3], (Z, CH), dtype=jnp.float32) * (1.0 / np.sqrt(Z))
        b_f = jnp.zeros((CH,), dtype=jnp.float32)
        W_s = jax.random.normal(ks[4], (Z, CH), dtype=jnp.float32) * (1.0 / np.sqrt(Z))
        b_s = jnp.zeros((CH,), dtype=jnp.float32)
        return {'x': x, 'edge_index': edge_index, 'edge_attr': edge_attr, 'W_f': W_f, 'b_f': b_f, 'W_s': W_s, 'b_s': b_s}
    _L2_gnn_all = _L2_gnn_setup()
    _L2_gnn_in = {k: v for k, v in _L2_gnn_all.items() if k in ('W_f', 'b_f', 'W_s', 'b_s')}
    del _L2_gnn_all

    def _L3_gnn_setup():
        import jax, jax.numpy as jnp
        import numpy as np
        H = 5
        NEG_SLOPE = 0.2
        N_NODES = 3125
        N_EDGES = 25000
        IN_CH = 64
        OUT_CH = 64

        def gatv2_layer(x, src, dst, Wl, bl, Wr, br, att, bias, n_nodes):
            C = att.shape[1]
            xl = (x @ Wl + bl).reshape(n_nodes, H, C)
            xr = (x @ Wr + br).reshape(n_nodes, H, C)
            e = jax.nn.leaky_relu(xl[src] + xr[dst], NEG_SLOPE)
            alpha = jnp.einsum('ehc,hc->eh', e, att)
            m = jax.ops.segment_max(alpha, dst, num_segments=n_nodes)
            m = jnp.where(jnp.isfinite(m), m, 0.0)
            a = jnp.exp(alpha - m[dst])
            denom = jax.ops.segment_sum(a, dst, num_segments=n_nodes)
            a = a / (denom[dst] + 1e-16)
            out = jax.ops.segment_sum(a[:, :, None] * xl[src], dst, num_segments=n_nodes)
            return out.mean(axis=1) + bias
        key = jax.random.key(seed)
        ks = jax.random.split(key, 17)
        s = 0.05
        inp = {'x': jax.random.normal(ks[0], (N_NODES, IN_CH), jnp.float32), 'edge_index': jax.random.randint(ks[1], (2, N_EDGES), 0, N_NODES, jnp.int64), 'W1l': jax.random.normal(ks[2], (IN_CH, H * IN_CH), jnp.float32) * s, 'b1l': jnp.zeros((H * IN_CH,), jnp.float32), 'W1r': jax.random.normal(ks[3], (IN_CH, H * IN_CH), jnp.float32) * s, 'b1r': jnp.zeros((H * IN_CH,), jnp.float32), 'att1': jax.random.normal(ks[4], (H, IN_CH), jnp.float32) * s, 'bias1': jnp.zeros((IN_CH,), jnp.float32), 'W2l': jax.random.normal(ks[5], (IN_CH, H * OUT_CH), jnp.float32) * s, 'b2l': jnp.zeros((H * OUT_CH,), jnp.float32), 'W2r': jax.random.normal(ks[6], (IN_CH, H * OUT_CH), jnp.float32) * s, 'b2r': jnp.zeros((H * OUT_CH,), jnp.float32), 'att2': jax.random.normal(ks[7], (H, OUT_CH), jnp.float32) * s, 'bias2': jnp.zeros((OUT_CH,), jnp.float32), 'Wfc': jax.random.normal(ks[8], (OUT_CH, OUT_CH), jnp.float32) * s, 'bfc': jnp.zeros((OUT_CH,), jnp.float32)}
        return inp
    _L3_gnn_all = _L3_gnn_setup()
    _L3_gnn_in = {k: v for k, v in _L3_gnn_all.items() if k in ('W1l', 'b1l', 'W1r', 'b1r', 'att1', 'bias1', 'W2l', 'b2l', 'W2r', 'b2r', 'att2', 'bias2', 'Wfc', 'bfc')}
    del _L3_gnn_all
    return {'x': x, 'src': src, 'dst': dst, 'edge_attr_128': edge_attr_128, 'edge_attr_64': edge_attr_64, 'edge_type_32': edge_type_32, 'L0_gnn_relation_weight': _L0_gnn_in['relation_weight'], 'L0_gnn_res_w1': _L0_gnn_in['res_w1'], 'L0_gnn_res_w2': _L0_gnn_in['res_w2'], 'L2_gnn_W_f': _L2_gnn_in['W_f'], 'L2_gnn_b_f': _L2_gnn_in['b_f'], 'L2_gnn_W_s': _L2_gnn_in['W_s'], 'L2_gnn_b_s': _L2_gnn_in['b_s'], 'L3_gnn_W1l': _L3_gnn_in['W1l'], 'L3_gnn_b1l': _L3_gnn_in['b1l'], 'L3_gnn_W1r': _L3_gnn_in['W1r'], 'L3_gnn_b1r': _L3_gnn_in['b1r'], 'L3_gnn_att1': _L3_gnn_in['att1'], 'L3_gnn_bias1': _L3_gnn_in['bias1'], 'L3_gnn_W2l': _L3_gnn_in['W2l'], 'L3_gnn_b2l': _L3_gnn_in['b2l'], 'L3_gnn_W2r': _L3_gnn_in['W2r'], 'L3_gnn_b2r': _L3_gnn_in['b2r'], 'L3_gnn_att2': _L3_gnn_in['att2'], 'L3_gnn_bias2': _L3_gnn_in['bias2'], 'L3_gnn_Wfc': _L3_gnn_in['Wfc'], 'L3_gnn_bfc': _L3_gnn_in['bfc']}

def reference(x, src, dst, edge_attr_128, edge_attr_64, edge_type_32, L0_gnn_relation_weight, L0_gnn_res_w1, L0_gnn_res_w2, L2_gnn_W_f, L2_gnn_b_f, L2_gnn_W_s, L2_gnn_b_s, L3_gnn_W1l, L3_gnn_b1l, L3_gnn_W1r, L3_gnn_b1r, L3_gnn_att1, L3_gnn_bias1, L3_gnn_W2l, L3_gnn_b2l, L3_gnn_W2r, L3_gnn_b2r, L3_gnn_att2, L3_gnn_bias2, L3_gnn_Wfc, L3_gnn_bfc):
    import jax
    import jax.numpy as jnp

    def _L0_gnn_ref(nfeat, efeat, src, dst, etype, relation_weight, res_w1, res_w2):
        import jax, jax.numpy as jnp
        import numpy as np
        NEG_SLOPE = 0.01
        N, D = nfeat.shape
        h = nfeat
        h_proj = jnp.einsum('nd,rde->rne', h, relation_weight)
        t_r = h_proj[etype, src]
        h_r = h_proj[etype, dst]
        att = jnp.sum(t_r * jnp.tanh(h_r + efeat), axis=-1)
        seg_max = jax.lax.stop_gradient(jax.ops.segment_max(att, dst, num_segments=N))
        att_exp = jnp.exp(att - seg_max[dst])
        denom = jax.ops.segment_sum(att_exp, dst, num_segments=N)
        a = att_exp / denom[dst]
        msg = h[src] * a[:, None]
        h_nb = jax.ops.segment_sum(msg, dst, num_segments=N)
        out = jax.nn.leaky_relu((h + h_nb) @ res_w1.T, NEG_SLOPE) + jax.nn.leaky_relu(h * h_nb @ res_w2.T, NEG_SLOPE)
        return out

    def _L1_gnn_ref(x, edge_index, num_steps):
        import jax, jax.numpy as jnp
        import numpy as np
        N_NODES = 6250

        def _gcn_norm(row, col, n_nodes, dtype):
            ones = jnp.ones(row.shape[0], dtype=dtype)
            deg = jax.ops.segment_sum(ones, col, num_segments=n_nodes)
            dinv = jnp.where(deg > 0, jax.lax.rsqrt(jnp.where(deg > 0, deg, 1.0)), 0.0)
            return dinv[row] * dinv[col]
        row, col = (edge_index[0], edge_index[1])
        n_nodes = x.shape[0]
        for _ in range(num_steps):
            w = _gcn_norm(row, col, n_nodes, x.dtype)
            msgs = w[:, None] * x[row]
            x = jax.ops.segment_sum(msgs, col, num_segments=n_nodes)
        return x

    def _L2_gnn_ref(x, edge_index, edge_attr, W_f, b_f, W_s, b_s):
        import jax, jax.numpy as jnp
        import numpy as np
        N_NODES = 2500
        N_EDGES = 40000
        CH = 64
        DIM = 128
        Z = 2 * CH + DIM
        src, dst = (edge_index[0], edge_index[1])
        z = jnp.concatenate([x[dst], x[src], edge_attr], axis=-1)
        gate = jax.nn.sigmoid(z @ W_f + b_f)
        core = jax.nn.softplus(z @ W_s + b_s)
        msg = gate * core
        agg = jax.ops.segment_sum(msg, dst, num_segments=x.shape[0])
        out = x + agg
        return jax.nn.relu(out)

    def _L3_gnn_ref(x, edge_index, W1l, b1l, W1r, b1r, att1, bias1, W2l, b2l, W2r, b2r, att2, bias2, Wfc, bfc):
        import jax, jax.numpy as jnp
        import numpy as np
        H = 5
        NEG_SLOPE = 0.2
        N_NODES = 3125
        N_EDGES = 25000
        IN_CH = 64
        OUT_CH = 64

        def gatv2_layer(x, src, dst, Wl, bl, Wr, br, att, bias, n_nodes):
            C = att.shape[1]
            xl = (x @ Wl + bl).reshape(n_nodes, H, C)
            xr = (x @ Wr + br).reshape(n_nodes, H, C)
            e = jax.nn.leaky_relu(xl[src] + xr[dst], NEG_SLOPE)
            alpha = jnp.einsum('ehc,hc->eh', e, att)
            m = jax.ops.segment_max(alpha, dst, num_segments=n_nodes)
            m = jnp.where(jnp.isfinite(m), m, 0.0)
            a = jnp.exp(alpha - m[dst])
            denom = jax.ops.segment_sum(a, dst, num_segments=n_nodes)
            a = a / (denom[dst] + 1e-16)
            out = jax.ops.segment_sum(a[:, :, None] * xl[src], dst, num_segments=n_nodes)
            return out.mean(axis=1) + bias
        n = x.shape[0]
        loop = jnp.arange(n, dtype=edge_index.dtype)
        src = jnp.concatenate([edge_index[0], loop])
        dst = jnp.concatenate([edge_index[1], loop])
        h = jax.nn.relu(gatv2_layer(x, src, dst, W1l, b1l, W1r, b1r, att1, bias1, n))
        h = jax.nn.relu(gatv2_layer(h, src, dst, W2l, b2l, W2r, b2r, att2, bias2, n))
        return h @ Wfc + bfc
    edge_index = jnp.stack([src, dst])
    x = _layernorm(x + _L0_gnn_ref(x, edge_attr_64, src, dst, edge_type_32, L0_gnn_relation_weight, L0_gnn_res_w1, L0_gnn_res_w2), axis=-1)
    x = _layernorm(x + _L1_gnn_ref(x, edge_index, 4), axis=-1)
    x = _layernorm(x + _L2_gnn_ref(x, edge_index, edge_attr_128, L2_gnn_W_f, L2_gnn_b_f, L2_gnn_W_s, L2_gnn_b_s), axis=-1)
    x = _layernorm(x + _L3_gnn_ref(x, edge_index, L3_gnn_W1l, L3_gnn_b1l, L3_gnn_W1r, L3_gnn_b1r, L3_gnn_att1, L3_gnn_bias1, L3_gnn_W2l, L3_gnn_b2l, L3_gnn_W2r, L3_gnn_b2r, L3_gnn_att2, L3_gnn_bias2, L3_gnn_Wfc, L3_gnn_bfc), axis=-1)
    return x

_drawn_inputs = setup_inputs


def setup_inputs(seed=0):
    import zlib

    import numpy as np

    out = dict(_drawn_inputs(seed))
    spreads = {'L2_gnn_b_f': (0.0, 0.1),
     'L2_gnn_b_s': (0.0, 0.1),
     'L3_gnn_b1l': (0.0, 0.8),
     'L3_gnn_b1r': (0.0, 0.8),
     'L3_gnn_bias1': (0.0, 0.8),
     'L3_gnn_b2l': (0.0, 0.545),
     'L3_gnn_b2r': (0.0, 0.8),
     'L3_gnn_bias2': (0.0, 0.36),
     'L3_gnn_bfc': (0.0, 0.1)}
    factors = {'L3_gnn_W1l': 8.0,
     'L3_gnn_W1r': 8.0,
     'L3_gnn_att1': 8.0,
     'L3_gnn_W2l': 8.0,
     'L3_gnn_W2r': 8.0,
     'L3_gnn_att2': 8.0}
    for name, (base, spread) in spreads.items():
        noise = np.random.default_rng([zlib.crc32(name.encode()), seed]).standard_normal(out[name].shape)
        drawn = base * np.exp(spread * noise) if base else spread * noise
        out[name] = jnp.asarray(drawn.astype(out[name].dtype))
    for name, factor in factors.items():
        out[name] = (out[name] * factor).astype(out[name].dtype)
    return out
```

```python
from contextlib import ExitStack, contextmanager

import concourse.bass as bass
from concourse import mybir

P = 128
N, D = 3125, 64
E = 100000
R = 32
H = 5
HD = H * D
DE = 128
NB = N // 125
NR = P * NB
J = 784
EP = P * J
BIG = 1.0e38
WHOLE = 1.5 * 2.0 ** 23
LN_EPS = 1.0e-5
K = 28
NCH = J // K

f32 = mybir.dt.float32
bf16 = mybir.dt.bfloat16
i32 = mybir.dt.int32
ALU = mybir.AluOpType
ACT = mybir.ActivationFunctionType
X = mybir.AxisListType.X


class Chain:

    def __init__(self, eng, sem):
        self.eng, self.sem, self.n, self.turn = eng, sem, 0, None

    def count(self):
        return self.n if self.turn is None else self.turn + self.n

    def mark(self, ins):
        self.n += 1
        ins.then_inc(self.sem, 1)
        return self.count()

    def wait(self, at=None):
        self.eng.wait_ge(self.sem, self.count() if at is None else at)

    def link(self, ins):
        self.mark(ins)
        self.wait()

    def begin(self, i, each):
        self.before, self.each, self.turn = self.n, each, i * each

    def end(self, turns):
        assert self.n - self.before == self.each, (self.n - self.before, self.each)
        self.n = self.before + self.each * turns
        self.turn = None


class Space:

    used = {}

    def __init__(self, nc, ctx):
        self.nc, self.ctx, self.sems = nc, ctx, []

    def sb(self, name, shape, dt=f32):
        return self.ctx.enter_context(self.nc.sbuf_tensor(self.own(name), shape, dt))

    def ps(self, name, shape, dt=f32):
        return self.ctx.enter_context(self.nc.psum_tensor(self.own(name), shape, dt))

    def sem(self, name):
        self.sems.append(self.ctx.enter_context(self.nc.semaphore(self.own(name))))
        return self.sems[-1]

    def pool_sem(self, g, n):
        self.sems.append(g.pool_sems[n])
        return g.pool_sems[n]

    def own(self, name):
        used = Space.used
        used[name] = used.get(name, 0) + 1
        return name if used[name] == 1 else f"{name}_{used[name]}"


@contextmanager
def phase(nc):
    with ExitStack() as ctx:
        s = Space(nc, ctx)
        yield s
        with nc.Block() as block:
            @block.gpsimd
            def _(pool):
                pool.dma_reset()
                for sem in s.sems:
                    pool.sem_clear(sem)


def setup(nc, g, a):
    g.srcI, g.dstI = g.sb("srcI", [P, J], i32), g.sb("dstI", [P, J], i32)
    g.hpS, g.hpD = g.sb("hpS", [P, J], i32), g.sb("hpD", [P, J], i32)
    g.cont, g.isend, g.notend = g.sb("cont", [P, J]), g.sb("isend", [P, J]), g.sb("notend", [P, J])
    g.Lm, g.Rm = g.sb("Lm", [P, J]), g.sb("Rm", [P, J])
    g.x = g.sb("x", [P, NB, D])
    g.ident = g.sb("ident", [P, P])
    g.contLrow, g.contRrow = g.sb("contLrow", [P, P]), g.sb("contRrow", [P, P])
    g.dinv, g.has, g.nothas = g.sb("dinv", [P, NB]), g.sb("has", [P, NB]), g.sb("nothas", [P, NB])
    g.idxEnd, g.idxCar = g.sb("idxEnd", [P, NB], i32), g.sb("idxCar", [P, NB], i32)
    g.idxStart, g.row0 = g.sb("idxStart", [P, NB], i32), g.sb("row0", [P, 1], i32)
    with phase(nc) as s:
        etI = s.sb("etI", [P, J], i32)
        edge_rows = s.sb("edge_rows", [P, 2], i32)
        dstF = s.sb("dstF", [P, J])
        dstP = s.sb("dstP", [P, J])
        dstB = s.sb("dstB", [P, J])
        nbr = s.sb("nbr", [P, 2])
        iotaI = s.sb("iotaI", [P, P], i32)
        iotaF = s.sb("iotaF", [P, P])
        nodeI = s.sb("nodeI", [P, NB], i32)
        nodeF = s.sb("nodeF", [P, NB])
        ones = s.sb("ones", [P, P])
        lower = s.sb("lower", [P, P])
        diag = s.sb("diag", [P, 2, P])
        zero = s.sb("zero", [P, P], bf16)
        hotP = s.sb("hotP", [P, 2, K, P], bf16)
        hotB = s.sb("hotB", [P, 2, K, NB], bf16)
        cols = s.sb("cols", [P, 2, 2, K])
        w = s.sb("w", [P, 12, NB])
        psC = s.ps("psC", [P, 512])
        psR = s.ps("psR", [P, 2, 256])
        psE = s.ps("psE", [P, 512])
        loaded = s.sem("loaded")
        cleared = s.sem("cleared")
        made = s.sem("made")
        dve = s.sem("dve")
        hot = [s.sem(f"hot{k}") for k in range(2)]
        counted = [s.sem(f"counted{k}") for k in range(2)]
        split = s.sem("split")
        rows = s.sem("rows")
        total = s.sem("total")
        sq = s.sem("sq")
        sqd = s.sem("sqd")
        zeroed = s.sem("zeroed")
        with nc.Block() as block:
            @block.sync
            def _(sp):
                sp.dma_start(g.srcI[:, :], a["src"].rearrange("(p j) -> p j", p=P)).then_inc(loaded, 16)
                sp.dma_start(g.dstI[:, :], a["dst"].rearrange("(p j) -> p j", p=P)).then_inc(loaded, 16)
                sp.dma_start(etI[:, :], a["et"].rearrange("(p j) -> p j", p=P)).then_inc(loaded, 16)
                d2 = a["dst"].rearrange("(p j) -> p j", p=P)
                sp.wait_ge(cleared, 2)
                sp.dma_start(edge_rows[1:P, 0:1], d2[0:P - 1, J - 1:J],
                             allow_slow_non_contiguous=True).then_inc(loaded, 16)
                sp.dma_start(edge_rows[0:P - 1, 1:2], d2[1:P, 0:1],
                             allow_slow_non_contiguous=True).then_inc(loaded, 16)
                sp.dma_start(g.x[0:N // NB], a["x"].rearrange("(p b) d -> p b d", b=NB)).then_inc(loaded, 16)
                sp.wait_ge(loaded, 6 * 16)

            @block.gpsimd
            def _(pool):
                pool.memset(edge_rows[:, :], -1).then_inc(cleared, 1)
                pool.memset(g.x[:, :, :], 0.0).then_inc(cleared, 1)
                pool.memset(ones[:, :], 1.0).then_inc(made, 1)
                pool.memset(g.ident[:, :], 0.0).then_inc(made, 1)
                pool.wait_ge(made, 2)
                pool.affine_select(out=g.ident[:, :], in_=g.ident[:, :], compare_op=ALU.not_equal, fill=1.0,
                                   base=0, pattern=[[-1, P]], channel_multiplier=1).then_inc(made, 1)
                pool.affine_select(out=lower[:, :], in_=ones[:, :], compare_op=ALU.is_gt, fill=0.0,
                                   base=0, pattern=[[1, P]], channel_multiplier=-1).then_inc(made, 1)
                pool.iota(iotaI[:, :], pattern=[[1, P]], base=0, channel_multiplier=0).then_inc(made, 1)
                pool.iota(nodeI[:, :], pattern=[[1, NB]], base=0, channel_multiplier=NB).then_inc(made, 1)
                pool.memset(zero[:, :], 0.0).then_inc(made, 1)
                pool.wait_ge(made, 7)

            @block.vector
            def _(v):
                c = Chain(v, dve)
                v.wait_ge(loaded, 6 * 16)
                v.wait_ge(made, 7)
                v.tensor_copy(iotaF[:, :], iotaI[:, :]).then_inc(dve, 1)
                v.tensor_copy(nodeF[:, :], nodeI[:, :]).then_inc(dve, 1)
                c.n = 2
                c.mark(v.tensor_copy(nbr[:, :], edge_rows[:, :]))
                c.link(v.tensor_copy(dstF[:, :], g.dstI[:, :]))
                c.mark(v.tensor_scalar(g.Lm[:, :], dstF[:, :], nbr[:, 0:1], None, ALU.is_equal))
                c.mark(v.tensor_scalar(g.Rm[:, :], dstF[:, :], nbr[:, 1:2], None, ALU.is_equal))
                c.mark(v.tensor_tensor(g.cont[:, 1:J], dstF[:, 1:J], dstF[:, 0:J - 1], ALU.is_equal))
                c.mark(v.tensor_tensor(g.cont[:, 0:1], dstF[:, 0:1], nbr[:, 0:1], ALU.is_equal))
                c.mark(v.tensor_tensor(g.isend[:, 0:J - 1], dstF[:, 1:J], dstF[:, 0:J - 1], ALU.not_equal))
                c.mark(v.memset(g.isend[:, J - 1:J], 1.0))
                c.mark(v.scalar_tensor_tensor(g.hpS[:, :], g.srcI[:, :], float(R), etI[:, :], ALU.mult, ALU.add))
                c.mark(v.scalar_tensor_tensor(g.hpD[:, :], g.dstI[:, :], float(R), etI[:, :], ALU.mult, ALU.add))
                c.mark(v.tensor_copy(g.row0[:, :], g.dstI[:, 0:1]))
                c.link(v.tensor_scalar(dstP[:, :], dstF[:, :], 1.0 / NB, -0.48, ALU.mult, ALU.add))
                c.mark(v.tensor_scalar(g.notend[:, :], g.isend[:, :], -1.0, 1.0, ALU.mult, ALU.add))
                c.link(v.tensor_scalar(dstP[:, :], dstP[:, :], WHOLE, -WHOLE, ALU.add, ALU.add))
                c.link(v.scalar_tensor_tensor(dstB[:, :], dstP[:, :], -float(NB), dstF[:, :], ALU.mult, ALU.add))
                c.mark(v.tensor_scalar(diag[:, 0, :], g.ident[:, :], g.Lm[:, J - 1:J], None, ALU.mult))
                c.link(v.tensor_scalar(diag[:, 1, :], g.ident[:, :], g.Rm[:, 0:1], None, ALU.mult))
                v.sem_inc(split, 1)
                with v.Fori(0, NCH // 2) as i:
                    c.begin(i, 4)
                    for k in range(2):
                        v.wait_ge(counted[k], i + 1)
                        c.mark(v.tensor_copy(cols[:, k, 0, :], dstP[:, bass.ds((i * 2 + k) * K, K)]))
                        c.link(v.tensor_copy(cols[:, k, 1, :], dstB[:, bass.ds((i * 2 + k) * K, K)]))
                        v.tensor_tensor(hotP[:, k], cols[:, k, 0, :].unsqueeze(2).to_broadcast([P, K, P]),
                                        iotaF[:, :].unsqueeze(1).to_broadcast([P, K, P]), ALU.is_equal).then_inc(hot[k], 1)
                        v.tensor_tensor(hotB[:, k], cols[:, k, 1, :].unsqueeze(2).to_broadcast([P, K, NB]),
                                        iotaF[:, 0:NB].unsqueeze(1).to_broadcast([P, K, NB]), ALU.is_equal).then_inc(hot[k], 1)
                c.end(NCH // 2)
                deg, cum, tot, start, has = (w[:, n, :] for n in range(5))
                t1, q, cross, end, t2 = (w[:, n, :] for n in range(5, 10))
                v.wait_ge(rows, 1)
                c.mark(v.tensor_copy(g.contLrow[:, :], psR[:, 0, 0:P]))
                c.mark(v.tensor_copy(g.contRrow[:, :], psR[:, 1, 0:P]))
                v.wait_ge(rows, 2)
                c.link(v.tensor_copy(deg, psC[:, 0:NB]))
                c.link(v.tensor_tensor_scan(cum, ones[:, 0:NB], deg, 0.0, ALU.mult, ALU.add))
                c.link(v.tensor_copy(tot[:, 0:1], cum[:, NB - 1:NB]))
                v.sem_inc(total, 1)
                v.wait_ge(rows, 3)
                c.link(v.tensor_copy(tot[:, 1:2], psE[:, 0:1]))
                c.link(v.tensor_scalar(end, cum, tot[:, 1:2], -1.0, ALU.add, ALU.add))
                c.link(v.scalar_tensor_tensor(start, deg, -1.0, end, ALU.mult, ALU.add))
                c.link(v.tensor_scalar(start, start, 1.0, None, ALU.add))
                c.link(v.tensor_scalar(has, deg, 0.0, None, ALU.is_gt))
                c.mark(v.tensor_copy(g.has[:, :], has))
                c.mark(v.tensor_scalar(g.nothas[:, :], has, -1.0, 1.0, ALU.mult, ALU.add))
                c.link(v.tensor_scalar(t1, deg, 1.0, None, ALU.max))
                v.sem_inc(sq, 1)
                c.link(v.tensor_scalar(q, end, 1.0 / J, -(0.5 - 0.5 / J), ALU.mult, ALU.add))
                c.link(v.tensor_scalar(q, q, WHOLE, -WHOLE, ALU.add, ALU.add))
                c.link(v.scalar_tensor_tensor(cross, q, float(J), start, ALU.mult, ALU.is_gt))
                c.link(v.tensor_tensor(cross, cross, has, ALU.mult))
                c.link(v.tensor_tensor(cross, cross, q, ALU.mult))
                c.mark(v.tensor_copy(g.idxCar[:, :], cross))
                c.link(v.tensor_scalar(t2, end, -float(EP), None, ALU.add))
                c.link(v.tensor_tensor(t2, t2, has, ALU.mult))
                c.link(v.tensor_scalar(t2, t2, float(EP), None, ALU.add))
                c.link(v.tensor_copy(g.idxEnd[:, :], t2))
                c.link(v.tensor_scalar(nodeF[:, :], nodeF[:, :], float(EP), None, ALU.add))
                c.link(v.tensor_tensor(t2, start, nodeF[:, :], ALU.subtract))
                c.link(v.tensor_tensor(t2, t2, has, ALU.mult))
                c.link(v.tensor_tensor(t2, t2, nodeF[:, :], ALU.add))
                c.link(v.tensor_copy(g.idxStart[:, :], t2))
                v.wait_ge(sqd, 1)
                c.link(v.reciprocal(g.dinv[:, :], g.dinv[:, :]))
                c.link(v.tensor_tensor(g.dinv[:, :], g.dinv[:, :], has, ALU.mult))

            @block.scalar
            def _(act):
                act.wait_ge(sq, 1)
                act.activation(g.dinv[:, :], w[:, 5, :], ACT.Sqrt).then_inc(sqd, 1)

            @block.tensor
            def _(pe):
                pe.sem_inc(counted[0], 1)
                pe.sem_inc(counted[1], 1)
                pe.wait_ge(made, 7)
                pe.wait_ge(split, 1)
                pe.matmul(psR[:, 0, 0:P], ones[:, :], diag[:, 0, :], start=True, stop=True)
                pe.matmul(psR[:, 1, 0:P], ones[:, :], diag[:, 1, :], start=True, stop=True).then_inc(rows, 1)
                pe.matmul(psC[:, 0:NB], zero[:, :], zero[:, 0:NB], start=True, stop=False, skip_group_check=True)
                with pe.Fori(0, NCH // 2) as i:
                    for k in range(2):
                        pe.wait_ge(hot[k], i * 2 + 2)
                        for j in range(K):
                            last = pe.matmul(psC[:, 0:NB], hotP[:, k, j, :], hotB[:, k, j, :], start=False,
                                             stop=False, skip_group_check=True)
                        last.then_inc(counted[k], 1)
                pe.matmul(psC[:, 0:NB], zero[:, :], zero[:, 0:NB], start=False, stop=True,
                          skip_group_check=True).then_inc(rows, 1)
                pe.wait_ge(total, 1)
                pe.matmul(psE[:, 0:1], lower[:, :], w[:, 2, 0:1], start=True, stop=True).then_inc(rows, 1)


def relation_table(nc, g, a):
    with phase(nc) as s:
        w = s.sb("relw", [D, R * D])
        xT = s.sb("xT", [D, 2, P])
        stage = s.sb("stage", [P, 2, R, 2 * D])
        zero = s.sb("zerof", [P, 3236])
        psT = s.ps("psT", [D, 2, 512])
        psH = s.ps("psH", [P, 2, 1024])
        loaded, zeroed, zeros = s.sem("w_loaded"), s.sem("zeroed"), s.sem("zeros_stored")
        turned, xT_ready, x_put = s.sem("turned"), s.sem("xT_ready"), s.sem("x_put")
        made = [s.sem(f"half_made{h}") for h in range(2)]
        evac = [s.sem(f"half_out{h}") for h in range(2)]
        stored = [s.sem(f"hpx_stored{k}") for k in range(2)]
        with nc.Block() as block:
            @block.sync
            def _(sp):
                sp.dma_start(w[:, :].rearrange("d (r e) -> d r e", r=R),
                             a["relw"].rearrange("r d e -> d r e")).then_inc(loaded, 16)
                for b in range(NB):
                    sp.wait_ge(evac[0], b + 1)
                    sp.wait_ge(evac[1], b + 1)
                    sp.wait_ge(x_put, b + 1)
                    sp.dma_start(g.hpx[0:NR * R, :].rearrange("(p b r) c -> p b (r c)", b=NB, r=R)[:, b, :],
                                 stage[:, b % 2].rearrange("p r c -> p (r c)")).then_inc(stored[b % 2], 16)
                for k in range(2):
                    sp.wait_ge(stored[k], 16 * ((NB + 1 - k) // 2))

            @block.gpsimd
            def _(pool):
                pool.memset(zero[:, :], 0.0).then_inc(zeroed, 1)
                for b in range(NB):
                    if b >= 2:
                        pool.wait_ge(stored[b % 2], 16 * (b // 2))
                    pool.tensor_copy(stage[:, b % 2, :, D:2 * D],
                                     g.x[:, b, :].unsqueeze(1).to_broadcast([P, R, D])).then_inc(x_put, 1)

            @block.tensor
            def _(pe):
                for b in range(NB):
                    pe.transpose(psT[:, b % 2, 0:P], g.x[:, b, :], g.ident[:, :]).then_inc(turned, 1)
                    pe.wait_ge(xT_ready, b + 1)
                    if b == 0:
                        pe.wait_ge(loaded, 16)
                    for h in range(2):
                        if b >= 1:
                            pe.wait_ge(evac[h], b)
                        for q in range(2):
                            last = pe.matmul(psH[:, h, q * 512:(q + 1) * 512], xT[:, b % 2, :],
                                             w[:, (2 * h + q) * 512:(2 * h + q + 1) * 512], start=True, stop=True)
                        last.then_inc(made[h], 1)

            @block.scalar
            def _(act):
                act.wait_ge(zeroed, 1)
                z = zero.shape[1]
                for n in range(16):
                    act.dma_start(g.start_rows.rearrange("(p j) c -> p (j c)", p=P)[:, n * z:(n + 1) * z],
                                  zero[:, :]).then_inc(zeros, 16)
                act.dma_start(g.start_self.rearrange("(p j) c -> p (j c)", p=P)[:, 0:2048],
                              zero[:, 0:2048]).then_inc(zeros, 16)
                act.dma_start(g.start_self.rearrange("(p j) c -> p (j c)", p=P)[:, 2048:4045],
                              zero[:, 0:1997]).then_inc(zeros, 16)
                act.dma_start(g.scanned[EP:EP + P, :], zero[:, 0:D]).then_inc(zeros, 16)
                act.dma_start(g.self_weight[EP:EP + P, :], zero[:, 0:H]).then_inc(zeros, 16)
                for b in range(NB):
                    act.wait_ge(turned, b + 1)
                    if b >= 2:
                        act.wait_ge(made[1], b - 1)
                    act.activation(xT[:, b % 2, :], psT[:, b % 2, 0:P], ACT.Copy).then_inc(xT_ready, 1)
                    act.wait_ge(made[0], b + 1)
                    if b >= 2:
                        act.wait_ge(stored[b % 2], 16 * (b // 2))
                    act.activation(stage[:, b % 2, 0:R // 2, 0:D],
                                   psH[:, 0, :].rearrange("p (r e) -> p r e", e=D), ACT.Copy).then_inc(evac[0], 1)
                act.wait_ge(zeros, 16 * 20)

            @block.vector
            def _(v):
                for b in range(NB):
                    v.wait_ge(made[1], b + 1)
                    if b >= 2:
                        v.wait_ge(stored[b % 2], 16 * (b // 2))
                    v.tensor_copy(stage[:, b % 2, R // 2:R, 0:D],
                                  psH[:, 1, :].rearrange("p (r e) -> p r e", e=D)).then_inc(evac[1], 1)


def gather_columns(pool, table, width, index, stage, buf, c, i, k, done, staged):
    c.link(pool.tensor_copy(stage[:, k, :], index[:, bass.ds((i * 2 + k) * K, K)]))
    pool.sem_inc(staged, 1)
    for j in range(K):
        pool.indirect_dma_start(buf[:, k, j, 0:width] if width == buf.shape[3] else buf[:, k, j, D:2 * D], None,
                                table, bass.IndirectOffsetOnAxis(stage[:, k, j:j + 1], 0)).then_inc(done[k], 16)


def relation_scores(nc, g, a):
    with phase(nc) as s:
        stS, stD = s.sb("stS", [P, 2, K], i32), s.sb("stD", [P, 2, K], i32)
        rows_s, rows_d = s.sb("rows_s", [P, 2, K, 2 * D]), s.sb("rows_d", [P, 2, K, 2 * D])
        ef = s.sb("ef", [P, 2, K, D])
        sc = s.sb("sc", [P, 2, K])
        got_s = [s.pool_sem(g, k) for k in range(2)]
        got_d = [s.pool_sem(g, 2 + k) for k in range(2)]
        edge = [s.sem(f"edge{k}") for k in range(2)]
        stored = [s.sem(f"x_src_stored{k}") for k in range(2)]
        used, kept = [s.sem(f"used{k}") for k in range(2)], [s.sem(f"kept{k}") for k in range(2)]
        summed, tanh, pool_c, dve_c, staged = s.sem("summed"), s.sem("tanh"), s.sem("pool_c"), s.sem("dve_c"), s.sem("staged")
        with nc.Block() as block:
            @block.sync
            def _(sp):
                with sp.Fori(0, NCH // 2) as i:
                    for k in range(2):
                        sp.wait_ge(used[k], i + 1)
                        sp.dma_start(ef[:, k].rearrange("p j c -> p (j c)"),
                                     a["ef"].rearrange("(p j) c -> p (j c)", p=P)[:, bass.ds((i * 2 + k) * (K * D), K * D)]
                                     ).then_inc(edge[k], 16)

            @block.gpsimd
            def _(pool):
                c = Chain(pool, pool_c)
                with pool.Fori(0, NCH // 2) as i:
                    c.begin(i, 4)
                    for k in range(2):
                        pool.wait_ge(used[k], i + 1)
                        pool.wait_ge(kept[k], i + 1)
                        gather_columns(pool, g.hpx, 2 * D, g.hpS, stS, rows_s, c, i, k, got_s, staged)
                        gather_columns(pool, g.hpx, 2 * D, g.hpD, stD, rows_d, c, i, k, got_d, staged)
                c.end(NCH // 2)

            @block.vector
            def _(v):
                c = Chain(v, dve_c)
                for k in range(2):
                    v.sem_inc(used[k], 1)
                with v.Fori(0, NCH // 2) as i:
                    c.begin(i, 4)
                    for k in range(2):
                        v.wait_ge(edge[k], i * 16 + 16)
                        v.wait_ge(got_d[k], i * (16 * K) + 16 * K)
                        v.tensor_tensor(ef[:, k], ef[:, k], rows_d[:, k, :, 0:D], ALU.add).then_inc(summed, 1)
                        v.wait_ge(tanh, i * 2 + k + 1)
                        v.wait_ge(got_s[k], i * (16 * K) + 16 * K)
                        c.link(v.tensor_tensor(ef[:, k], ef[:, k], rows_s[:, k, :, 0:D], ALU.mult))
                        c.link(v.tensor_reduce(sc[:, k, :], ef[:, k], X, ALU.add))
                        v.tensor_copy(g.score[:, 0, bass.ds((i * 2 + k) * K, K)], sc[:, k, :]).then_inc(used[k], 1)
                c.end(NCH // 2)

            @block.scalar
            def _(act):
                for k in range(2):
                    act.sem_inc(kept[k], 1)
                with act.Fori(0, NCH // 2) as i:
                    for k in range(2):
                        act.wait_ge(got_s[k], i * (16 * K) + 16 * K)
                        act.dma_start(g.x_src.rearrange("(p j) c -> p j c", p=P)[:, bass.ds((i * 2 + k) * K, K), :],
                                      rows_s[:, k, :, D:2 * D]).then_inc(stored[k], 16)
                        act.wait_ge(summed, i * 2 + k + 1)
                        act.activation(ef[:, k], ef[:, k], ACT.Tanh).then_inc(tanh, 1)
                        act.wait_ge(stored[k], i * 16 + 16)
                        act.sem_inc(kept[k], 1)


def carry_over(nc, g, s, heads, first, last, out, combine):
    big = combine == ALU.max
    neutral = -BIG if big else 0.0
    flag = s.sb("flag", [P, 2, P])
    left, right = s.sb("left", [D, P + 1]), s.sb("right", [D, P + 1])
    ps = s.ps("ps_carry", [P, 2, P])
    pt = s.ps("ps_carried", [P, 2, D])
    ready, turned, scanned, back, chain = (s.sem(f"carry_{n}") for n in ("ready", "turned", "scanned", "back", "chain"))
    with nc.Block() as block:
        @block.vector
        def _(v):
            c = Chain(v, chain)
            for n, row in enumerate((g.contLrow, g.contRrow)):
                if big:
                    c.mark(v.tensor_scalar(flag[:, n, :], row[:, :], BIG, -BIG, ALU.mult, ALU.add))
                else:
                    c.mark(v.tensor_copy(flag[:, n, :], row[:, :]))
            c.mark(v.memset(left[:, 0:1], neutral))
            c.link(v.memset(right[:, P:P + 1], neutral))
            op = ALU.add if big else ALU.mult
            v.wait_ge(turned, 1)
            v.tensor_tensor_scan(left[0:heads, 1:P + 1], flag[0:heads, 0, :], ps[0:heads, 0, :], neutral, op, combine)
            v.tensor_tensor_scan(right[0:heads, 0:P][:, ::-1], flag[0:heads, 1, ::-1], ps[0:heads, 1, ::-1], neutral,
                                 op, combine).then_inc(scanned, 1)
            v.wait_ge(back, 1)
            c.link(v.tensor_copy(out, pt[:, :, 0:heads]))

        @block.tensor
        def _(pe):
            pe.transpose(ps[0:heads, 0, :], last, g.ident[:, :])
            pe.transpose(ps[0:heads, 1, :], first, g.ident[:, :]).then_inc(turned, 1)
            pe.wait_ge(scanned, 1)
            pe.transpose(pt[:, 0, 0:heads], left[0:heads, 0:P], g.ident[0:heads, 0:heads])
            pe.transpose(pt[:, 1, 0:heads], right[0:heads, 1:P + 1], g.ident[0:heads, 0:heads]).then_inc(back, 1)


def softmax(nc, g, heads, selfs=None):
    for stage, combine in (("max", ALU.max), ("sum", ALU.add)):
        with phase(nc) as s:
            run = s.sb("run", [P, 2, J])
            total = s.sb("total", [P, heads, J])
            ends = s.sb("ends", [P, 2, heads])
            carried = s.sb("carried", [P, 2, heads])
            pen = s.sb("pen", [P, 3, J])
            chain, shifted, exped = s.sem("chain"), s.sem("shifted"), s.sem("exped")
            with nc.Block() as block:
                @block.vector
                def _(v):
                    c = Chain(v, chain)
                    if stage == "max":
                        for n, m in enumerate((g.cont, g.Lm, g.Rm)):
                            c.link(v.tensor_scalar(pen[:, n, :], m[:, :], BIG, -BIG, ALU.mult, ALU.add))
                    for h in range(heads):
                        if stage == "max":
                            c.link(v.tensor_tensor_scan(run[:, 0, :], pen[:, 0, :], g.score[:, h, :], -BIG, ALU.add, ALU.max))
                        else:
                            c.link(v.tensor_tensor_scan(run[:, 0, :], g.cont[:, :], g.score[:, h, :], 0.0, ALU.mult, ALU.add))
                        c.link(v.tensor_tensor(run[:, 1, :], run[:, 0, :], g.isend[:, :], ALU.mult))
                        c.link(v.tensor_tensor_scan(total[:, h, ::-1], g.notend[:, ::-1], run[:, 1, ::-1], 0.0, ALU.mult, ALU.add))
                        c.mark(v.tensor_copy(ends[:, 0, h:h + 1], total[:, h, 0:1]))
                        c.link(v.tensor_copy(ends[:, 1, h:h + 1], total[:, h, J - 1:J]))
            carry_over(nc, g, s, heads, ends[:, 0, :], ends[:, 1, :], carried[:, :, :], combine)
            with nc.Block() as block:
                @block.vector
                def _(v):
                    c = Chain(v, chain)
                    c.n = (3 if stage == "max" else 0) + 5 * heads
                    if stage == "max":
                        for h in range(heads):
                            for n in range(2):
                                c.link(v.scalar_tensor_tensor(total[:, h, :], pen[:, 1 + n, :], carried[:, n, h:h + 1],
                                                              total[:, h, :], ALU.add, ALU.max))
                        if selfs is not None:
                            c.link(v.tensor_tensor(total[:, :, :], total[:, :, :], selfs, ALU.max))
                            c.mark(v.tensor_tensor(selfs, selfs, total[:, :, :], ALU.subtract))
                        c.link(v.tensor_tensor(g.score[:, 0:heads, :], g.score[:, 0:heads, :], total[:, :, :], ALU.subtract))
                        v.sem_inc(shifted, 1)
                    else:
                        for h in range(heads):
                            for n, m in enumerate((g.Lm, g.Rm)):
                                c.link(v.scalar_tensor_tensor(total[:, h, :], m[:, :], carried[:, n, h:h + 1],
                                                              total[:, h, :], ALU.mult, ALU.add))
                        if selfs is not None:
                            c.link(v.tensor_tensor(total[:, :, :], total[:, :, :], selfs, ALU.add))
                            c.link(v.tensor_scalar(total[:, :, :], total[:, :, :], 1.0e-16, None, ALU.add))
                        c.link(v.reciprocal(total[:, :, :], total[:, :, :]))
                        if selfs is not None:
                            c.link(v.tensor_scalar(total[:, :, :], total[:, :, :], 1.0 / H, None, ALU.mult))
                            c.mark(v.tensor_tensor(selfs, selfs, total[:, :, :], ALU.mult))
                        c.link(v.tensor_tensor(g.score[:, 0:heads, :], g.score[:, 0:heads, :], total[:, :, :], ALU.mult))

                if stage == "max":
                    @block.scalar
                    def _(act):
                        act.wait_ge(shifted, 1)
                        if selfs is not None:
                            act.activation(selfs, selfs, ACT.Exp).then_inc(exped, 1)
                        act.activation(g.score[:, 0:heads, :], g.score[:, 0:heads, :], ACT.Exp).then_inc(exped, 1)


def scan_columns(v, c, out, data, prev, cont):
    for f in range(D):
        last = v.tensor_tensor_scan(out[:, :, f], cont, data[:, :, f], prev[:, f:f + 1], ALU.mult, ALU.add)
    c.link(last)


def weighted_sums(nc, g, name):
    with phase(nc) as s:
        rows, run = s.sb("rows", [P, 2, K, D]), s.sb("run", [P, 2, K, D])
        cs, ws = s.sb("cs", [P, 2, K]), s.sb("ws", [P, 2, K])
        got = [s.sem(f"got{k}") for k in range(2)]
        used, free = [s.sem(f"used{k}") for k in range(2)], [s.sem(f"free{k}") for k in range(2)]
        stored = [s.sem(f"stored{k}") for k in range(2)]
        ready, dve_c = s.sem("ready"), s.sem("dve_c")
        with nc.Block() as block:
            @block.sync
            def _(sp):
                with sp.Fori(0, NCH // 2) as i:
                    for k in range(2):
                        sp.wait_ge(used[k], i + 1)
                        sp.dma_start(rows[:, k].rearrange("p j c -> p (j c)"),
                                     g.x_src.rearrange("(p j) c -> p (j c)", p=P)[:, bass.ds((i * 2 + k) * (K * D), K * D)]
                                     ).then_inc(got[k], 16)

            @block.vector
            def _(v):
                c = Chain(v, dve_c)
                for k in range(2):
                    v.sem_inc(used[k], 1)
                c.link(v.memset(run[:, 1, K - 1, :], 0.0))
                with v.Fori(0, NCH // 2) as i:
                    c.begin(i, 8)
                    for k in range(2):
                        c.mark(v.tensor_copy(cs[:, k, :], g.cont[:, bass.ds((i * 2 + k) * K, K)]))
                        c.link(v.tensor_copy(ws[:, k, :], g.score[:, 0, bass.ds((i * 2 + k) * K, K)]))
                        v.wait_ge(got[k], i * 16 + 16)
                        c.link(v.tensor_tensor(rows[:, k], rows[:, k], ws[:, k, :].unsqueeze(2).to_broadcast([P, K, D]), ALU.mult))
                        v.wait_ge(free[k], i + 1)
                        scan_columns(v, c, run[:, k], rows[:, k], run[:, 1 - k, K - 1, :], cs[:, k, :])
                        v.sem_inc(used[k], 1)
                        v.sem_inc(ready, 1)
                c.end(NCH // 2)
                v.tensor_copy(g.tail[:, :], run[:, 1, K - 1, :]).then_inc(dve_c, 1)
                v.wait_ge(dve_c, c.n + 1)

            @block.scalar
            def _(act):
                store_runs(act, g, run, ready, stored, free)


def store_run(eng, g, run, i, k, stored):
    eng.dma_start(g.scanned[0:EP, :].rearrange("(p j) c -> p (j c)", p=P)[:, bass.ds((i * 2 + k) * (K * D), K * D)],
                  run[:, k].rearrange("p j c -> p (j c)")).then_inc(stored[k], 16)


def store_runs(eng, g, run, ready, stored, free):
    for k in range(2):
        eng.sem_inc(free[k], 1)
    with eng.Fori(0, NCH // 2) as i:
        for k in range(2):
            eng.wait_ge(ready, i * 2 + k + 1)
            store_run(eng, g, run, i, k, stored)
            eng.wait_ge(stored[k], i * 16 + 16)
            eng.sem_inc(free[k], 1)


def node_sums(nc, g, out):
    with phase(nc) as s:
        part = s.sb("part", [P, NB, D])
        carried = s.sb("carried", [P, 2, D])
        carry_over(nc, g, s, D, g.tail[:, :], g.tail[:, :], carried[:, :, :], ALU.add)
        kept, got_e, got_c, chain = s.sem("kept"), s.pool_sem(g, 0), s.pool_sem(g, 1), s.sem("chain")
        with nc.Block() as block:
            @block.sync
            def _(sp):
                sp.dma_start(g.carry, carried[:, 0, :]).then_inc(kept, 16)
                sp.wait_ge(kept, 16)

            @block.gpsimd
            def _(pool):
                for b in range(NB):
                    pool.indirect_dma_start(out[:, b, :], None, g.scanned,
                                            bass.IndirectOffsetOnAxis(g.idxEnd[:, b:b + 1], 0)).then_inc(got_e, 16)
                pool.wait_ge(kept, 16)
                for b in range(NB):
                    pool.indirect_dma_start(part[:, b, :], None, g.carry,
                                            bass.IndirectOffsetOnAxis(g.idxCar[:, b:b + 1], 0)).then_inc(got_c, 16)

            @block.vector
            def _(v):
                v.wait_ge(got_e, 16 * NB)
                v.wait_ge(got_c, 16 * NB)
                v.tensor_tensor(out[:, :, :], out[:, :, :], part[:, :, :], ALU.add).then_inc(chain, 1)
                v.wait_ge(chain, 1)


def node_linear(nc, g, srcs, weights, out):
    with phase(nc) as s:
        S, nout = len(srcs), out.shape[3]
        kin = srcs[0].shape[2]
        xT = s.sb("xT", [kin, 2, S, P])
        psT = s.ps("psT", [kin, 2, 512])
        psZ = s.ps("psZ", [P, 2, 512])
        turned, ready, made, evac = (s.sem(n) for n in ("turned", "ready", "made", "evac"))
        with nc.Block() as block:
            @block.tensor
            def _(pe):
                for b in range(NB):
                    for n in range(S):
                        last = pe.transpose(psT[:, b % 2, n * P:(n + 1) * P], srcs[n][:, b, :], g.ident[:, :])
                    last.then_inc(turned, 1)
                    pe.wait_ge(ready, b + 1)
                    if b >= 2:
                        pe.wait_ge(evac, b - 1)
                    for n in range(S):
                        last = pe.matmul(psZ[:, b % 2, n * nout:(n + 1) * nout], xT[:, b % 2, n, :], weights[n],
                                         start=True, stop=True)
                    last.then_inc(made, 1)

            @block.scalar
            def _(act):
                for b in range(NB):
                    act.wait_ge(turned, b + 1)
                    if b >= 2:
                        act.wait_ge(made, b - 1)
                    act.activation(xT[:, b % 2], psT[:, b % 2, 0:S * P].rearrange("k (s e) -> k s e", s=S),
                                   ACT.Copy).then_inc(ready, 1)

            @block.vector
            def _(v):
                for b in range(NB):
                    v.wait_ge(made, b + 1)
                    v.tensor_copy(out[:, b], psZ[:, b % 2, 0:S * nout].rearrange("p (s n) -> p s n", s=S)).then_inc(evac, 1)
                v.wait_ge(evac, NB)


def layernorm(v, c, data, tmp, stat, var_ready, std_ready, at=1):
    over = lambda t: t.unsqueeze(2).to_broadcast([P, NB, D])
    c.link(v.tensor_reduce(stat[:, 0, :], data, X, ALU.add))
    c.link(v.tensor_scalar(stat[:, 0, :], stat[:, 0, :], 1.0 / D, None, ALU.mult))
    c.link(v.tensor_tensor(data, data, over(stat[:, 0, :]), ALU.subtract))
    c.link(v.tensor_tensor(tmp, data, data, ALU.mult))
    c.link(v.tensor_reduce(stat[:, 1, :], tmp, X, ALU.add))
    v.tensor_scalar(stat[:, 1, :], stat[:, 1, :], 1.0 / D, LN_EPS, ALU.mult, ALU.add).then_inc(var_ready, 1)
    v.wait_ge(std_ready, at)
    c.link(v.reciprocal(stat[:, 2, :], stat[:, 2, :]))
    c.link(v.tensor_tensor(data, data, over(stat[:, 2, :]), ALU.mult))


def root(act, stat, var_ready, std_ready, at=1):
    act.wait_ge(var_ready, at)
    act.activation(stat[:, 2, :], stat[:, 1, :], ACT.Sqrt).then_inc(std_ready, 1)


def relation_output(nc, g, a, nbh):
    with phase(nc) as s:
        ab = s.sb("ab", [P, 2, NB, D])
        wr, wT = s.sb("wr", [D, 2, D]), s.sb("wT", [D, 2, D])
        z = s.sb("z", [P, NB, 2, D])
        stat = s.sb("stat", [P, 3, NB])
        ps = s.ps("psw", [D, 2, D])
        loaded, turned, chain, var_ready, std_ready = (s.sem(n) for n in ("loaded", "wturned", "chain", "var", "std"))
        with nc.Block() as block:
            @block.sync
            def _(sp):
                sp.dma_start(wr[:, 0, :], a["rw1"]).then_inc(loaded, 16)
                sp.dma_start(wr[:, 1, :], a["rw2"]).then_inc(loaded, 16)

            @block.tensor
            def _(pe):
                pe.wait_ge(loaded, 32)
                for n in range(2):
                    last = pe.transpose(ps[:, n, :], wr[:, n, :], g.ident[0:D, 0:D])
                last.then_inc(turned, 1)

            @block.vector
            def _(v):
                c = Chain(v, chain)
                c.mark(v.tensor_tensor(ab[:, 0], g.x[:, :, :], nbh[:, :, :], ALU.add))
                c.mark(v.tensor_tensor(ab[:, 1], g.x[:, :, :], nbh[:, :, :], ALU.mult))
                v.wait_ge(turned, 1)
                c.link(v.tensor_copy(wT[:, :, :], ps[:, :, :]))
        node_linear(nc, g, [ab[:, 0], ab[:, 1]], [wT[:, 0, :], wT[:, 1, :]], z)
        with nc.Block() as block:
            @block.vector
            def _(v):
                c = Chain(v, chain)
                c.n = 3
                c.link(v.scalar_tensor_tensor(z[:, :, :, :].rearrange("p b s d -> p (b s d)"),
                                              z[:, :, :, :].rearrange("p b s d -> p (b s d)"), 0.01,
                                              z[:, :, :, :].rearrange("p b s d -> p (b s d)"), ALU.mult, ALU.max))
                c.link(v.tensor_tensor(g.x[:, :, :], g.x[:, :, :], z[:, :, 0, :], ALU.add))
                c.link(v.tensor_tensor(g.x[:, :, :], g.x[:, :, :], z[:, :, 1, :], ALU.add))
                layernorm(v, c, g.x[:, :, :], ab[:, 0], stat, var_ready, std_ready)

            @block.scalar
            def _(act):
                root(act, stat, var_ready, std_ready)


def propagate(nc, g, y, tmp):
    with phase(nc) as s:
        stage = s.sb("stage_i", [P, 2, K], i32)
        rows, run = s.sb("rows", [P, 2, K, D]), s.sb("run", [P, 2, K, D])
        cs = s.sb("cs", [P, 2, K])
        got = [s.pool_sem(g, k) for k in range(2)]
        used, free = [s.sem(f"used{k}") for k in range(2)], [s.sem(f"free{k}") for k in range(2)]
        stored = [s.sem(f"stored{k}") for k in range(2)]
        ready, dve_c, pool_c, staged = s.sem("ready"), s.sem("dve_c"), s.sem("pool_c"), s.sem("staged")
        scaled, put = s.sem("scaled"), s.sem("put")
        with nc.Block() as block:
            @block.sync
            def _(sp):
                sp.wait_ge(scaled, 1)
                sp.dma_start(g.table.rearrange("(p b) d -> p b d", b=NB), tmp[:, :, :]).then_inc(put, 16)
                store_runs(sp, g, run, ready, stored, free)

            @block.gpsimd
            def _(pool):
                c = Chain(pool, pool_c)
                pool.wait_ge(put, 16)
                with pool.Fori(0, NCH // 2) as i:
                    c.begin(i, 2)
                    for k in range(2):
                        pool.wait_ge(used[k], i + 1)
                        gather_columns(pool, g.table, D, g.srcI, stage, rows, c, i, k, got, staged)
                c.end(NCH // 2)

            @block.vector
            def _(v):
                c = Chain(v, dve_c)
                c.link(v.tensor_tensor(tmp[:, :, :], y[:, :, :], g.dinv[:, :].unsqueeze(2).to_broadcast([P, NB, D]), ALU.mult))
                v.sem_inc(scaled, 1)
                for k in range(2):
                    v.sem_inc(used[k], 1)
                c.link(v.memset(run[:, 1, K - 1, :], 0.0))
                with v.Fori(0, NCH // 2) as i:
                    c.begin(i, 4)
                    for k in range(2):
                        c.link(v.tensor_copy(cs[:, k, :], g.cont[:, bass.ds((i * 2 + k) * K, K)]))
                        v.wait_ge(got[k], i * (16 * K) + 16 * K)
                        v.wait_ge(free[k], i + 1)
                        scan_columns(v, c, run[:, k], rows[:, k], run[:, 1 - k, K - 1, :], cs[:, k, :])
                        v.sem_inc(used[k], 1)
                        v.sem_inc(ready, 1)
                c.end(NCH // 2)
                c.link(v.tensor_copy(g.tail[:, :], run[:, 1, K - 1, :]))
    node_sums(nc, g, y)
    with phase(nc) as s:
        chain = s.sem("chain")
        with nc.Block() as block:
            @block.vector
            def _(v):
                c = Chain(v, chain)
                c.link(v.tensor_tensor(y[:, :, :], y[:, :, :], g.dinv[:, :].unsqueeze(2).to_broadcast([P, NB, D]), ALU.mult))


def add_norm(nc, g, terms, first=None):
    with phase(nc) as s:
        tmp, stat = s.sb("tmp", [P, NB, D]), s.sb("stat", [P, 3, NB])
        chain, var_ready, std_ready = s.sem("chain"), s.sem("var"), s.sem("std")
        with nc.Block() as block:
            @block.vector
            def _(v):
                c = Chain(v, chain)
                if first is not None:
                    first(v, c)
                for t in terms:
                    c.link(v.tensor_tensor(g.x[:, :, :], g.x[:, :, :], t, ALU.add))
                layernorm(v, c, g.x[:, :, :], tmp[:, :, :], stat, var_ready, std_ready)

            @block.scalar
            def _(act):
                root(act, stat, var_ready, std_ready)


def put_nodes(nc, g, h, loops=None):
    with phase(nc) as s:
        put, sent, got = s.sem("put"), s.pool_sem(g, 0), s.pool_sem(g, 1)
        with nc.Block() as block:
            @block.sync
            def _(sp):
                sp.dma_start(g.table.rearrange("(p b) d -> p b d", b=NB), h[:, :, :]).then_inc(put, 16)
                if loops is not None:
                    sp.dma_start(g.table_self.rearrange("(p b) d -> p b d", b=NB), loops[:, :, :]).then_inc(put, 16)

            @block.gpsimd
            def _(pool):
                for b in range(NB):
                    at = bass.IndirectOffsetOnAxis(g.idxStart[:, b:b + 1], 0)
                    pool.indirect_dma_start(g.start_rows, at, h[:, b, :], None).then_inc(sent, 16)
                    if loops is not None:
                        pool.indirect_dma_start(g.start_self, at, loops[:, b, :], None).then_inc(sent, 16)
                at = bass.IndirectOffsetOnAxis(g.row0[:, 0:1], 0)
                pool.wait_ge(put, 16 if loops is None else 32)
                pool.indirect_dma_start(g.row_start[:, :], None, g.table, at).then_inc(got, 16)
                if loops is not None:
                    pool.indirect_dma_start(g.row_self[:, :], None, g.table_self, at).then_inc(got, 16)
                pool.wait_ge(got, 16 if loops is None else 32)
                pool.wait_ge(sent, 16 * NB if loops is None else 32 * NB)


def split_bias(nc, row, b3, ones3):
    n = b3.shape[1]
    with phase(nc) as s:
        low = s.sb("low", [1, 3, n], bf16)
        moved, chain, split = s.sem("b_moved"), s.sem("b_chain"), s.sem("b_split")
        with nc.Block() as block:
            @block.sync
            def _(sp):
                sp.wait_ge(split, 1)
                for q in range(3):
                    sp.dma_start(b3[q:q + 1, :], low[0:1, q, :]).then_inc(moved, 16)
                sp.wait_ge(moved, 48)

            @block.vector
            def _(v):
                c = Chain(v, chain)
                c.link(v.memset(ones3[:, :], 1.0))
                for q in range(3):
                    c.link(v.tensor_copy(low[0:1, q, :], row))
                    if q < 2:
                        c.link(v.tensor_tensor(row, row, low[0:1, q, :], ALU.subtract))
                v.sem_inc(split, 1)


def gated_convolution(nc, g, a):
    G = 4
    NG = K // G
    with phase(nc) as s:
        w1, w2 = s.sb("w1", [2 * D, 2 * D]), s.sb("w2", [DE, 2 * D])
        b3, ones3 = s.sb("b3", [3, 2 * D], bf16), s.sb("ones3", [3, P], bf16)
        row = s.sb("bias_row", [1, 2 * D])
        b_in = s.sem("b_in")
        with nc.Block() as block:
            @block.sync
            def _(sp):
                sp.dma_start(row[0:1, 0:D], a["bf"].rearrange("(o n) -> o n", o=1)).then_inc(b_in, 16)
                sp.dma_start(row[0:1, D:2 * D], a["bs"].rearrange("(o n) -> o n", o=1)).then_inc(b_in, 16)
                sp.wait_ge(b_in, 32)
        split_bias(nc, row[0:1, :], b3, ones3)
        stage = s.sb("stage_i", [P, 2, K], i32)
        both = s.sb("both", [P, 2, K, 2 * D])
        starts = s.sb("starts", [P, 2, K, D])
        ea = s.sb("ea", [P, 2, K, DE])
        bothT, eaT = s.sb("bothT", [P, 2, G, P]), s.sb("eaT", [P, 2, G, P])
        la = s.sb("la", [P, 2, G, 2 * D])
        gate, core = s.sb("gate", [P, 4, G, D]), s.sb("core", [P, 4, G, D])
        msg, run = s.sb("msg", [P, 2, K, D]), s.sb("run", [P, 2, K, D])
        cs = s.sb("cs", [P, 2, K])
        psB, psE, psZ = s.ps("psB", [P, 2, G, P]), s.ps("psE", [P, 2, G, P]), s.ps("psZ", [P, 2, G, P])
        two = lambda name: [s.sem(f"{name}{k}") for k in range(2)]
        loaded_s, loaded_e, used, spread, free, stored = (
            two(n) for n in ("starts_in", "ea_in", "slot_used", "spread", "free", "stored"))
        got = [s.pool_sem(g, k) for k in range(2)]
        ready, dve_c, pool_c, staged, w_in = s.sem("ready"), s.sem("dve_c"), s.sem("pool_c"), s.sem("staged"), s.sem("w_in")
        turned, both_out, ea_out, made, logs, low, sig, chained, multiplied = (
            s.sem(n) for n in ("turned", "both_out", "ea_out", "made", "logs", "low", "sig", "chained", "multiplied"))
        grp = lambda i, k, n: i * (2 * NG) + (k * NG + n + 1)
        with nc.Block() as block:
            @block.sync
            def _(sp):
                sp.dma_start(w1[:, 0:D], a["Wf"][0:2 * D, :]).then_inc(w_in, 16)
                sp.dma_start(w1[:, D:2 * D], a["Ws"][0:2 * D, :]).then_inc(w_in, 16)
                sp.dma_start(w2[:, 0:D], a["Wf"][2 * D:2 * D + DE, :]).then_inc(w_in, 16)
                sp.dma_start(w2[:, D:2 * D], a["Ws"][2 * D:2 * D + DE, :]).then_inc(w_in, 16)
                with sp.Fori(0, NCH // 2) as i:
                    for k in range(2):
                        sp.wait_ge(spread[k], i + 1)
                        sp.dma_start(starts[:, k].rearrange("p j c -> p (j c)"),
                                     g.start_rows[0:EP, :].rearrange("(p j) c -> p (j c)", p=P)[:, bass.ds((i * 2 + k) * (K * D), K * D)]
                                     ).then_inc(loaded_s[k], 16)
                        sp.wait_ge(used[k], i + 1)
                        sp.dma_start(ea[:, k].rearrange("p j c -> p (j c)"),
                                     a["ea"].rearrange("(p j) c -> p (j c)", p=P)[:, bass.ds((i * 2 + k) * (K * DE), K * DE)]
                                     ).then_inc(loaded_e[k], 16)

            @block.gpsimd
            def _(pool):
                c = Chain(pool, pool_c)
                with pool.Fori(0, NCH // 2) as i:
                    c.begin(i, 2)
                    for k in range(2):
                        pool.wait_ge(used[k], i + 1)
                        gather_columns(pool, g.table, D, g.srcI, stage, both, c, i, k, got, staged)
                c.end(NCH // 2)

            @block.tensor
            def _(pe):
                for k in range(2):
                    pe.sem_inc(used[k], 1)
                pe.wait_ge(w_in, 64)
                with pe.Fori(0, NCH // 2) as i:
                    for n in range(2 * NG + 1):
                        if n < 2 * NG:
                            k, m = divmod(n, NG)
                            if m == 0:
                                pe.wait_ge(spread[k], i + 2)
                                pe.wait_ge(got[k], i * (16 * K) + 16 * K)
                                pe.wait_ge(loaded_e[k], i * 16 + 16)
                            for j in range(G):
                                pe.transpose(psB[:, n % 2, j, :], both[:, k, m * G + j, :], g.ident[:, :])
                            for j in range(G):
                                last = pe.transpose(psE[:, n % 2, j, :], ea[:, k, m * G + j, :], g.ident[:, :])
                            last.then_inc(turned, 1)
                            if m == NG - 1:
                                pe.wait_ge(turned, grp(i, 0, n))
                                pe.sem_inc(used[k], 1)
                        if n >= 1:
                            q = n - 1
                            pe.wait_ge(both_out, grp(i, 0, q))
                            pe.wait_ge(ea_out, grp(i, 0, q))
                            if q >= 2:
                                pe.wait_ge(logs, grp(i, 0, q - 2))
                                pe.wait_ge(low, grp(i, 0, q - 2))
                            for j in range(G):
                                pe.matmul(psZ[:, q % 2, j, :], ones3[:, :], b3[:, :], start=True, stop=False)
                                pe.matmul(psZ[:, q % 2, j, :], bothT[:, q % 2, j, :], w1[:, :], start=False, stop=False)
                                last = pe.matmul(psZ[:, q % 2, j, :], eaT[:, q % 2, j, :], w2[:, :], start=False, stop=True)
                            last.then_inc(made, 1)
                    pe.wait_ge(logs, grp(i, 0, 2 * NG - 1))
                    pe.wait_ge(low, grp(i, 0, 2 * NG - 1))

            @block.scalar
            def _(act):
                for k in range(2):
                    act.sem_inc(free[k], 1)
                with act.Fori(0, NCH // 2) as i:
                    for n in range(2 * NG + 2):
                        if n < 2 * NG:
                            act.wait_ge(turned, grp(i, 0, n))
                            if n >= 2:
                                act.wait_ge(made, grp(i, 0, n - 2))
                            act.activation(bothT[:, n % 2], psB[:, n % 2], ACT.Copy).then_inc(both_out, 1)
                        if 1 <= n <= 2 * NG:
                            q = n - 1
                            act.wait_ge(made, grp(i, 0, q))
                            if q >= 2:
                                act.wait_ge(low, grp(i, 0, q - 2))
                            act.activation(la[:, q % 2], psZ[:, q % 2], ACT.Abs).then_inc(chained, 1)
                            act.wait_ge(chained, i * (4 * NG) + 2 * q + 1)
                            act.activation(la[:, q % 2], la[:, q % 2], ACT.Exp, scale=-1.0).then_inc(chained, 1)
                            act.wait_ge(chained, i * (4 * NG) + 2 * q + 2)
                            act.activation(la[:, q % 2], la[:, q % 2], ACT.Ln, bias=1.0).then_inc(logs, 1)
                        if n >= 2:
                            q = n - 2
                            act.wait_ge(low, grp(i, 0, q))
                            act.activation(gate[:, q % 4], gate[:, q % 4], ACT.Exp).then_inc(sig, 1)
                    for k in range(2):
                        act.wait_ge(ready, i * 2 + k + 1)
                        store_run(act, g, run, i, k, stored)
                    for k in range(2):
                        act.wait_ge(stored[k], i * 16 + 16)
                        act.sem_inc(free[k], 1)

            @block.vector
            def _(v):
                c = Chain(v, dve_c)
                for k in range(2):
                    v.sem_inc(spread[k], 1)
                c.mark(v.tensor_copy(both[:, 1, K - 1, 0:D], g.row_start[:, :]))
                c.link(v.memset(run[:, 1, K - 1, :], 0.0))
                with v.Fori(0, NCH // 2) as i:
                    c.begin(i, 4)
                    for k in range(2):
                        c.link(v.tensor_copy(cs[:, k, :], g.cont[:, bass.ds((i * 2 + k) * K, K)]))
                        v.wait_ge(loaded_s[k], i * 16 + 16)
                        v.wait_ge(used[k], i + 1)
                        scan_columns(v, c, both[:, k], starts[:, k], both[:, 1 - k, K - 1, 0:D], cs[:, k, :])
                        v.sem_inc(spread[k], 1)
                    for n in range(2 * NG + 3):
                        if n < 2 * NG:
                            v.wait_ge(turned, grp(i, 0, n))
                            if n >= 2:
                                v.wait_ge(made, grp(i, 0, n - 2))
                            v.tensor_copy(eaT[:, n % 2], psE[:, n % 2]).then_inc(ea_out, 1)
                        if 1 <= n <= 2 * NG:
                            q = n - 1
                            v.wait_ge(logs, grp(i, 0, q))
                            if q >= 4:
                                v.wait_ge(multiplied, grp(i, 0, q - 4))
                            v.scalar_tensor_tensor(gate[:, q % 4], psZ[:, q % 2, :, 0:D], 0.0, la[:, q % 2, :, 0:D],
                                                   ALU.min, ALU.subtract)
                            v.scalar_tensor_tensor(core[:, q % 4], psZ[:, q % 2, :, D:2 * D], 0.0, la[:, q % 2, :, D:2 * D],
                                                   ALU.max, ALU.add).then_inc(low, 1)
                        if n >= 3:
                            q = n - 3
                            k, m = divmod(q, NG)
                            v.wait_ge(sig, grp(i, 0, q))
                            v.wait_ge(low, grp(i, 0, q))
                            v.tensor_tensor(msg[:, k, m * G:(m + 1) * G, :], gate[:, q % 4], core[:, q % 4],
                                            ALU.mult).then_inc(multiplied, 1)
                            if m == NG - 1:
                                v.wait_ge(multiplied, grp(i, 0, q))
                                v.wait_ge(free[k], i + 1)
                                for f in range(D):
                                    last = v.tensor_tensor_scan(run[:, k, :, f], cs[:, k, :], msg[:, k, :, f],
                                                                run[:, 1 - k, K - 1, f:f + 1], ALU.mult, ALU.add)
                                last.then_inc(ready, 1)
                                v.wait_ge(ready, i * 2 + k + 1)
                c.end(NCH // 2)
                c.link(v.tensor_copy(g.tail[:, :], run[:, 1, K - 1, :]))


def gat_weights(nc, g, a, layer):
    s = g.layer
    w = lambda name: a[name.format(layer)]
    g.wrl, g.wl = s.sb("wrl", [2 * D, HD + H]), s.sb("wl", [D, HD])
    g.bl, g.brl, g.att, g.bias = s.sb("bl", [P, HD]), s.sb("brl", [P, HD + H]), s.sb("att", [P, HD]), s.sb("bias", [P, D])
    g.brl3, g.bl3, g.ones3 = s.sb("brl3", [3, HD + H], bf16), s.sb("bl3", [3, HD], bf16), s.sb("ones3", [3, P], bf16)
    g.att1 = s.sb("att1", [P, H, D + 1])
    with phase(nc) as t:
        loaded, chain = t.sem("loaded"), t.sem("chain")
        prod, row = t.sb("prod_w", [P, HD]), t.sb("row", [1, 2, HD + H])
        with nc.Block() as block:
            @block.sync
            def _(sp):
                sp.dma_start(g.wrl[0:D, 0:HD], w("W{}r")).then_inc(loaded, 16)
                sp.dma_start(g.wrl[D:2 * D, 0:HD], w("W{}l")).then_inc(loaded, 16)
                sp.dma_start(g.wl[:, :], w("W{}l")).then_inc(loaded, 16)
                sp.dma_start(g.bl[:, :], w("b{}l").partition_broadcast(P)).then_inc(loaded, 16)
                sp.dma_start(g.brl[:, 0:HD], w("b{}r").partition_broadcast(P)).then_inc(loaded, 16)
                sp.dma_start(g.att[:, :], w("att{}").rearrange("h c -> (h c)").partition_broadcast(P)).then_inc(loaded, 16)
                sp.dma_start(g.bias[:, :], w("bias{}").partition_broadcast(P)).then_inc(loaded, 16)
                sp.wait_ge(loaded, 7 * 16)

            @block.vector
            def _(v):
                v.wait_ge(loaded, 7 * 16)
                c = Chain(v, chain)
                c.link(v.tensor_tensor(g.brl[:, 0:HD], g.brl[:, 0:HD], g.bl[:, :], ALU.add))
                for w_ in (g.wrl, g.brl):
                    c.link(v.tensor_tensor(prod[:, :], w_[:, 0:HD], g.att[:, :], ALU.mult))
                    c.link(v.tensor_reduce(w_[:, HD:HD + H], prod[:, :].rearrange("p (h c) -> p h c", h=H), X, ALU.add))
                    c.link(v.tensor_scalar(w_[:, HD:HD + H], w_[:, HD:HD + H], 0.6, None, ALU.mult))
                c.mark(v.memset(g.att1[:, :, D:D + 1], 1.0))
                c.mark(v.tensor_scalar(g.att1[:, :, 0:D], g.att[:, :].rearrange("p (h c) -> p h c", h=H), 0.4, None, ALU.mult))
                c.mark(v.tensor_copy(row[0:1, 0, :], g.brl[0:1, :]))
                c.link(v.tensor_copy(row[0:1, 1, 0:HD], g.bl[0:1, :]))
        split_bias(nc, row[0:1, 0, :], g.brl3, g.ones3)
        split_bias(nc, row[0:1, 1, 0:HD], g.bl3, g.ones3)


def gat_loops(nc, g, h, loops):
    with phase(nc) as s:
        hh, z = s.sb("hh", [P, NB, 2 * D]), s.sb("zz", [P, NB, 1, HD])
        chain = s.sem("chain")
        with nc.Block() as block:
            @block.vector
            def _(v):
                c = Chain(v, chain)
                c.mark(v.tensor_copy(hh[:, :, 0:D], h[:, :, :]))
                c.link(v.tensor_copy(hh[:, :, D:2 * D], h[:, :, :]))
        node_linear(nc, g, [hh[:, :, :]], [g.wrl[:, 0:HD]], z)
        with nc.Block() as block:
            @block.vector
            def _(v):
                c = Chain(v, chain)
                c.n = 2
                flat = z[:, :, 0, :]
                over = lambda t: t[:, 0:HD].unsqueeze(1).to_broadcast([P, NB, HD])
                c.link(v.tensor_tensor(flat, flat, over(g.brl), ALU.add))
                c.link(v.scalar_tensor_tensor(flat, flat, 0.2, flat, ALU.mult, ALU.max))
                c.link(v.tensor_tensor(flat, flat, over(g.att), ALU.mult))
                c.link(v.tensor_reduce(loops[:, :, :], flat.rearrange("p b (h c) -> p b h c", h=H), X, ALU.add))


def gat_scores(nc, g):
    G = 2
    NG = K // G
    with phase(nc) as s:
        stage = s.sb("stage_i", [P, 2, K], i32)
        both, starts = s.sb("both", [P, 2, K, 2 * D]), s.sb("starts", [P, 2, K, D])
        bothT, lz = s.sb("bothT", [P, 2, G, P]), s.sb("lz", [P, 2, G, H, D + 1])
        sc, cs = s.sb("sc", [P, 2, K, H]), s.sb("cs", [P, 2, K])
        psB, psZ = s.ps("psB", [P, 2, 512]), s.ps("psZ", [P, 2, G, 512])
        two = lambda name: [s.sem(f"{name}{k}") for k in range(2)]
        loaded_s, used, spread, stored, kept = (two(n) for n in ("starts_in", "slot_used", "spread", "stored", "kept"))
        got = [s.pool_sem(g, k) for k in range(2)]
        dve_c, pool_c, staged, turned, out, made, leaky, prod, scored = (
            s.sem(n) for n in ("dve_c", "pool_c", "staged", "turned", "both_out", "made", "leaky", "prod", "scored"))
        grp = lambda i, n: i * (2 * NG) + (n + 1)
        with nc.Block() as block:
            @block.sync
            def _(sp):
                with sp.Fori(0, NCH // 2) as i:
                    for k in range(2):
                        sp.wait_ge(spread[k], i + 1)
                        sp.dma_start(starts[:, k].rearrange("p j c -> p (j c)"),
                                     g.start_rows[0:EP, :].rearrange("(p j) c -> p (j c)", p=P)[:, bass.ds((i * 2 + k) * (K * D), K * D)]
                                     ).then_inc(loaded_s[k], 16)

            @block.gpsimd
            def _(pool):
                c = Chain(pool, pool_c)
                with pool.Fori(0, NCH // 2) as i:
                    c.begin(i, 2)
                    for k in range(2):
                        pool.wait_ge(used[k], i + 1)
                        pool.wait_ge(kept[k], i + 1)
                        gather_columns(pool, g.table, D, g.srcI, stage, both, c, i, k, got, staged)
                c.end(NCH // 2)

            @block.tensor
            def _(pe):
                for k in range(2):
                    pe.sem_inc(used[k], 1)
                with pe.Fori(0, NCH // 2) as i:
                    for n in range(2 * NG + 1):
                        if n < 2 * NG:
                            k, m = divmod(n, NG)
                            if m == 0:
                                pe.wait_ge(spread[k], i + 2)
                                pe.wait_ge(got[k], i * (16 * K) + 16 * K)
                            for j in range(G):
                                last = pe.transpose(psB[:, n % 2, j * P:(j + 1) * P], both[:, k, m * G + j, :], g.ident[:, :])
                            last.then_inc(turned, 1)
                            if m == NG - 1:
                                pe.wait_ge(turned, grp(i, n))
                                pe.sem_inc(used[k], 1)
                        if n >= 1:
                            q = n - 1
                            pe.wait_ge(out, grp(i, q))
                            if q >= 2:
                                pe.wait_ge(leaky, grp(i, q - 2))
                            for j in range(G):
                                pe.matmul(psZ[:, q % 2, j, 0:HD + H], g.ones3[:, :], g.brl3[:, :], start=True, stop=False)
                                last = pe.matmul(psZ[:, q % 2, j, 0:HD + H], bothT[:, q % 2, j, :], g.wrl[:, :],
                                                 start=False, stop=True)
                            last.then_inc(made, 1)
                    pe.wait_ge(leaky, grp(i, 2 * NG - 1))

            @block.scalar
            def _(act):
                for k in range(2):
                    act.sem_inc(kept[k], 1)
                with act.Fori(0, NCH // 2) as i:
                    for n in range(2 * NG + 1):
                        if n < 2 * NG:
                            k, m = divmod(n, NG)
                            if m == 0:
                                act.wait_ge(got[k], i * (16 * K) + 16 * K)
                                act.dma_start(g.x_src.rearrange("(p j) c -> p j c", p=P)[:, bass.ds((i * 2 + k) * K, K), :],
                                              both[:, k, :, D:2 * D]).then_inc(stored[k], 16)
                            act.wait_ge(turned, grp(i, n))
                            if n >= 2:
                                act.wait_ge(made, grp(i, n - 2))
                            act.activation(bothT[:, n % 2], psB[:, n % 2, 0:G * P].rearrange("p (g e) -> p g e", g=G),
                                           ACT.Copy).then_inc(out, 1)
                            if m == NG - 1:
                                act.wait_ge(stored[k], i * 16 + 16)
                                act.sem_inc(kept[k], 1)
                        if n >= 1:
                            q = n - 1
                            act.wait_ge(made, grp(i, q))
                            if q >= 2:
                                act.wait_ge(scored, grp(i, q - 2))
                            act.activation(lz[:, q % 2, :, :, 0:D], psZ[:, q % 2, :, 0:HD].rearrange("p g (h c) -> p g h c", h=H),
                                           ACT.Abs)
                            act.activation(lz[:, q % 2, :, :, D], psZ[:, q % 2, :, HD:HD + H], ACT.Copy).then_inc(leaky, 1)
                    act.wait_ge(scored, grp(i, 2 * NG - 1))

            @block.vector
            def _(v):
                c = Chain(v, dve_c)
                for k in range(2):
                    v.sem_inc(spread[k], 1)
                c.link(v.tensor_copy(both[:, 1, K - 1, 0:D], g.row_start[:, :]))
                with v.Fori(0, NCH // 2) as i:
                    c.begin(i, 6)
                    for k in range(2):
                        c.link(v.tensor_copy(cs[:, k, :], g.cont[:, bass.ds((i * 2 + k) * K, K)]))
                        v.wait_ge(loaded_s[k], i * 16 + 16)
                        v.wait_ge(used[k], i + 1)
                        scan_columns(v, c, both[:, k], starts[:, k], both[:, 1 - k, K - 1, 0:D], cs[:, k, :])
                        v.sem_inc(spread[k], 1)
                    for n in range(2 * NG + 1):
                        if n < 2 * NG:
                            v.wait_ge(leaky, grp(i, n))
                            v.tensor_tensor(lz[:, n % 2].rearrange("p g h c -> p g (h c)"),
                                            lz[:, n % 2].rearrange("p g h c -> p g (h c)"),
                                            g.att1[:, :, :].rearrange("p h c -> p (h c)").unsqueeze(1).to_broadcast([P, G, HD + H]),
                                            ALU.mult).then_inc(prod, 1)
                        if n >= 1:
                            q = n - 1
                            k, m = divmod(q, NG)
                            v.wait_ge(prod, grp(i, q))
                            v.tensor_reduce(sc[:, k, m * G:(m + 1) * G, :],
                                            lz[:, q % 2], X, ALU.add).then_inc(scored, 1)
                            if m == NG - 1:
                                v.wait_ge(scored, grp(i, q))
                                c.link(v.tensor_copy(g.score[:, :, bass.ds((i * 2 + k) * K, K)],
                                                     sc[:, k].rearrange("p j h -> p h j")))
                c.end(NCH // 2)


def spread_loops(nc, g, selfs):
    with phase(nc) as s:
        at = s.sb("at_starts", [P, J, H])
        loaded, chain = s.sem("loaded"), s.sem("chain")
        with nc.Block() as block:
            @block.sync
            def _(sp):
                sp.dma_start(at[:, :, :].rearrange("p j h -> p (j h)"),
                             g.start_self[0:EP, :].rearrange("(p j) h -> p (j h)", p=P)).then_inc(loaded, 16)

            @block.vector
            def _(v):
                c = Chain(v, chain)
                v.wait_ge(loaded, 16)
                for h in range(H):
                    c.mark(v.tensor_tensor_scan(selfs[:, h, :], g.cont[:, :], at[:, :, h], g.row_self[:, h:h + 1], ALU.mult, ALU.add))
                c.wait()


def gather_loop_weights(nc, g, selfs, loops):
    with phase(nc) as s:
        at = s.sb("at_edges", [P, J, H])
        turned, kept, got, chain = s.sem("turned"), s.sem("kept"), s.pool_sem(g, 0), s.sem("chain")
        with nc.Block() as block:
            @block.vector
            def _(v):
                v.tensor_copy(at[:, :, :], selfs.rearrange("p h j -> p j h")).then_inc(turned, 1)
                c = Chain(v, chain)
                v.wait_ge(got, 16 * NB)
                for h in range(H):
                    c.mark(v.scalar_tensor_tensor(loops[:, :, h], g.nothas[:, :], 1.0 / H, loops[:, :, h], ALU.mult, ALU.add))
                c.wait()

            @block.sync
            def _(sp):
                sp.wait_ge(turned, 1)
                sp.dma_start(g.self_weight[0:EP, :].rearrange("(p j) h -> p (j h)", p=P),
                             at[:, :, :].rearrange("p j h -> p (j h)")).then_inc(kept, 16)

            @block.gpsimd
            def _(pool):
                pool.wait_ge(kept, 16)
                for b in range(NB):
                    pool.indirect_dma_start(loops[:, b, :], None, g.self_weight,
                                            bass.IndirectOffsetOnAxis(g.idxEnd[:, b:b + 1], 0)).then_inc(got, 16)


def gat_sums(nc, g):
    G = 2
    NG = K // G
    with phase(nc) as s:
        rows, msg, run = s.sb("rows", [P, 2, K, D]), s.sb("msg", [P, 2, K, D]), s.sb("run", [P, 2, K, D])
        rowsT, prod = s.sb("rowsT", [D, 2, G, P]), s.sb("prod", [P, 2, G, HD])
        ws, cs = s.sb("ws", [P, 2, K, H]), s.sb("cs", [P, 2, K])
        psT, psZ = s.ps("psT", [D, 2, 512]), s.ps("psZ", [P, 2, G, 512])
        two = lambda name: [s.sem(f"{name}{k}") for k in range(2)]
        got, used, free = (two(n) for n in ("got", "slot_used", "free"))
        stored = [s.pool_sem(g, k) for k in range(2)]
        dve_c, begun, turned, out, made, weighed, summed, ready = (
            s.sem(n) for n in ("dve_c", "begun", "turned", "rows_out", "made", "weighed", "summed", "ready"))
        grp = lambda i, n: i * (2 * NG) + (n + 1)
        with nc.Block() as block:
            @block.sync
            def _(sp):
                with sp.Fori(0, NCH // 2) as i:
                    for k in range(2):
                        sp.wait_ge(used[k], i + 1)
                        sp.dma_start(rows[:, k].rearrange("p j c -> p (j c)"),
                                     g.x_src.rearrange("(p j) c -> p (j c)", p=P)[:, bass.ds((i * 2 + k) * (K * D), K * D)]
                                     ).then_inc(got[k], 16)

            @block.gpsimd
            def _(pool):
                store_runs(pool, g, run, ready, stored, free)

            @block.tensor
            def _(pe):
                for k in range(2):
                    pe.sem_inc(used[k], 1)
                with pe.Fori(0, NCH // 2) as i:
                    for n in range(2 * NG + 1):
                        if n < 2 * NG:
                            k, m = divmod(n, NG)
                            if m == 0:
                                pe.wait_ge(got[k], i * 16 + 16)
                                pe.sem_inc(begun, 1)
                            for j in range(G):
                                last = pe.transpose(psT[:, n % 2, j * P:(j + 1) * P], rows[:, k, m * G + j, :], g.ident[:, :])
                            last.then_inc(turned, 1)
                            if m == NG - 1:
                                pe.wait_ge(turned, grp(i, n))
                                pe.sem_inc(used[k], 1)
                        if n >= 1:
                            q = n - 1
                            pe.wait_ge(out, grp(i, q))
                            if q >= 2:
                                pe.wait_ge(weighed, grp(i, q - 2))
                            for j in range(G):
                                pe.matmul(psZ[:, q % 2, j, 0:HD], g.ones3[:, :], g.bl3[:, :], start=True, stop=False)
                                last = pe.matmul(psZ[:, q % 2, j, 0:HD], rowsT[:, q % 2, j, :], g.wl[:, :],
                                                 start=False, stop=True)
                            last.then_inc(made, 1)
                    pe.wait_ge(weighed, grp(i, 2 * NG - 1))

            @block.scalar
            def _(act):
                with act.Fori(0, NCH // 2) as i:
                    for n in range(2 * NG):
                        act.wait_ge(turned, grp(i, n))
                        if n >= 2:
                            act.wait_ge(made, grp(i, n - 2))
                        act.activation(rowsT[:, n % 2], psT[:, n % 2, 0:G * P].rearrange("p (g e) -> p g e", g=G),
                                       ACT.Copy).then_inc(out, 1)
                    act.wait_ge(made, grp(i, 2 * NG - 1))

            @block.vector
            def _(v):
                c = Chain(v, dve_c)
                c.link(v.memset(run[:, 1, K - 1, :], 0.0))
                with v.Fori(0, NCH // 2) as i:
                    c.begin(i, 6)
                    for k in range(2):
                        c.mark(v.tensor_copy(cs[:, k, :], g.cont[:, bass.ds((i * 2 + k) * K, K)]))
                        c.link(v.tensor_copy(ws[:, k].rearrange("p j h -> p h j"), g.score[:, :, bass.ds((i * 2 + k) * K, K)]))
                    for n in range(2 * NG + 1):
                        if n < 2 * NG:
                            k, m = divmod(n, NG)
                            v.wait_ge(made, grp(i, n))
                            if n >= 2:
                                v.wait_ge(summed, grp(i, n - 2))
                            v.tensor_tensor(prod[:, n % 2].rearrange("p g (h c) -> p g h c", h=H),
                                            psZ[:, n % 2, :, 0:HD].rearrange("p g (h c) -> p g h c", h=H),
                                            ws[:, k, m * G:(m + 1) * G, :].unsqueeze(3).to_broadcast([P, G, H, D]),
                                            ALU.mult).then_inc(weighed, 1)
                        if n >= 1:
                            q = n - 1
                            k, m = divmod(q, NG)
                            v.wait_ge(weighed, grp(i, q))
                            v.tensor_reduce(msg[:, k, m * G:(m + 1) * G, :],
                                            prod[:, q % 2].rearrange("p g (h c) -> p g c h", h=H), X, ALU.add).then_inc(summed, 1)
                            if m == NG - 1:
                                v.wait_ge(summed, grp(i, q))
                                v.wait_ge(free[k], i + 1)
                                scan_columns(v, c, run[:, k], msg[:, k], run[:, 1 - k, K - 1, :], cs[:, k, :])
                                v.sem_inc(ready, 1)
                c.end(NCH // 2)
                c.link(v.tensor_copy(g.tail[:, :], run[:, 1, K - 1, :]))


def gat_layer(nc, g, a, layer, h, out):
    with phase(nc) as s:
        g.layer = s
        gat_weights(nc, g, a, layer)
        loops = s.sb("loops", [P, NB, H])
        gat_loops(nc, g, h, loops)
        with phase(nc) as t:
            g.score = t.sb("score", [P, H, J])
            selfs = t.sb("selfs", [P, H, J])
            put_nodes(nc, g, h, loops)
            gat_scores(nc, g)
            spread_loops(nc, g, selfs)
            softmax(nc, g, H, selfs[:, :, :])
            gather_loop_weights(nc, g, selfs[:, :, :], loops)
            gat_sums(nc, g)
        with phase(nc) as t:
            xl, acc = t.sb("xl", [P, NB, 1, HD]), t.sb("acc", [P, NB, D])
            chain = t.sem("chain")
            node_sums(nc, g, acc)
            node_linear(nc, g, [h[:, :, :]], [g.wl[:, :]], xl)
            with nc.Block() as block:
                @block.vector
                def _(v):
                    c = Chain(v, chain)
                    flat = xl[:, :, 0, :]
                    c.link(v.tensor_tensor(flat, flat, g.bl[:, :].unsqueeze(1).to_broadcast([P, NB, HD]), ALU.add))
                    c.link(v.tensor_tensor(flat.rearrange("p b (h c) -> p b h c", h=H),
                                           flat.rearrange("p b (h c) -> p b h c", h=H),
                                           loops[:, :, :].unsqueeze(3).to_broadcast([P, NB, H, D]), ALU.mult))
                    for n in range(H):
                        c.link(v.tensor_tensor(acc[:, :, :], acc[:, :, :], xl[:, :, 0, n * D:(n + 1) * D], ALU.add))
                    c.link(v.tensor_tensor(acc[:, :, :], acc[:, :, :], g.bias[:, :].unsqueeze(1).to_broadcast([P, NB, D]), ALU.add))
                    c.link(v.tensor_scalar(out[:, :, :], acc[:, :, :], 0.0, None, ALU.max))


def build(nc, a, out):
    Space.used = {}
    g = Space(nc, ExitStack())

    def scratch(name, shape):
        return nc.dram_tensor(name, shape, f32, kind="Internal").ap()

    g.hpx = scratch("hpx", (NR * R, 2 * D))
    g.x_src = scratch("x_src", (EP, D))
    g.scanned = scratch("scanned", (EP + P, D))
    g.carry = scratch("carry", (P, D))
    g.table = scratch("table", (NR, D))
    g.start_rows = scratch("start_rows", (EP + NR, D))
    g.table_self = scratch("table_self", (NR, H))
    g.start_self = scratch("start_self", (EP + NR, H))
    g.self_weight = scratch("self_weight", (EP + P, H))
    with g.ctx:
        g.pool_sems = [g.sem(f"pool_dma{n}") for n in range(4)]
        setup(nc, g, a)
        g.tail = g.sb("tail", [P, D])
        relation_table(nc, g, a)
        with phase(nc) as s:
            g.score = s.sb("score", [P, 1, J])
            relation_scores(nc, g, a)
            softmax(nc, g, 1)
            weighted_sums(nc, g, "L0")
        with phase(nc) as s:
            nbh = s.sb("nbh", [P, NB, D])
            node_sums(nc, g, nbh)
            relation_output(nc, g, a, nbh)
        with phase(nc) as s:
            y, tmp = s.sb("y", [P, NB, D]), s.sb("ytmp", [P, NB, D])
            with phase(nc) as t:
                copied = t.sem("copied")
                with nc.Block() as block:
                    @block.vector
                    def _(v):
                        v.tensor_copy(y[:, :, :], g.x[:, :, :]).then_inc(copied, 1)
                        v.wait_ge(copied, 1)
            for _ in range(4):
                propagate(nc, g, y, tmp)
            add_norm(nc, g, [y[:, :, :]])
        g.row_start = g.sb("row_start", [P, D])
        g.row_self = g.sb("row_self", [P, H])
        put_nodes(nc, g, g.x)
        gated_convolution(nc, g, a)
        with phase(nc) as s:
            agg = s.sb("agg", [P, NB, D])
            node_sums(nc, g, agg)

            def gated(v, c):
                c.link(v.tensor_tensor(agg[:, :, :], agg[:, :, :], g.x[:, :, :], ALU.add))
                c.link(v.tensor_scalar(agg[:, :, :], agg[:, :, :], 0.0, None, ALU.max))

            add_norm(nc, g, [agg[:, :, :]], gated)
        with phase(nc) as s:
            h1 = s.sb("h1", [P, NB, D])
            gat_layer(nc, g, a, 1, g.x, h1)
            gat_layer(nc, g, a, 2, h1, h1)
            z, fc, bfc = s.sb("z_fc", [P, NB, 1, D]), s.sb("fc", [D, D]), s.sb("bfc", [P, D])
            loaded = s.sem("fc_loaded")
            with nc.Block() as block:
                @block.sync
                def _(sp):
                    sp.dma_start(fc[:, :], a["Wfc"]).then_inc(loaded, 16)
                    sp.dma_start(bfc[:, :], a["bfc"].partition_broadcast(P)).then_inc(loaded, 16)
                    sp.wait_ge(loaded, 32)
            node_linear(nc, g, [h1[:, :, :]], [fc[:, :]], z)
            add_norm(nc, g, [z[:, :, 0, :], bfc[:, :].unsqueeze(1).to_broadcast([P, NB, D])])
            stored = s.sem("out_stored")
            with nc.Block() as block:
                @block.sync
                def _(sp):
                    sp.dma_start(out.rearrange("(p b) d -> p b d", b=NB), g.x[0:N // NB, :, :]).then_inc(stored, 16)
                    sp.wait_ge(stored, 16)


_INS = {"x": "x", "src": "src", "dst": "dst", "et": "edge_type_32", "ea": "edge_attr_128", "ef": "edge_attr_64",
        "relw": "L0_gnn_relation_weight", "rw1": "L0_gnn_res_w1", "rw2": "L0_gnn_res_w2",
        "Wf": "L2_gnn_W_f", "bf": "L2_gnn_b_f", "Ws": "L2_gnn_W_s", "bs": "L2_gnn_b_s",
        "W1l": "L3_gnn_W1l", "b1l": "L3_gnn_b1l", "W1r": "L3_gnn_W1r", "b1r": "L3_gnn_b1r", "att1": "L3_gnn_att1",
        "bias1": "L3_gnn_bias1", "W2l": "L3_gnn_W2l", "b2l": "L3_gnn_b2l", "W2r": "L3_gnn_W2r", "b2r": "L3_gnn_b2r",
        "att2": "L3_gnn_att2", "bias2": "L3_gnn_bias2", "Wfc": "L3_gnn_Wfc", "bfc": "L3_gnn_bfc"}
_EDGES = {"src": 0, "dst": N, "et": 0, "ea": 0, "ef": 0}


def kernel(**inputs):
    import numpy as np
    import concourse.bacc as bacc
    from concourse.bass_utils import run_bass_kernel_spmd as run

    nc = bacc.Bacc("TRN2", target_bir_lowering=False, num_devices=1)
    arrays, args = {}, {}
    for short, name in _INS.items():
        v = np.ascontiguousarray(inputs[name])
        if short in _EDGES:
            pad = np.full((EP - E,) + v.shape[1:], _EDGES[short], v.dtype)
            v = np.concatenate([v, pad])
        arrays[f"in_{short}"] = v
        args[short] = nc.dram_tensor(f"in_{short}", v.shape, mybir.dt.from_np(v.dtype), kind="ExternalInput").ap()
    out = nc.dram_tensor("out_0", (N, D), f32, kind="ExternalOutput").ap()
    build(nc, args, out)
    r = run(nc, [arrays], core_ids=[0])
    return r.results[0]["out_0"]
```

```python
from contextlib import ExitStack, contextmanager

import concourse.bass as bass
from concourse import mybir

P = 128
N, D = 3125, 64
E = 100000
R = 32
H = 5
HD = H * D
DE = 128
NB = N // 125
NR = P * NB
J = 784
EP = P * J
BIG = 1.0e38
WHOLE = 1.5 * 2.0 ** 23
LN_EPS = 1.0e-5
K = 28
NCH = J // K

CE = 128
CH = EP // CE
WD = 5
NW = N // WD
TS = 25
TC = TS * WD
NT = 57
S = NT * TS
SP = 95
SQ = S // SP
assert S >= CH + N // WD + 1 and SP * SQ == S and NB % WD == 0

f32 = mybir.dt.float32
bf16 = mybir.dt.bfloat16
i32 = mybir.dt.int32
ALU = mybir.AluOpType
ACT = mybir.ActivationFunctionType
X = mybir.AxisListType.X


class Chain:

    def __init__(self, eng, sem):
        self.eng, self.sem, self.n, self.turn = eng, sem, 0, None

    def count(self):
        return self.n if self.turn is None else self.turn + self.n

    def mark(self, ins):
        self.n += 1
        ins.then_inc(self.sem, 1)
        return self.count()

    def wait(self, at=None):
        self.eng.wait_ge(self.sem, self.count() if at is None else at)

    def link(self, ins):
        self.mark(ins)
        self.wait()

    def begin(self, i, each):
        self.before, self.each, self.turn = self.n, each, i * each

    def end(self, turns):
        assert self.n - self.before == self.each, (self.n - self.before, self.each)
        self.n = self.before + self.each * turns
        self.turn = None


class Space:

    used = {}

    def __init__(self, nc, ctx):
        self.nc, self.ctx, self.sems = nc, ctx, []

    def sb(self, name, shape, dt=f32):
        return self.ctx.enter_context(self.nc.sbuf_tensor(self.own(name), shape, dt))

    def ps(self, name, shape, dt=f32):
        return self.ctx.enter_context(self.nc.psum_tensor(self.own(name), shape, dt))

    def sem(self, name):
        self.sems.append(self.ctx.enter_context(self.nc.semaphore(self.own(name))))
        return self.sems[-1]

    def pool_sem(self, g, n):
        self.sems.append(g.pool_sems[n])
        return g.pool_sems[n]

    def own(self, name):
        used = Space.used
        used[name] = used.get(name, 0) + 1
        return name if used[name] == 1 else f"{name}_{used[name]}"


@contextmanager
def phase(nc):
    with ExitStack() as ctx:
        s = Space(nc, ctx)
        yield s
        with nc.Block() as block:
            @block.gpsimd
            def _(pool):
                pool.dma_reset()
                for sem in s.sems:
                    pool.sem_clear(sem)


def setup(nc, g, a):
    g.srcI, g.dstI = g.sb("srcI", [P, J], i32), g.sb("dstI", [P, J], i32)
    g.hpS, g.hpD = g.sb("hpS", [P, J], i32), g.sb("hpD", [P, J], i32)
    g.cont, g.isend, g.notend = g.sb("cont", [P, J]), g.sb("isend", [P, J]), g.sb("notend", [P, J])
    g.Lm, g.Rm = g.sb("Lm", [P, J]), g.sb("Rm", [P, J])
    g.x = g.sb("x", [P, NB, D])
    g.ident = g.sb("ident", [P, P])
    g.contLrow, g.contRrow = g.sb("contLrow", [P, P]), g.sb("contRrow", [P, P])
    g.dinv, g.has, g.nothas = g.sb("dinv", [P, NB]), g.sb("has", [P, NB]), g.sb("nothas", [P, NB])
    g.idxEnd, g.idxCar = g.sb("idxEnd", [P, NB], i32), g.sb("idxCar", [P, NB], i32)
    g.idxStart, g.row0 = g.sb("idxStart", [P, NB], i32), g.sb("row0", [P, 1], i32)
    with phase(nc) as s:
        etI = s.sb("etI", [P, J], i32)
        edge_rows = s.sb("edge_rows", [P, 2], i32)
        dstF = s.sb("dstF", [P, J])
        dstP = s.sb("dstP", [P, J])
        dstB = s.sb("dstB", [P, J])
        nbr = s.sb("nbr", [P, 2])
        iotaI = s.sb("iotaI", [P, P], i32)
        iotaF = s.sb("iotaF", [P, P])
        nodeI = s.sb("nodeI", [P, NB], i32)
        nodeF = s.sb("nodeF", [P, NB])
        ones = s.sb("ones", [P, P])
        lower = s.sb("lower", [P, P])
        diag = s.sb("diag", [P, 2, P])
        zero = s.sb("zero", [P, P], bf16)
        hotP = s.sb("hotP", [P, 2, K, P], bf16)
        hotB = s.sb("hotB", [P, 2, K, NB], bf16)
        cols = s.sb("cols", [P, 2, 2, K])
        w = s.sb("w", [P, 12, NB])
        psC = s.ps("psC", [P, 512])
        psR = s.ps("psR", [P, 2, 256])
        psE = s.ps("psE", [P, 512])
        loaded = s.sem("loaded")
        cleared = s.sem("cleared")
        made = s.sem("made")
        dve = s.sem("dve")
        hot = [s.sem(f"hot{k}") for k in range(2)]
        counted = [s.sem(f"counted{k}") for k in range(2)]
        split = s.sem("split")
        rows = s.sem("rows")
        total = s.sem("total")
        sq = s.sem("sq")
        sqd = s.sem("sqd")
        zeroed = s.sem("zeroed")
        with nc.Block() as block:
            @block.sync
            def _(sp):
                sp.dma_start(g.srcI[:, :], a["src"].rearrange("(p j) -> p j", p=P)).then_inc(loaded, 16)
                sp.dma_start(g.dstI[:, :], a["dst"].rearrange("(p j) -> p j", p=P)).then_inc(loaded, 16)
                sp.dma_start(etI[:, :], a["et"].rearrange("(p j) -> p j", p=P)).then_inc(loaded, 16)
                d2 = a["dst"].rearrange("(p j) -> p j", p=P)
                sp.wait_ge(cleared, 2)
                sp.dma_start(edge_rows[1:P, 0:1], d2[0:P - 1, J - 1:J],
                             allow_slow_non_contiguous=True).then_inc(loaded, 16)
                sp.dma_start(edge_rows[0:P - 1, 1:2], d2[1:P, 0:1],
                             allow_slow_non_contiguous=True).then_inc(loaded, 16)
                sp.dma_start(g.x[0:N // NB], a["x"].rearrange("(p b) d -> p b d", b=NB)).then_inc(loaded, 16)
                sp.wait_ge(loaded, 6 * 16)

            @block.gpsimd
            def _(pool):
                pool.memset(edge_rows[:, :], -1).then_inc(cleared, 1)
                pool.memset(g.x[:, :, :], 0.0).then_inc(cleared, 1)
                pool.memset(ones[:, :], 1.0).then_inc(made, 1)
                pool.memset(g.ident[:, :], 0.0).then_inc(made, 1)
                pool.wait_ge(made, 2)
                pool.affine_select(out=g.ident[:, :], in_=g.ident[:, :], compare_op=ALU.not_equal, fill=1.0,
                                   base=0, pattern=[[-1, P]], channel_multiplier=1).then_inc(made, 1)
                pool.affine_select(out=lower[:, :], in_=ones[:, :], compare_op=ALU.is_gt, fill=0.0,
                                   base=0, pattern=[[1, P]], channel_multiplier=-1).then_inc(made, 1)
                pool.iota(iotaI[:, :], pattern=[[1, P]], base=0, channel_multiplier=0).then_inc(made, 1)
                pool.iota(nodeI[:, :], pattern=[[1, NB]], base=0, channel_multiplier=NB).then_inc(made, 1)
                pool.memset(zero[:, :], 0.0).then_inc(made, 1)
                pool.wait_ge(made, 7)

            @block.vector
            def _(v):
                c = Chain(v, dve)
                v.wait_ge(loaded, 6 * 16)
                v.wait_ge(made, 7)
                v.tensor_copy(iotaF[:, :], iotaI[:, :]).then_inc(dve, 1)
                v.tensor_copy(nodeF[:, :], nodeI[:, :]).then_inc(dve, 1)
                c.n = 2
                c.mark(v.tensor_copy(nbr[:, :], edge_rows[:, :]))
                c.link(v.tensor_copy(dstF[:, :], g.dstI[:, :]))
                c.mark(v.tensor_scalar(g.Lm[:, :], dstF[:, :], nbr[:, 0:1], None, ALU.is_equal))
                c.mark(v.tensor_scalar(g.Rm[:, :], dstF[:, :], nbr[:, 1:2], None, ALU.is_equal))
                c.mark(v.tensor_tensor(g.cont[:, 1:J], dstF[:, 1:J], dstF[:, 0:J - 1], ALU.is_equal))
                c.mark(v.tensor_tensor(g.cont[:, 0:1], dstF[:, 0:1], nbr[:, 0:1], ALU.is_equal))
                c.mark(v.tensor_tensor(g.isend[:, 0:J - 1], dstF[:, 1:J], dstF[:, 0:J - 1], ALU.not_equal))
                c.mark(v.memset(g.isend[:, J - 1:J], 1.0))
                c.mark(v.scalar_tensor_tensor(g.hpS[:, :], g.srcI[:, :], float(R), etI[:, :], ALU.mult, ALU.add))
                c.mark(v.scalar_tensor_tensor(g.hpD[:, :], g.dstI[:, :], float(R), etI[:, :], ALU.mult, ALU.add))
                c.mark(v.tensor_copy(g.row0[:, :], g.dstI[:, 0:1]))
                c.link(v.tensor_scalar(dstP[:, :], dstF[:, :], 1.0 / NB, -0.48, ALU.mult, ALU.add))
                c.mark(v.tensor_scalar(g.notend[:, :], g.isend[:, :], -1.0, 1.0, ALU.mult, ALU.add))
                c.link(v.tensor_scalar(dstP[:, :], dstP[:, :], WHOLE, -WHOLE, ALU.add, ALU.add))
                c.link(v.scalar_tensor_tensor(dstB[:, :], dstP[:, :], -float(NB), dstF[:, :], ALU.mult, ALU.add))
                c.mark(v.tensor_scalar(diag[:, 0, :], g.ident[:, :], g.Lm[:, J - 1:J], None, ALU.mult))
                c.link(v.tensor_scalar(diag[:, 1, :], g.ident[:, :], g.Rm[:, 0:1], None, ALU.mult))
                v.sem_inc(split, 1)
                with v.Fori(0, NCH // 2) as i:
                    c.begin(i, 4)
                    for k in range(2):
                        v.wait_ge(counted[k], i + 1)
                        c.mark(v.tensor_copy(cols[:, k, 0, :], dstP[:, bass.ds((i * 2 + k) * K, K)]))
                        c.link(v.tensor_copy(cols[:, k, 1, :], dstB[:, bass.ds((i * 2 + k) * K, K)]))
                        v.tensor_tensor(hotP[:, k], cols[:, k, 0, :].unsqueeze(2).to_broadcast([P, K, P]),
                                        iotaF[:, :].unsqueeze(1).to_broadcast([P, K, P]), ALU.is_equal).then_inc(hot[k], 1)
                        v.tensor_tensor(hotB[:, k], cols[:, k, 1, :].unsqueeze(2).to_broadcast([P, K, NB]),
                                        iotaF[:, 0:NB].unsqueeze(1).to_broadcast([P, K, NB]), ALU.is_equal).then_inc(hot[k], 1)
                c.end(NCH // 2)
                deg, cum, tot, start, has = (w[:, n, :] for n in range(5))
                t1, q, cross, end, t2 = (w[:, n, :] for n in range(5, 10))
                v.wait_ge(rows, 1)
                c.mark(v.tensor_copy(g.contLrow[:, :], psR[:, 0, 0:P]))
                c.mark(v.tensor_copy(g.contRrow[:, :], psR[:, 1, 0:P]))
                v.wait_ge(rows, 2)
                c.link(v.tensor_copy(deg, psC[:, 0:NB]))
                c.link(v.tensor_tensor_scan(cum, ones[:, 0:NB], deg, 0.0, ALU.mult, ALU.add))
                c.link(v.tensor_copy(tot[:, 0:1], cum[:, NB - 1:NB]))
                v.sem_inc(total, 1)
                v.wait_ge(rows, 3)
                c.link(v.tensor_copy(tot[:, 1:2], psE[:, 0:1]))
                c.link(v.tensor_scalar(end, cum, tot[:, 1:2], -1.0, ALU.add, ALU.add))
                c.link(v.scalar_tensor_tensor(start, deg, -1.0, end, ALU.mult, ALU.add))
                c.link(v.tensor_scalar(start, start, 1.0, None, ALU.add))
                c.link(v.tensor_scalar(has, deg, 0.0, None, ALU.is_gt))
                c.mark(v.tensor_copy(g.has[:, :], has))
                c.mark(v.tensor_scalar(g.nothas[:, :], has, -1.0, 1.0, ALU.mult, ALU.add))
                c.link(v.tensor_scalar(t1, deg, 1.0, None, ALU.max))
                v.sem_inc(sq, 1)
                c.link(v.tensor_scalar(q, end, 1.0 / J, -(0.5 - 0.5 / J), ALU.mult, ALU.add))
                c.link(v.tensor_scalar(q, q, WHOLE, -WHOLE, ALU.add, ALU.add))
                c.link(v.scalar_tensor_tensor(cross, q, float(J), start, ALU.mult, ALU.is_gt))
                c.link(v.tensor_tensor(cross, cross, has, ALU.mult))
                c.link(v.tensor_tensor(cross, cross, q, ALU.mult))
                c.mark(v.tensor_copy(g.idxCar[:, :], cross))
                c.link(v.tensor_scalar(t2, end, -float(EP), None, ALU.add))
                c.link(v.tensor_tensor(t2, t2, has, ALU.mult))
                c.link(v.tensor_scalar(t2, t2, float(EP), None, ALU.add))
                c.link(v.tensor_copy(g.idxEnd[:, :], t2))
                c.link(v.tensor_scalar(nodeF[:, :], nodeF[:, :], float(EP), None, ALU.add))
                c.link(v.tensor_tensor(t2, start, nodeF[:, :], ALU.subtract))
                c.link(v.tensor_tensor(t2, t2, has, ALU.mult))
                c.link(v.tensor_tensor(t2, t2, nodeF[:, :], ALU.add))
                c.link(v.tensor_copy(g.idxStart[:, :], t2))
                v.wait_ge(sqd, 1)
                c.link(v.reciprocal(g.dinv[:, :], g.dinv[:, :]))
                c.link(v.tensor_tensor(g.dinv[:, :], g.dinv[:, :], has, ALU.mult))

            @block.scalar
            def _(act):
                act.wait_ge(sq, 1)
                act.activation(g.dinv[:, :], w[:, 5, :], ACT.Sqrt).then_inc(sqd, 1)

            @block.tensor
            def _(pe):
                pe.sem_inc(counted[0], 1)
                pe.sem_inc(counted[1], 1)
                pe.wait_ge(made, 7)
                pe.wait_ge(split, 1)
                pe.matmul(psR[:, 0, 0:P], ones[:, :], diag[:, 0, :], start=True, stop=True)
                pe.matmul(psR[:, 1, 0:P], ones[:, :], diag[:, 1, :], start=True, stop=True).then_inc(rows, 1)
                pe.matmul(psC[:, 0:NB], zero[:, :], zero[:, 0:NB], start=True, stop=False, skip_group_check=True)
                with pe.Fori(0, NCH // 2) as i:
                    for k in range(2):
                        pe.wait_ge(hot[k], i * 2 + 2)
                        for j in range(K):
                            last = pe.matmul(psC[:, 0:NB], hotP[:, k, j, :], hotB[:, k, j, :], start=False,
                                             stop=False, skip_group_check=True)
                        last.then_inc(counted[k], 1)
                pe.matmul(psC[:, 0:NB], zero[:, :], zero[:, 0:NB], start=False, stop=True,
                          skip_group_check=True).then_inc(rows, 1)
                pe.wait_ge(total, 1)
                pe.matmul(psE[:, 0:1], lower[:, :], w[:, 2, 0:1], start=True, stop=True).then_inc(rows, 1)


def relation_table(nc, g, a):
    with phase(nc) as s:
        w = s.sb("relw", [D, R * D])
        xT = s.sb("xT", [D, 2, P])
        stage = s.sb("stage", [P, 2, R, 2 * D])
        zero = s.sb("zerof", [P, 3236])
        psT = s.ps("psT", [D, 2, 512])
        psH = s.ps("psH", [P, 2, 1024])
        loaded, zeroed, zeros = s.sem("w_loaded"), s.sem("zeroed"), s.sem("zeros_stored")
        turned, xT_ready, x_put = s.sem("turned"), s.sem("xT_ready"), s.sem("x_put")
        made = [s.sem(f"half_made{h}") for h in range(2)]
        evac = [s.sem(f"half_out{h}") for h in range(2)]
        stored = [s.sem(f"hpx_stored{k}") for k in range(2)]
        with nc.Block() as block:
            @block.sync
            def _(sp):
                sp.dma_start(w[:, :].rearrange("d (r e) -> d r e", r=R),
                             a["relw"].rearrange("r d e -> d r e")).then_inc(loaded, 16)
                for b in range(NB):
                    sp.wait_ge(evac[0], b + 1)
                    sp.wait_ge(evac[1], b + 1)
                    sp.wait_ge(x_put, b + 1)
                    sp.dma_start(g.hpx[0:NR * R, :].rearrange("(p b r) c -> p b (r c)", b=NB, r=R)[:, b, :],
                                 stage[:, b % 2].rearrange("p r c -> p (r c)")).then_inc(stored[b % 2], 16)
                for k in range(2):
                    sp.wait_ge(stored[k], 16 * ((NB + 1 - k) // 2))

            @block.gpsimd
            def _(pool):
                pool.memset(zero[:, :], 0.0).then_inc(zeroed, 1)
                for b in range(NB):
                    if b >= 2:
                        pool.wait_ge(stored[b % 2], 16 * (b // 2))
                    pool.tensor_copy(stage[:, b % 2, :, D:2 * D],
                                     g.x[:, b, :].unsqueeze(1).to_broadcast([P, R, D])).then_inc(x_put, 1)

            @block.tensor
            def _(pe):
                for b in range(NB):
                    pe.transpose(psT[:, b % 2, 0:P], g.x[:, b, :], g.ident[:, :]).then_inc(turned, 1)
                    pe.wait_ge(xT_ready, b + 1)
                    if b == 0:
                        pe.wait_ge(loaded, 16)
                    for h in range(2):
                        if b >= 1:
                            pe.wait_ge(evac[h], b)
                        for q in range(2):
                            last = pe.matmul(psH[:, h, q * 512:(q + 1) * 512], xT[:, b % 2, :],
                                             w[:, (2 * h + q) * 512:(2 * h + q + 1) * 512], start=True, stop=True)
                        last.then_inc(made[h], 1)

            @block.scalar
            def _(act):
                act.wait_ge(zeroed, 1)
                z = zero.shape[1]
                for n in range(16):
                    act.dma_start(g.start_rows.rearrange("(p j) c -> p (j c)", p=P)[:, n * z:(n + 1) * z],
                                  zero[:, :]).then_inc(zeros, 16)
                act.dma_start(g.start_self.rearrange("(p j) c -> p (j c)", p=P)[:, 0:2048],
                              zero[:, 0:2048]).then_inc(zeros, 16)
                act.dma_start(g.start_self.rearrange("(p j) c -> p (j c)", p=P)[:, 2048:4045],
                              zero[:, 0:1997]).then_inc(zeros, 16)
                act.dma_start(g.scanned[EP:EP + P, :], zero[:, 0:D]).then_inc(zeros, 16)
                act.dma_start(g.self_weight[EP:EP + P, :], zero[:, 0:H]).then_inc(zeros, 16)
                for b in range(NB):
                    act.wait_ge(turned, b + 1)
                    if b >= 2:
                        act.wait_ge(made[1], b - 1)
                    act.activation(xT[:, b % 2, :], psT[:, b % 2, 0:P], ACT.Copy).then_inc(xT_ready, 1)
                    act.wait_ge(made[0], b + 1)
                    if b >= 2:
                        act.wait_ge(stored[b % 2], 16 * (b // 2))
                    act.activation(stage[:, b % 2, 0:R // 2, 0:D],
                                   psH[:, 0, :].rearrange("p (r e) -> p r e", e=D), ACT.Copy).then_inc(evac[0], 1)
                act.wait_ge(zeros, 16 * 20)

            @block.vector
            def _(v):
                for b in range(NB):
                    v.wait_ge(made[1], b + 1)
                    if b >= 2:
                        v.wait_ge(stored[b % 2], 16 * (b // 2))
                    v.tensor_copy(stage[:, b % 2, R // 2:R, 0:D],
                                  psH[:, 1, :].rearrange("p (r e) -> p r e", e=D)).then_inc(evac[1], 1)


def gather_columns(pool, table, width, index, stage, buf, c, i, k, done, staged):
    c.link(pool.tensor_copy(stage[:, k, :], index[:, bass.ds((i * 2 + k) * K, K)]))
    pool.sem_inc(staged, 1)
    for j in range(K):
        pool.indirect_dma_start(buf[:, k, j, 0:width] if width == buf.shape[3] else buf[:, k, j, D:2 * D], None,
                                table, bass.IndirectOffsetOnAxis(stage[:, k, j:j + 1], 0)).then_inc(done[k], 16)


def relation_scores(nc, g, a):
    with phase(nc) as s:
        stS, stD = s.sb("stS", [P, 2, K], i32), s.sb("stD", [P, 2, K], i32)
        rows_s, rows_d = s.sb("rows_s", [P, 2, K, 2 * D]), s.sb("rows_d", [P, 2, K, 2 * D])
        ef = s.sb("ef", [P, 2, K, D])
        sc = s.sb("sc", [P, 2, K])
        got_s = [s.pool_sem(g, k) for k in range(2)]
        got_d = [s.pool_sem(g, 2 + k) for k in range(2)]
        edge = [s.sem(f"edge{k}") for k in range(2)]
        stored = [s.sem(f"x_src_stored{k}") for k in range(2)]
        used, kept = [s.sem(f"used{k}") for k in range(2)], [s.sem(f"kept{k}") for k in range(2)]
        summed, tanh, pool_c, dve_c, staged = s.sem("summed"), s.sem("tanh"), s.sem("pool_c"), s.sem("dve_c"), s.sem("staged")
        with nc.Block() as block:
            @block.sync
            def _(sp):
                with sp.Fori(0, NCH // 2) as i:
                    for k in range(2):
                        sp.wait_ge(used[k], i + 1)
                        sp.dma_start(ef[:, k].rearrange("p j c -> p (j c)"),
                                     a["ef"].rearrange("(p j) c -> p (j c)", p=P)[:, bass.ds((i * 2 + k) * (K * D), K * D)]
                                     ).then_inc(edge[k], 16)

            @block.gpsimd
            def _(pool):
                c = Chain(pool, pool_c)
                with pool.Fori(0, NCH // 2) as i:
                    c.begin(i, 4)
                    for k in range(2):
                        pool.wait_ge(used[k], i + 1)
                        pool.wait_ge(kept[k], i + 1)
                        gather_columns(pool, g.hpx, 2 * D, g.hpS, stS, rows_s, c, i, k, got_s, staged)
                        gather_columns(pool, g.hpx, 2 * D, g.hpD, stD, rows_d, c, i, k, got_d, staged)
                c.end(NCH // 2)

            @block.vector
            def _(v):
                c = Chain(v, dve_c)
                for k in range(2):
                    v.sem_inc(used[k], 1)
                with v.Fori(0, NCH // 2) as i:
                    c.begin(i, 4)
                    for k in range(2):
                        v.wait_ge(edge[k], i * 16 + 16)
                        v.wait_ge(got_d[k], i * (16 * K) + 16 * K)
                        v.tensor_tensor(ef[:, k], ef[:, k], rows_d[:, k, :, 0:D], ALU.add).then_inc(summed, 1)
                        v.wait_ge(tanh, i * 2 + k + 1)
                        v.wait_ge(got_s[k], i * (16 * K) + 16 * K)
                        c.link(v.tensor_tensor(ef[:, k], ef[:, k], rows_s[:, k, :, 0:D], ALU.mult))
                        c.link(v.tensor_reduce(sc[:, k, :], ef[:, k], X, ALU.add))
                        v.tensor_copy(g.score[:, 0, bass.ds((i * 2 + k) * K, K)], sc[:, k, :]).then_inc(used[k], 1)
                c.end(NCH // 2)

            @block.scalar
            def _(act):
                for k in range(2):
                    act.sem_inc(kept[k], 1)
                with act.Fori(0, NCH // 2) as i:
                    for k in range(2):
                        act.wait_ge(got_s[k], i * (16 * K) + 16 * K)
                        act.dma_start(g.x_src.rearrange("(p j) c -> p j c", p=P)[:, bass.ds((i * 2 + k) * K, K), :],
                                      rows_s[:, k, :, D:2 * D]).then_inc(stored[k], 16)
                        act.wait_ge(summed, i * 2 + k + 1)
                        act.activation(ef[:, k], ef[:, k], ACT.Tanh).then_inc(tanh, 1)
                        act.wait_ge(stored[k], i * 16 + 16)
                        act.sem_inc(kept[k], 1)


def carry_over(nc, g, s, heads, first, last, out, combine):
    big = combine == ALU.max
    neutral = -BIG if big else 0.0
    flag = s.sb("flag", [P, 2, P])
    left, right = s.sb("left", [D, P + 1]), s.sb("right", [D, P + 1])
    ps = s.ps("ps_carry", [P, 2, P])
    pt = s.ps("ps_carried", [P, 2, D])
    ready, turned, scanned, back, chain = (s.sem(f"carry_{n}") for n in ("ready", "turned", "scanned", "back", "chain"))
    with nc.Block() as block:
        @block.vector
        def _(v):
            c = Chain(v, chain)
            for n, row in enumerate((g.contLrow, g.contRrow)):
                if big:
                    c.mark(v.tensor_scalar(flag[:, n, :], row[:, :], BIG, -BIG, ALU.mult, ALU.add))
                else:
                    c.mark(v.tensor_copy(flag[:, n, :], row[:, :]))
            c.mark(v.memset(left[:, 0:1], neutral))
            c.link(v.memset(right[:, P:P + 1], neutral))
            op = ALU.add if big else ALU.mult
            v.wait_ge(turned, 1)
            v.tensor_tensor_scan(left[0:heads, 1:P + 1], flag[0:heads, 0, :], ps[0:heads, 0, :], neutral, op, combine)
            v.tensor_tensor_scan(right[0:heads, 0:P][:, ::-1], flag[0:heads, 1, ::-1], ps[0:heads, 1, ::-1], neutral,
                                 op, combine).then_inc(scanned, 1)
            v.wait_ge(back, 1)
            c.link(v.tensor_copy(out, pt[:, :, 0:heads]))

        @block.tensor
        def _(pe):
            pe.transpose(ps[0:heads, 0, :], last, g.ident[:, :])
            pe.transpose(ps[0:heads, 1, :], first, g.ident[:, :]).then_inc(turned, 1)
            pe.wait_ge(scanned, 1)
            pe.transpose(pt[:, 0, 0:heads], left[0:heads, 0:P], g.ident[0:heads, 0:heads])
            pe.transpose(pt[:, 1, 0:heads], right[0:heads, 1:P + 1], g.ident[0:heads, 0:heads]).then_inc(back, 1)


def softmax(nc, g, heads, selfs=None):
    for stage, combine in (("max", ALU.max), ("sum", ALU.add)):
        with phase(nc) as s:
            run = s.sb("run", [P, 2, J])
            total = s.sb("total", [P, heads, J])
            ends = s.sb("ends", [P, 2, heads])
            carried = s.sb("carried", [P, 2, heads])
            pen = s.sb("pen", [P, 3, J])
            chain, shifted, exped = s.sem("chain"), s.sem("shifted"), s.sem("exped")
            with nc.Block() as block:
                @block.vector
                def _(v):
                    c = Chain(v, chain)
                    if stage == "max":
                        for n, m in enumerate((g.cont, g.Lm, g.Rm)):
                            c.link(v.tensor_scalar(pen[:, n, :], m[:, :], BIG, -BIG, ALU.mult, ALU.add))
                    for h in range(heads):
                        if stage == "max":
                            c.link(v.tensor_tensor_scan(run[:, 0, :], pen[:, 0, :], g.score[:, h, :], -BIG, ALU.add, ALU.max))
                        else:
                            c.link(v.tensor_tensor_scan(run[:, 0, :], g.cont[:, :], g.score[:, h, :], 0.0, ALU.mult, ALU.add))
                        c.link(v.tensor_tensor(run[:, 1, :], run[:, 0, :], g.isend[:, :], ALU.mult))
                        c.link(v.tensor_tensor_scan(total[:, h, ::-1], g.notend[:, ::-1], run[:, 1, ::-1], 0.0, ALU.mult, ALU.add))
                        c.mark(v.tensor_copy(ends[:, 0, h:h + 1], total[:, h, 0:1]))
                        c.link(v.tensor_copy(ends[:, 1, h:h + 1], total[:, h, J - 1:J]))
            carry_over(nc, g, s, heads, ends[:, 0, :], ends[:, 1, :], carried[:, :, :], combine)
            with nc.Block() as block:
                @block.vector
                def _(v):
                    c = Chain(v, chain)
                    c.n = (3 if stage == "max" else 0) + 5 * heads
                    if stage == "max":
                        for h in range(heads):
                            for n in range(2):
                                c.link(v.scalar_tensor_tensor(total[:, h, :], pen[:, 1 + n, :], carried[:, n, h:h + 1],
                                                              total[:, h, :], ALU.add, ALU.max))
                        if selfs is not None:
                            c.link(v.tensor_tensor(total[:, :, :], total[:, :, :], selfs, ALU.max))
                            c.mark(v.tensor_tensor(selfs, selfs, total[:, :, :], ALU.subtract))
                        c.link(v.tensor_tensor(g.score[:, 0:heads, :], g.score[:, 0:heads, :], total[:, :, :], ALU.subtract))
                        v.sem_inc(shifted, 1)
                    else:
                        for h in range(heads):
                            for n, m in enumerate((g.Lm, g.Rm)):
                                c.link(v.scalar_tensor_tensor(total[:, h, :], m[:, :], carried[:, n, h:h + 1],
                                                              total[:, h, :], ALU.mult, ALU.add))
                        if selfs is not None:
                            c.link(v.tensor_tensor(total[:, :, :], total[:, :, :], selfs, ALU.add))
                            c.link(v.tensor_scalar(total[:, :, :], total[:, :, :], 1.0e-16, None, ALU.add))
                        c.link(v.reciprocal(total[:, :, :], total[:, :, :]))
                        if selfs is not None:
                            c.link(v.tensor_scalar(total[:, :, :], total[:, :, :], 1.0 / H, None, ALU.mult))
                            c.mark(v.tensor_tensor(selfs, selfs, total[:, :, :], ALU.mult))
                        c.link(v.tensor_tensor(g.score[:, 0:heads, :], g.score[:, 0:heads, :], total[:, :, :], ALU.mult))

                if stage == "max":
                    @block.scalar
                    def _(act):
                        act.wait_ge(shifted, 1)
                        if selfs is not None:
                            act.activation(selfs, selfs, ACT.Exp).then_inc(exped, 1)
                        act.activation(g.score[:, 0:heads, :], g.score[:, 0:heads, :], ACT.Exp).then_inc(exped, 1)


def scan_columns(v, c, out, data, prev, cont):
    for f in range(D):
        last = v.tensor_tensor_scan(out[:, :, f], cont, data[:, :, f], prev[:, f:f + 1], ALU.mult, ALU.add)
    c.link(last)


def weighted_sums(nc, g, name):
    with phase(nc) as s:
        rows, run = s.sb("rows", [P, 2, K, D]), s.sb("run", [P, 2, K, D])
        cs, ws = s.sb("cs", [P, 2, K]), s.sb("ws", [P, 2, K])
        got = [s.sem(f"got{k}") for k in range(2)]
        used, free = [s.sem(f"used{k}") for k in range(2)], [s.sem(f"free{k}") for k in range(2)]
        stored = [s.sem(f"stored{k}") for k in range(2)]
        ready, dve_c = s.sem("ready"), s.sem("dve_c")
        with nc.Block() as block:
            @block.sync
            def _(sp):
                with sp.Fori(0, NCH // 2) as i:
                    for k in range(2):
                        sp.wait_ge(used[k], i + 1)
                        sp.dma_start(rows[:, k].rearrange("p j c -> p (j c)"),
                                     g.x_src.rearrange("(p j) c -> p (j c)", p=P)[:, bass.ds((i * 2 + k) * (K * D), K * D)]
                                     ).then_inc(got[k], 16)

            @block.vector
            def _(v):
                c = Chain(v, dve_c)
                for k in range(2):
                    v.sem_inc(used[k], 1)
                c.link(v.memset(run[:, 1, K - 1, :], 0.0))
                with v.Fori(0, NCH // 2) as i:
                    c.begin(i, 8)
                    for k in range(2):
                        c.mark(v.tensor_copy(cs[:, k, :], g.cont[:, bass.ds((i * 2 + k) * K, K)]))
                        c.link(v.tensor_copy(ws[:, k, :], g.score[:, 0, bass.ds((i * 2 + k) * K, K)]))
                        v.wait_ge(got[k], i * 16 + 16)
                        c.link(v.tensor_tensor(rows[:, k], rows[:, k], ws[:, k, :].unsqueeze(2).to_broadcast([P, K, D]), ALU.mult))
                        v.wait_ge(free[k], i + 1)
                        scan_columns(v, c, run[:, k], rows[:, k], run[:, 1 - k, K - 1, :], cs[:, k, :])
                        v.sem_inc(used[k], 1)
                        v.sem_inc(ready, 1)
                c.end(NCH // 2)
                v.tensor_copy(g.tail[:, :], run[:, 1, K - 1, :]).then_inc(dve_c, 1)
                v.wait_ge(dve_c, c.n + 1)

            @block.scalar
            def _(act):
                store_runs(act, g, run, ready, stored, free)


def store_run(eng, g, run, i, k, stored):
    eng.dma_start(g.scanned[0:EP, :].rearrange("(p j) c -> p (j c)", p=P)[:, bass.ds((i * 2 + k) * (K * D), K * D)],
                  run[:, k].rearrange("p j c -> p (j c)")).then_inc(stored[k], 16)


def store_runs(eng, g, run, ready, stored, free):
    for k in range(2):
        eng.sem_inc(free[k], 1)
    with eng.Fori(0, NCH // 2) as i:
        for k in range(2):
            eng.wait_ge(ready, i * 2 + k + 1)
            store_run(eng, g, run, i, k, stored)
            eng.wait_ge(stored[k], i * 16 + 16)
            eng.sem_inc(free[k], 1)


def node_sums(nc, g, out):
    with phase(nc) as s:
        part = s.sb("part", [P, NB, D])
        carried = s.sb("carried", [P, 2, D])
        carry_over(nc, g, s, D, g.tail[:, :], g.tail[:, :], carried[:, :, :], ALU.add)
        kept, got_e, got_c, chain = s.sem("kept"), s.pool_sem(g, 0), s.pool_sem(g, 1), s.sem("chain")
        with nc.Block() as block:
            @block.sync
            def _(sp):
                sp.dma_start(g.carry, carried[:, 0, :]).then_inc(kept, 16)
                sp.wait_ge(kept, 16)

            @block.gpsimd
            def _(pool):
                for b in range(NB):
                    pool.indirect_dma_start(out[:, b, :], None, g.scanned,
                                            bass.IndirectOffsetOnAxis(g.idxEnd[:, b:b + 1], 0)).then_inc(got_e, 16)
                pool.wait_ge(kept, 16)
                for b in range(NB):
                    pool.indirect_dma_start(part[:, b, :], None, g.carry,
                                            bass.IndirectOffsetOnAxis(g.idxCar[:, b:b + 1], 0)).then_inc(got_c, 16)

            @block.vector
            def _(v):
                v.wait_ge(got_e, 16 * NB)
                v.wait_ge(got_c, 16 * NB)
                v.tensor_tensor(out[:, :, :], out[:, :, :], part[:, :, :], ALU.add).then_inc(chain, 1)
                v.wait_ge(chain, 1)


def node_linear(nc, g, srcs, weights, out):
    with phase(nc) as s:
        S, nout = len(srcs), out.shape[3]
        kin = srcs[0].shape[2]
        xT = s.sb("xT", [kin, 2, S, P])
        psT = s.ps("psT", [kin, 2, 512])
        psZ = s.ps("psZ", [P, 2, 512])
        turned, ready, made, evac = (s.sem(n) for n in ("turned", "ready", "made", "evac"))
        with nc.Block() as block:
            @block.tensor
            def _(pe):
                for b in range(NB):
                    for n in range(S):
                        last = pe.transpose(psT[:, b % 2, n * P:(n + 1) * P], srcs[n][:, b, :], g.ident[:, :])
                    last.then_inc(turned, 1)
                    pe.wait_ge(ready, b + 1)
                    if b >= 2:
                        pe.wait_ge(evac, b - 1)
                    for n in range(S):
                        last = pe.matmul(psZ[:, b % 2, n * nout:(n + 1) * nout], xT[:, b % 2, n, :], weights[n],
                                         start=True, stop=True)
                    last.then_inc(made, 1)

            @block.scalar
            def _(act):
                for b in range(NB):
                    act.wait_ge(turned, b + 1)
                    if b >= 2:
                        act.wait_ge(made, b - 1)
                    act.activation(xT[:, b % 2], psT[:, b % 2, 0:S * P].rearrange("k (s e) -> k s e", s=S),
                                   ACT.Copy).then_inc(ready, 1)

            @block.vector
            def _(v):
                for b in range(NB):
                    v.wait_ge(made, b + 1)
                    v.tensor_copy(out[:, b], psZ[:, b % 2, 0:S * nout].rearrange("p (s n) -> p s n", s=S)).then_inc(evac, 1)
                v.wait_ge(evac, NB)


def layernorm(v, c, data, tmp, stat, var_ready, std_ready, at=1):
    over = lambda t: t.unsqueeze(2).to_broadcast([P, NB, D])
    c.link(v.tensor_reduce(stat[:, 0, :], data, X, ALU.add))
    c.link(v.tensor_scalar(stat[:, 0, :], stat[:, 0, :], 1.0 / D, None, ALU.mult))
    c.link(v.tensor_tensor(data, data, over(stat[:, 0, :]), ALU.subtract))
    c.link(v.tensor_tensor(tmp, data, data, ALU.mult))
    c.link(v.tensor_reduce(stat[:, 1, :], tmp, X, ALU.add))
    v.tensor_scalar(stat[:, 1, :], stat[:, 1, :], 1.0 / D, LN_EPS, ALU.mult, ALU.add).then_inc(var_ready, 1)
    v.wait_ge(std_ready, at)
    c.link(v.reciprocal(stat[:, 2, :], stat[:, 2, :]))
    c.link(v.tensor_tensor(data, data, over(stat[:, 2, :]), ALU.mult))


def root(act, stat, var_ready, std_ready, at=1):
    act.wait_ge(var_ready, at)
    act.activation(stat[:, 2, :], stat[:, 1, :], ACT.Sqrt).then_inc(std_ready, 1)


def relation_output(nc, g, a, nbh):
    with phase(nc) as s:
        ab = s.sb("ab", [P, 2, NB, D])
        wr, wT = s.sb("wr", [D, 2, D]), s.sb("wT", [D, 2, D])
        z = s.sb("z", [P, NB, 2, D])
        stat = s.sb("stat", [P, 3, NB])
        ps = s.ps("psw", [D, 2, D])
        loaded, turned, chain, var_ready, std_ready = (s.sem(n) for n in ("loaded", "wturned", "chain", "var", "std"))
        with nc.Block() as block:
            @block.sync
            def _(sp):
                sp.dma_start(wr[:, 0, :], a["rw1"]).then_inc(loaded, 16)
                sp.dma_start(wr[:, 1, :], a["rw2"]).then_inc(loaded, 16)

            @block.tensor
            def _(pe):
                pe.wait_ge(loaded, 32)
                for n in range(2):
                    last = pe.transpose(ps[:, n, :], wr[:, n, :], g.ident[0:D, 0:D])
                last.then_inc(turned, 1)

            @block.vector
            def _(v):
                c = Chain(v, chain)
                c.mark(v.tensor_tensor(ab[:, 0], g.x[:, :, :], nbh[:, :, :], ALU.add))
                c.mark(v.tensor_tensor(ab[:, 1], g.x[:, :, :], nbh[:, :, :], ALU.mult))
                v.wait_ge(turned, 1)
                c.link(v.tensor_copy(wT[:, :, :], ps[:, :, :]))
        node_linear(nc, g, [ab[:, 0], ab[:, 1]], [wT[:, 0, :], wT[:, 1, :]], z)
        with nc.Block() as block:
            @block.vector
            def _(v):
                c = Chain(v, chain)
                c.n = 3
                c.link(v.scalar_tensor_tensor(z[:, :, :, :].rearrange("p b s d -> p (b s d)"),
                                              z[:, :, :, :].rearrange("p b s d -> p (b s d)"), 0.01,
                                              z[:, :, :, :].rearrange("p b s d -> p (b s d)"), ALU.mult, ALU.max))
                c.link(v.tensor_tensor(g.x[:, :, :], g.x[:, :, :], z[:, :, 0, :], ALU.add))
                c.link(v.tensor_tensor(g.x[:, :, :], g.x[:, :, :], z[:, :, 1, :], ALU.add))
                layernorm(v, c, g.x[:, :, :], ab[:, 0], stat, var_ready, std_ready)

            @block.scalar
            def _(act):
                root(act, stat, var_ready, std_ready)


def adjacency(nc, g, a):
    g.same, g.prefix = g.step.sb("same", [SP, SQ]), g.step.sb("prefix", [SP, SQ])
    g.hand = g.step.sb("hand", [SP, SP])
    g.last_step = g.step.sb("last_step", [NW // WD, NB // WD], i32)
    with phase(nc) as s:
        colsT = s.sb("colsT", [P, 2, S], bf16)
        iotaB = s.sb("iotaB", [P, P], bf16)
        with phase(nc) as t:
            first_i, first = t.sb("first_i", [CH // 7, 7], i32), t.sb("first", [CH // 7, 7])
            ones, iotaI = t.sb("ones", [P, P]), t.sb("iotaI", [P, P], i32)
            diag = t.sb("diag", [CH // 7, 7, CH // 7])
            win, begin = t.sb("win", [P, CH]), t.sb("begin", [P, CH])
            chunk_i, stepG_i, stepR_i, win_i = (t.sb("chunk_i", [P, 7, CH // 7], i32), t.sb("stepG_i", [SP, SQ], i32),
                                                t.sb("stepR_i", [SP, SQ + 1], i32), t.sb("win_i", [NW // WD, WD], i32))
            stepG, stepR, winF = t.sb("stepG", [SP, SQ]), t.sb("stepR", [SP, SQ + 1]), t.sb("winF", [NW // WD, WD])
            before = t.sb("before", [P, SQ + 1, CH], bf16)
            chG, chR, chW = t.sb("chG", [SP, SQ]), t.sb("chR", [SP, SQ + 1]), t.sb("chW", [NW // WD, WD])
            chG_i = t.sb("chG_i", [SP, SQ], i32)
            raw = t.sb("raw", [SP, 2, SQ, CE], i32)
            srcF, dstF, quo = t.sb("srcF_c", [SP, SQ, CE]), t.sb("dstF_c", [SP, SQ, CE]), t.sb("quo", [SP, SQ, CE])
            shift, band, diag2 = t.sb("shift", [SP, SP]), t.sb("band", [SP, SP]), t.sb("diag2", [SP, SP])
            psW, psS, psT = t.ps("psW", [P, 2, 512]), t.ps("psS", [P, 512]), t.ps("psT", [P, 2, 512])
            loaded, made, dve, cols, wide, flags, spread, turned, taken = (
                t.sem(n) for n in ("loaded", "made", "dve", "cols", "wide", "flags", "spread", "turned", "taken"))
            got, rows_in = t.pool_sem(g, 0), t.sem("rows_in")
            with nc.Block() as block:
                @block.sync
                def _(sp):
                    sp.dma_start(first_i[:, :].unsqueeze(2), a["dst"].rearrange("(p q e) -> p q e", q=7, e=CE)[:, :, 0:1],
                                 allow_slow_non_contiguous=True).then_inc(loaded, 16)
                    sp.wait_ge(loaded, 16)

                @block.gpsimd
                def _(pool):
                    pool.memset(ones[:, :], 1.0).then_inc(made, 1)
                    pool.iota(iotaI[:, :], pattern=[[1, P]], base=0, channel_multiplier=0).then_inc(made, 1)
                    pool.iota(chunk_i[:, :, :], pattern=[[1, 7], [7, CH // 7]], base=0, channel_multiplier=0).then_inc(made, 1)
                    pool.iota(stepG_i[:, :], pattern=[[SP, SQ]], base=0, channel_multiplier=1).then_inc(made, 1)
                    pool.iota(stepR_i[:, :], pattern=[[1, SQ + 1]], base=-1, channel_multiplier=SQ).then_inc(made, 1)
                    pool.iota(win_i[:, :], pattern=[[1, WD]], base=0, channel_multiplier=WD).then_inc(made, 1)
                    pool.wait_ge(made, 6)
                    pool.memset(band[:, :], 0.0).then_inc(made, 1)
                    pool.wait_ge(made, 7)
                    pool.affine_select(out=band[:, :], in_=band[:, :], compare_op=ALU.not_equal, fill=1.0,
                                       base=1, pattern=[[-1, SP]], channel_multiplier=1).then_inc(made, 1)
                    pool.wait_ge(made, 8)
                    pool.wait_ge(cols, 1)
                    for q in range(SQ):
                        for n, name in enumerate(("src", "dst")):
                            pool.indirect_dma_start(raw[:, n, q, :], None, a[name].rearrange("(c e) -> c e", e=CE),
                                                    bass.IndirectOffsetOnAxis(chG_i[:, q:q + 1], 0)).then_inc(got, 16)
                    pool.wait_ge(got, 2 * SQ * 16)
                    pool.sem_inc(rows_in, 1)

                @block.tensor
                def _(pe):
                    pe.wait_ge(wide, 1)
                    for q in range(7):
                        at = (q % 4) * (CH // 7)
                        last = pe.matmul(psW[:, q // 4, at:at + CH // 7], ones[0:CH // 7, :], diag[:, q, :], start=True, stop=True)
                    last.then_inc(spread, 1)
                    pe.wait_ge(flags, 1)
                    pe.matmul(psS[0:SP, 0:SP], ones[0:SP, 0:SP], diag2[:, :], start=True, stop=True).then_inc(spread, 1)
                    pe.wait_ge(wide, 2)
                    for q in range(SQ):
                        if q >= 2:
                            pe.wait_ge(taken, q - 1)
                        pe.transpose(psT[:, q % 2, 0:SP], quo[:, q, :], g.ident[0:SP, 0:SP])
                        pe.transpose(psT[:, q % 2, P:P + SP], dstF[:, q, :], g.ident[0:SP, 0:SP]).then_inc(turned, 1)

                @block.vector
                def _(v):
                    c = Chain(v, dve)
                    v.wait_ge(loaded, 16)
                    v.wait_ge(made, 8)
                    c.mark(v.tensor_copy(iotaB[:, :], iotaI[:, :]))
                    c.mark(v.tensor_copy(stepG[:, :], stepG_i[:, :]))
                    c.mark(v.tensor_copy(stepR[:, :], stepR_i[:, :]))
                    c.mark(v.tensor_copy(winF[:, :], win_i[:, :]))
                    c.mark(v.tensor_copy(begin[:, :], chunk_i[:, :, :].rearrange("p q c -> p (q c)")))
                    c.link(v.tensor_copy(first[:, :], first_i[:, :]))
                    c.link(v.tensor_scalar(first[:, :], first[:, :], 1.0 / WD, -0.4, ALU.mult, ALU.add))
                    c.link(v.tensor_scalar(first[:, :], first[:, :], WHOLE, -WHOLE, ALU.add, ALU.add))
                    c.link(v.tensor_tensor(diag[:, :, :], first[:, :].unsqueeze(2).to_broadcast([CH // 7, 7, CH // 7]),
                                           g.ident[0:CH // 7, 0:CH // 7].unsqueeze(1).to_broadcast([CH // 7, 7, CH // 7]), ALU.mult))
                    v.sem_inc(wide, 1)
                    v.wait_ge(spread, 1)
                    half = 4 * (CH // 7)
                    c.mark(v.tensor_copy(win[:, 0:half], psW[:, 0, 0:half]))
                    c.link(v.tensor_copy(win[:, half:CH], psW[:, 1, 0:CH - half]))
                    c.link(v.tensor_tensor(begin[:, :], begin[:, :], win[:, :], ALU.add))

                    def chunks(out, bounds, at, rows, n):
                        c.link(v.tensor_tensor(before[0:rows, 0:n, :], bounds[0:rows, :].unsqueeze(1).to_broadcast([rows, n, CH]),
                                               at[:, :].unsqueeze(2).to_broadcast([rows, n, CH]), ALU.is_le))
                        c.link(v.tensor_reduce(out[:, :], before[0:rows, 0:n, :], X, ALU.add))
                        c.link(v.tensor_scalar(out[:, :], out[:, :], -1.0, None, ALU.add))

                    chunks(chG, begin, stepG, SP, SQ)
                    c.link(v.tensor_scalar(chG[:, :], chG[:, :], 0.0, None, ALU.max))
                    c.link(v.tensor_copy(chG_i[:, :], chG[:, :]))
                    v.sem_inc(cols, 1)
                    chunks(chR, begin, stepR, SP, SQ + 1)
                    c.link(v.tensor_tensor(g.same[:, :], chR[:, 1:SQ + 1], chR[:, 0:SQ], ALU.subtract))
                    c.link(v.tensor_tensor_scan(g.prefix[:, :], g.same[:, :], g.same[:, :], 1.0, ALU.mult, ALU.min))
                    c.link(v.tensor_scalar(diag2[:, :], g.ident[0:SP, 0:SP], g.prefix[:, SQ - 1:SQ], None, ALU.mult))
                    v.sem_inc(flags, 1)
                    chunks(chW, win, winF, NW // WD, WD)
                    c.link(v.tensor_scalar(chW[:, :], chW[:, :], 0.0, None, ALU.max))
                    c.link(v.tensor_tensor(chW[:, :], chW[:, :], winF[:, :], ALU.add))
                    c.link(v.tensor_copy(g.last_step[:, :], chW[:, :]))
                    v.wait_ge(spread, 2)
                    c.mark(v.memset(shift[:, 0:1], 0.0))
                    c.link(v.tensor_copy(shift[:, 1:SP], psS[0:SP, 0:SP - 1]))
                    c.link(v.tensor_tensor_scan(g.hand[:, :], shift[:, :], band[:, :], 0.0, ALU.mult, ALU.add))
                    c.link(v.tensor_tensor(stepG[:, :], stepG[:, :], chG[:, :], ALU.subtract))
                    c.link(v.tensor_scalar(stepG[:, :], stepG[:, :], float(WD * NB), None, ALU.mult))
                    v.wait_ge(rows_in, 1)
                    c.mark(v.tensor_copy(srcF[:, :, :], raw[:, 0]))
                    c.link(v.tensor_copy(dstF[:, :, :], raw[:, 1]))
                    c.link(v.tensor_scalar(quo[:, :, :], srcF[:, :, :], 1.0 / NB, -0.48, ALU.mult, ALU.add))
                    c.link(v.tensor_scalar(quo[:, :, :], quo[:, :, :], WHOLE, -WHOLE, ALU.add, ALU.add))
                    c.link(v.scalar_tensor_tensor(srcF[:, :, :], quo[:, :, :], -float(NB), srcF[:, :, :], ALU.mult, ALU.add))
                    c.link(v.scalar_tensor_tensor(dstF[:, :, :], dstF[:, :, :], float(NB), srcF[:, :, :], ALU.mult, ALU.add))
                    c.link(v.tensor_tensor(dstF[:, :, :], dstF[:, :, :], stepG[:, :].unsqueeze(2).to_broadcast([SP, SQ, CE]),
                                           ALU.subtract))
                    c.link(v.tensor_scalar(dstF[:, :, :], dstF[:, :, :], -1.0, 255.0, ALU.max, ALU.min))
                    v.sem_inc(wide, 1)
                    for q in range(SQ):
                        v.wait_ge(turned, q + 1)
                        v.tensor_copy(colsT[:, 0, q * SP:(q + 1) * SP], psT[:, q % 2, 0:SP])
                        v.tensor_copy(colsT[:, 1, q * SP:(q + 1) * SP], psT[:, q % 2, P:P + SP]).then_inc(taken, 1)
                    v.wait_ge(taken, SQ)

        cols = s.sb("cols", [P, 2, 2, TS], bf16)
        hot = s.sb("hot", [P, 2, 2 * TS, P], bf16)
        tile = s.sb("tile", [P, 2, NB, TC], bf16)
        GS = 4
        NG = (TS + GS - 1) // GS
        psA = s.ps("psA", [P, NG, 512])
        dve_c = s.sem("dve_c")
        hot_made, hot_used, stored = ([s.sem(f"{n}{k}") for k in range(2)] for n in ("hot_made", "hot_used", "stored"))
        counted, moved = s.sem("counted"), s.sem("moved")

        def steps(i, k, c, v):
            c.link(v.tensor_copy(cols[:, k], colsT[:, :, bass.ds(i * TS, TS)]))
            v.tensor_tensor(hot[:, k], cols[:, k].rearrange("p n s -> p (n s)").unsqueeze(2).to_broadcast([P, 2 * TS, P]),
                            iotaB[:, :].unsqueeze(1).to_broadcast([P, 2 * TS, P]), ALU.is_equal).then_inc(hot_made[k], 1)

        with nc.Block() as block:
            @block.vector
            def _(v):
                c = Chain(v, dve_c)
                with v.Fori(0, NT // 2) as i:
                    c.begin(i, 2)
                    for k in range(2):
                        v.wait_ge(hot_used[k], i + 1)
                        steps(i * 2 + k, k, c, v)
                c.end(NT // 2)
                v.wait_ge(hot_used[0], NT // 2 + 1)
                steps(NT - 1, 0, c, v)

            @block.tensor
            def _(pe):
                for k in range(2):
                    pe.sem_inc(hot_used[k], 1)

                def products(i, k, turn):
                    pe.wait_ge(hot_made[k], i + 1)
                    for n in range(NG):
                        at = k * NG + n
                        pe.wait_ge(moved, turn + NG + at + 1)
                        for j in range(min(GS, TS - n * GS)):
                            st = n * GS + j
                            last = pe.matmul(psA[:, at % NG, j * TC:(j + 1) * TC], hot[:, k, st, :], hot[:, k, TS + st, 0:TC],
                                             start=True, stop=True)
                        last.then_inc(counted, 1)
                    pe.wait_ge(counted, turn + at + 1)
                    pe.sem_inc(hot_used[k], 1)

                with pe.Fori(0, NT // 2) as i:
                    for k in range(2):
                        products(i, k, i * (2 * NG))
                pe.wait_ge(moved, 2 * NG * (NT // 2 + 1))
                products(NT // 2, 0, 2 * NG * (NT // 2))

            @block.scalar
            def _(act):
                act.sem_inc(moved, 2 * NG)
                for k in range(2):
                    act.sem_inc(stored[k], 16)

                def move(i, k, turn):
                    act.wait_ge(stored[k], i * 16 + 16)
                    for n in range(NG):
                        at, m = k * NG + n, min(GS, TS - n * GS)
                        act.wait_ge(counted, turn + at + 1)
                        act.activation(tile[:, k, :, n * GS * WD:(n * GS + m) * WD],
                                       psA[:, at % NG, 0:m * TC].rearrange("p (s a) -> p a s", a=NB), ACT.Copy).then_inc(moved, 1)

                with act.Fori(0, NT // 2) as i:
                    for k in range(2):
                        move(i, k, i * (2 * NG))
                move(NT // 2, 0, 2 * NG * (NT // 2))

            @block.sync
            def _(sp):
                def store(t, k, at):
                    sp.wait_ge(moved, at)
                    sp.dma_start(g.adj[bass.ds(t * P, P), :] if not isinstance(t, int) else g.adj[t * P:(t + 1) * P, :],
                                 tile[:, k].rearrange("p a c -> p (a c)")).then_inc(stored[k], 16)

                with sp.Fori(0, NT // 2) as i:
                    for k in range(2):
                        store(i * 2 + k, k, i * (2 * NG) + 2 * NG + (k + 1) * NG)
                store(NT - 1, 0, 2 * NG * (NT // 2) + 3 * NG)
                sp.wait_ge(stored[0], (NT // 2 + 2) * 16)
                sp.wait_ge(stored[1], (NT // 2 + 1) * 16)


def propagate(nc, g, y):
    with phase(nc) as s:
        parts = s.sb("parts", [P, NB, 3, D], bf16)
        with phase(nc) as t:
            rest = t.sb("rest", [P, NB, D])
            chain = t.sem("chain")
            with nc.Block() as block:
                @block.vector
                def _(v):
                    c = Chain(v, chain)
                    c.link(v.tensor_tensor(rest[:, :, :], y[:, :, :], g.dinv[:, :].unsqueeze(2).to_broadcast([P, NB, D]), ALU.mult))
                    for n in range(3):
                        c.link(v.tensor_copy(parts[:, :, n, :], rest[:, :, :]))
                        if n < 2:
                            c.link(v.tensor_tensor(rest[:, :, :], rest[:, :, :], parts[:, :, n, :], ALU.subtract))
        B = 3
        tile, z = s.sb("tile", [P, B, NB, TC], bf16), s.sb("z", [TC, B, D])
        psY = s.ps("psY", [P, B, 512])
        three = lambda name: [s.sem(f"{name}{k}") for k in range(B)]
        tile_in, used, product, summed, stored = (three(n) for n in ("tile_in", "used", "product", "summed", "stored"))
        with nc.Block() as block:
            @block.sync
            def _(sp):
                with sp.Fori(0, NT // B) as i:
                    for k in range(B):
                        sp.wait_ge(used[k], i + 1)
                        sp.dma_start(tile[:, k].rearrange("p a c -> p (a c)"),
                                     g.adj[bass.ds((i * B + k) * P, P), :]).then_inc(tile_in[k], 16)

            @block.tensor
            def _(pe):
                for k in range(B):
                    pe.sem_inc(used[k], 1)
                with pe.Fori(0, NT // B) as i:
                    for k in range(B):
                        pe.wait_ge(tile_in[k], i * 16 + 16)
                        pe.wait_ge(summed[k], i + 1)
                        for b in range(NB):
                            last = pe.matmul(psY[0:TC, k, 0:3 * D], tile[:, k, b, :], parts[:, b].rearrange("p n c -> p (n c)"),
                                             start=b == 0, stop=b == NB - 1)
                        last.then_inc(product[k], 1)
                        pe.wait_ge(product[k], i + 1)
                        pe.sem_inc(used[k], 1)

            @block.vector
            def _(v):
                for k in range(B):
                    v.sem_inc(summed[k], 1)
                with v.Fori(0, NT // B) as i:
                    for k in range(B):
                        v.wait_ge(product[k], i + 1)
                        v.wait_ge(stored[k], i * 16 + 16)
                        v.tensor_reduce(z[:, k, :], psY[0:TC, k, 0:3 * D].rearrange("p (n c) -> p c n", n=3), X, ALU.add
                                        ).then_inc(summed[k], 1)

            @block.scalar
            def _(act):
                for k in range(B):
                    act.sem_inc(stored[k], 16)
                with act.Fori(0, NT // B) as i:
                    for k in range(B):
                        act.wait_ge(summed[k], i + 2)
                        act.dma_start(g.step_rows[bass.ds((i * B + k) * TC, TC), :], z[:, k, :]).then_inc(stored[k], 16)
                for k in range(B):
                    act.wait_ge(stored[k], (NT // B + 1) * 16)
    with phase(nc) as s:
        acc, back = s.sb("acc", [SP, SQ, WD * D]), s.sb("back", [SP, WD * D])
        psH = s.ps("psH", [P, 512])
        loaded, chain, tails, handed, ready, put, got = (
            s.sem("loaded"), s.sem("chain"), s.sem("tails"), s.sem("handed"), s.sem("ready"), s.sem("put"), s.pool_sem(g, 0))
        with nc.Block() as block:
            @block.sync
            def _(sp):
                rows = lambda ap: ap.rearrange("(p q d) c -> p q (d c)", p=SP, d=WD)
                sp.dma_start(acc[:, :, :], rows(g.step_rows)).then_inc(loaded, 16)
                sp.wait_ge(ready, 1)
                sp.dma_start(rows(g.step_sums), acc[:, :, :]).then_inc(put, 16)

            @block.vector
            def _(v):
                c = Chain(v, chain)
                v.wait_ge(loaded, 16)
                for q in range(1, SQ):
                    c.link(v.scalar_tensor_tensor(acc[:, q, :], acc[:, q - 1, :], g.same[:, q:q + 1], acc[:, q, :], ALU.mult, ALU.add))
                v.sem_inc(tails, 1)
                v.wait_ge(handed, 1)
                c.link(v.tensor_copy(back[:, :], psH[0:SP, 0:WD * D]))
                for q in range(SQ):
                    c.mark(v.scalar_tensor_tensor(acc[:, q, :], back[:, :], g.prefix[:, q:q + 1], acc[:, q, :], ALU.mult, ALU.add))
                c.wait()
                v.sem_inc(ready, 1)

            @block.tensor
            def _(pe):
                pe.wait_ge(tails, 1)
                pe.matmul(psH[0:SP, 0:WD * D], g.hand[:, :], acc[:, SQ - 1, :], start=True, stop=True).then_inc(handed, 1)

            @block.gpsimd
            def _(pool):
                pool.wait_ge(put, 16)
                for q in range(WD):
                    pool.indirect_dma_start(y[0:NW // WD, q * WD:(q + 1) * WD, :].rearrange("p b c -> p (b c)"), None,
                                            g.step_sums.rearrange("(s d) c -> s (d c)", d=WD),
                                            bass.IndirectOffsetOnAxis(g.last_step[:, q:q + 1], 0)).then_inc(got, 16)
                pool.wait_ge(got, WD * 16)
    with phase(nc) as s:
        chain = s.sem("chain")
        with nc.Block() as block:
            @block.vector
            def _(v):
                c = Chain(v, chain)
                c.link(v.tensor_tensor(y[:, :, :], y[:, :, :], g.dinv[:, :].unsqueeze(2).to_broadcast([P, NB, D]), ALU.mult))


def add_norm(nc, g, terms, first=None):
    with phase(nc) as s:
        tmp, stat = s.sb("tmp", [P, NB, D]), s.sb("stat", [P, 3, NB])
        chain, var_ready, std_ready = s.sem("chain"), s.sem("var"), s.sem("std")
        with nc.Block() as block:
            @block.vector
            def _(v):
                c = Chain(v, chain)
                if first is not None:
                    first(v, c)
                for t in terms:
                    c.link(v.tensor_tensor(g.x[:, :, :], g.x[:, :, :], t, ALU.add))
                layernorm(v, c, g.x[:, :, :], tmp[:, :, :], stat, var_ready, std_ready)

            @block.scalar
            def _(act):
                root(act, stat, var_ready, std_ready)


def put_nodes(nc, g, h, loops=None):
    with phase(nc) as s:
        put, sent, got = s.sem("put"), s.pool_sem(g, 0), s.pool_sem(g, 1)
        with nc.Block() as block:
            @block.sync
            def _(sp):
                sp.dma_start(g.table.rearrange("(p b) d -> p b d", b=NB), h[:, :, :]).then_inc(put, 16)
                if loops is not None:
                    sp.dma_start(g.table_self.rearrange("(p b) d -> p b d", b=NB), loops[:, :, :]).then_inc(put, 16)

            @block.gpsimd
            def _(pool):
                for b in range(NB):
                    at = bass.IndirectOffsetOnAxis(g.idxStart[:, b:b + 1], 0)
                    pool.indirect_dma_start(g.start_rows, at, h[:, b, :], None).then_inc(sent, 16)
                    if loops is not None:
                        pool.indirect_dma_start(g.start_self, at, loops[:, b, :], None).then_inc(sent, 16)
                at = bass.IndirectOffsetOnAxis(g.row0[:, 0:1], 0)
                pool.wait_ge(put, 16 if loops is None else 32)
                pool.indirect_dma_start(g.row_start[:, :], None, g.table, at).then_inc(got, 16)
                if loops is not None:
                    pool.indirect_dma_start(g.row_self[:, :], None, g.table_self, at).then_inc(got, 16)
                pool.wait_ge(got, 16 if loops is None else 32)
                pool.wait_ge(sent, 16 * NB if loops is None else 32 * NB)


def split_bias(nc, row, b3, ones3):
    n = b3.shape[1]
    with phase(nc) as s:
        low = s.sb("low", [1, 3, n], bf16)
        moved, chain, split = s.sem("b_moved"), s.sem("b_chain"), s.sem("b_split")
        with nc.Block() as block:
            @block.sync
            def _(sp):
                sp.wait_ge(split, 1)
                for q in range(3):
                    sp.dma_start(b3[q:q + 1, :], low[0:1, q, :]).then_inc(moved, 16)
                sp.wait_ge(moved, 48)

            @block.vector
            def _(v):
                c = Chain(v, chain)
                c.mark(v.memset(ones3[:, :], 1.0))
                c.link(v.memset(b3[:, :], 0.0))
                for q in range(3):
                    c.link(v.tensor_copy(low[0:1, q, :], row))
                    if q < 2:
                        c.link(v.tensor_tensor(row, row, low[0:1, q, :], ALU.subtract))
                v.sem_inc(split, 1)


def gated_convolution(nc, g, a):
    G = 4
    NG = K // G
    with phase(nc) as s:
        w1, w2 = s.sb("w1", [2 * D, 2 * D]), s.sb("w2", [DE, 2 * D])
        b3, ones3 = s.sb("b3", [P, 2 * D], bf16), s.sb("ones3", [P, P], bf16)
        row = s.sb("bias_row", [1, 2 * D])
        b_in = s.sem("b_in")
        with nc.Block() as block:
            @block.sync
            def _(sp):
                sp.dma_start(row[0:1, 0:D], a["bf"].rearrange("(o n) -> o n", o=1)).then_inc(b_in, 16)
                sp.dma_start(row[0:1, D:2 * D], a["bs"].rearrange("(o n) -> o n", o=1)).then_inc(b_in, 16)
                sp.wait_ge(b_in, 32)
        split_bias(nc, row[0:1, :], b3, ones3)
        stage = s.sb("stage_i", [P, 2, K], i32)
        both = s.sb("both", [P, 2, K, 2 * D])
        starts = s.sb("starts", [P, 2, K, D])
        ea = s.sb("ea", [P, 2, K, DE])
        bothT, eaT = s.sb("bothT", [P, 2, G, P]), s.sb("eaT", [P, 2, G, P])
        la = s.sb("la", [P, 4, G, 2 * D])
        gate, core = s.sb("gate", [P, 4, G, D]), s.sb("core", [P, 4, G, D])
        msg, run = s.sb("msg", [P, 2, K, D]), s.sb("run", [P, 2, K, D])
        cs = s.sb("cs", [P, 2, K])
        psB, psE, psZ = s.ps("psB", [P, 2, G, P]), s.ps("psE", [P, 2, G, P]), s.ps("psZ", [P, 4, G, P])
        two = lambda name: [s.sem(f"{name}{k}") for k in range(2)]
        loaded_s, loaded_e, used, spread, free, stored = (
            two(n) for n in ("starts_in", "ea_in", "slot_used", "spread", "free", "stored"))
        got = [s.pool_sem(g, k) for k in range(2)]
        ready, dve_c, pool_c, staged, w_in = s.sem("ready"), s.sem("dve_c"), s.sem("pool_c"), s.sem("staged"), s.sem("w_in")
        turned, both_out, ea_out, made, logs, low, sig, chained, multiplied = (
            s.sem(n) for n in ("turned", "both_out", "ea_out", "made", "logs", "low", "sig", "chained", "multiplied"))
        grp = lambda i, k, n: i * (2 * NG) + (k * NG + n + 1)
        with nc.Block() as block:
            @block.sync
            def _(sp):
                sp.dma_start(w1[:, 0:D], a["Wf"][0:2 * D, :]).then_inc(w_in, 16)
                sp.dma_start(w1[:, D:2 * D], a["Ws"][0:2 * D, :]).then_inc(w_in, 16)
                sp.dma_start(w2[:, 0:D], a["Wf"][2 * D:2 * D + DE, :]).then_inc(w_in, 16)
                sp.dma_start(w2[:, D:2 * D], a["Ws"][2 * D:2 * D + DE, :]).then_inc(w_in, 16)
                with sp.Fori(0, NCH // 2) as i:
                    for k in range(2):
                        sp.wait_ge(spread[k], i + 1)
                        sp.dma_start(starts[:, k].rearrange("p j c -> p (j c)"),
                                     g.start_rows[0:EP, :].rearrange("(p j) c -> p (j c)", p=P)[:, bass.ds((i * 2 + k) * (K * D), K * D)]
                                     ).then_inc(loaded_s[k], 16)
                        sp.wait_ge(used[k], i + 1)
                        sp.dma_start(ea[:, k].rearrange("p j c -> p (j c)"),
                                     a["ea"].rearrange("(p j) c -> p (j c)", p=P)[:, bass.ds((i * 2 + k) * (K * DE), K * DE)]
                                     ).then_inc(loaded_e[k], 16)

            @block.gpsimd
            def _(pool):
                c = Chain(pool, pool_c)
                with pool.Fori(0, NCH // 2) as i:
                    c.begin(i, 2)
                    for k in range(2):
                        pool.wait_ge(used[k], i + 1)
                        gather_columns(pool, g.table, D, g.srcI, stage, both, c, i, k, got, staged)
                c.end(NCH // 2)

            @block.tensor
            def _(pe):
                for k in range(2):
                    pe.sem_inc(used[k], 1)
                pe.wait_ge(w_in, 64)
                with pe.Fori(0, NCH // 2) as i:
                    for n in range(2 * NG + 1):
                        if n < 2 * NG:
                            k, m = divmod(n, NG)
                            if m == 0:
                                pe.wait_ge(spread[k], i + 2)
                                pe.wait_ge(got[k], i * (16 * K) + 16 * K)
                                pe.wait_ge(loaded_e[k], i * 16 + 16)
                            for j in range(G):
                                pe.transpose(psB[:, n % 2, j, :], both[:, k, m * G + j, :], g.ident[:, :])
                            for j in range(G):
                                last = pe.transpose(psE[:, n % 2, j, :], ea[:, k, m * G + j, :], g.ident[:, :])
                            last.then_inc(turned, 1)
                            if m == NG - 1:
                                pe.wait_ge(turned, grp(i, 0, n))
                                pe.sem_inc(used[k], 1)
                        if n >= 1:
                            q = n - 1
                            pe.wait_ge(both_out, grp(i, 0, q))
                            pe.wait_ge(ea_out, grp(i, 0, q))
                            if q >= 4:
                                pe.wait_ge(logs, grp(i, 0, q - 4))
                                pe.wait_ge(low, grp(i, 0, q - 4))
                            for j in range(G):
                                pe.matmul(psZ[:, q % 4, j, :], ones3[:, :], b3[:, :], start=True, stop=False)
                                pe.matmul(psZ[:, q % 4, j, :], bothT[:, q % 2, j, :], w1[:, :], start=False, stop=False)
                                last = pe.matmul(psZ[:, q % 4, j, :], eaT[:, q % 2, j, :], w2[:, :], start=False, stop=True)
                            last.then_inc(made, 1)
                    pe.wait_ge(logs, grp(i, 0, 2 * NG - 1))
                    pe.wait_ge(low, grp(i, 0, 2 * NG - 1))

            @block.scalar
            def _(act):
                act.preload_act_table_set("natural_log_exp_and_others")
                for k in range(2):
                    act.sem_inc(free[k], 1)
                with act.Fori(0, NCH // 2) as i:
                    for n in range(2 * NG + 2):
                        if n < 2 * NG:
                            act.wait_ge(turned, grp(i, 0, n))
                            if n >= 2:
                                act.wait_ge(made, grp(i, 0, n - 2))
                            act.activation(bothT[:, n % 2], psB[:, n % 2], ACT.Copy).then_inc(both_out, 1)
                            act.activation(eaT[:, n % 2], psE[:, n % 2], ACT.Copy).then_inc(ea_out, 1)
                        if 1 <= n <= 2 * NG:
                            q = n - 1
                            act.wait_ge(made, grp(i, 0, q))
                            if q >= 4:
                                act.wait_ge(low, grp(i, 0, q - 4))
                            act.activation(la[:, q % 4], psZ[:, q % 4], ACT.Abs).then_inc(chained, 1)
                            act.wait_ge(chained, i * (4 * NG) + 2 * q + 1)
                            act.activation(la[:, q % 4], la[:, q % 4], ACT.Exp, scale=-1.0).then_inc(chained, 1)
                            act.wait_ge(chained, i * (4 * NG) + 2 * q + 2)
                            act.activation(la[:, q % 4], la[:, q % 4], ACT.Ln, bias=1.0).then_inc(logs, 1)
                        if n >= 2:
                            q = n - 2
                            act.wait_ge(low, grp(i, 0, q))
                            act.activation(gate[:, q % 4], gate[:, q % 4], ACT.Exp).then_inc(sig, 1)
                    for k in range(2):
                        act.wait_ge(ready, i * 2 + k + 1)
                        store_run(act, g, run, i, k, stored)
                    for k in range(2):
                        act.wait_ge(stored[k], i * 16 + 16)
                        act.sem_inc(free[k], 1)

            @block.vector
            def _(v):
                c = Chain(v, dve_c)
                for k in range(2):
                    v.sem_inc(spread[k], 1)
                c.mark(v.tensor_copy(both[:, 1, K - 1, 0:D], g.row_start[:, :]))
                c.link(v.memset(run[:, 1, K - 1, :], 0.0))
                def spread_starts(i, k):
                    c.link(v.tensor_copy(cs[:, k, :], g.cont[:, bass.ds((i * 2 + k) * K, K)]))
                    v.wait_ge(loaded_s[k], i * 16 + 16)
                    v.wait_ge(used[k], i + 1)
                    scan_columns(v, c, both[:, k], starts[:, k], both[:, 1 - k, K - 1, 0:D], cs[:, k, :])
                    v.sem_inc(spread[k], 1)

                with v.Fori(0, NCH // 2) as i:
                    c.begin(i, 4)
                    spread_starts(i, 0)
                    for n in range(2 * NG + 3):
                        if n == NG - 2:
                            spread_starts(i, 1)
                        if 1 <= n <= 2 * NG:
                            q = n - 1
                            v.wait_ge(logs, grp(i, 0, q))
                            if q >= 4:
                                v.wait_ge(multiplied, grp(i, 0, q - 4))
                            v.scalar_tensor_tensor(gate[:, q % 4], psZ[:, q % 4, :, 0:D], 0.0, la[:, q % 4, :, 0:D],
                                                   ALU.min, ALU.subtract)
                            v.scalar_tensor_tensor(core[:, q % 4], psZ[:, q % 4, :, D:2 * D], 0.0, la[:, q % 4, :, D:2 * D],
                                                   ALU.max, ALU.add).then_inc(low, 1)
                        if n >= 3:
                            q = n - 3
                            k, m = divmod(q, NG)
                            v.wait_ge(sig, grp(i, 0, q))
                            v.wait_ge(low, grp(i, 0, q))
                            v.tensor_tensor(msg[:, k, m * G:(m + 1) * G, :], gate[:, q % 4], core[:, q % 4],
                                            ALU.mult).then_inc(multiplied, 1)
                            if m == NG - 1:
                                v.wait_ge(multiplied, grp(i, 0, q))
                                v.wait_ge(free[k], i + 1)
                                for f in range(D):
                                    last = v.tensor_tensor_scan(run[:, k, :, f], cs[:, k, :], msg[:, k, :, f],
                                                                run[:, 1 - k, K - 1, f:f + 1], ALU.mult, ALU.add)
                                last.then_inc(ready, 1)
                                v.wait_ge(ready, i * 2 + k + 1)
                c.end(NCH // 2)
                c.link(v.tensor_copy(g.tail[:, :], run[:, 1, K - 1, :]))


def gat_weights(nc, g, a, layer):
    s = g.layer
    w = lambda name: a[name.format(layer)]
    g.wrl, g.wl = s.sb("wrl", [2 * D, HD + H]), s.sb("wl", [D, HD])
    g.bl, g.brl, g.att, g.bias = s.sb("bl", [P, HD]), s.sb("brl", [P, HD + H]), s.sb("att", [P, HD]), s.sb("bias", [P, D])
    g.brl3, g.ones3 = s.sb("brl3", [P, HD + H], bf16), s.sb("ones3", [P, P], bf16)
    g.wlb = s.sb("wlb", [P, HD])
    g.att1 = s.sb("att1", [P, H, D + 1])
    with phase(nc) as t:
        loaded, zeroed, chain = t.sem("loaded"), t.sem("zeroed"), t.sem("chain")
        prod, row = t.sb("prod_w", [P, HD]), t.sb("row", [1, HD + H])
        with nc.Block() as block:
            @block.sync
            def _(sp):
                sp.dma_start(g.wrl[0:D, 0:HD], w("W{}r")).then_inc(loaded, 16)
                sp.dma_start(g.wrl[D:2 * D, 0:HD], w("W{}l")).then_inc(loaded, 16)
                sp.dma_start(g.wl[:, :], w("W{}l")).then_inc(loaded, 16)
                sp.dma_start(g.bl[:, :], w("b{}l").partition_broadcast(P)).then_inc(loaded, 16)
                sp.dma_start(g.brl[:, 0:HD], w("b{}r").partition_broadcast(P)).then_inc(loaded, 16)
                sp.dma_start(g.att[:, :], w("att{}").rearrange("h c -> (h c)").partition_broadcast(P)).then_inc(loaded, 16)
                sp.dma_start(g.bias[:, :], w("bias{}").partition_broadcast(P)).then_inc(loaded, 16)
                sp.wait_ge(zeroed, 1)
                sp.dma_start(g.wlb[0:D, :], w("W{}l")).then_inc(loaded, 16)
                sp.dma_start(g.wlb[D:D + 1, :], w("b{}l").rearrange("(o n) -> o n", o=1)).then_inc(loaded, 16)
                sp.wait_ge(loaded, 9 * 16)

            @block.gpsimd
            def _(pool):
                pool.memset(g.wlb[:, :], 0.0).then_inc(zeroed, 1)

            @block.vector
            def _(v):
                v.wait_ge(loaded, 9 * 16)
                c = Chain(v, chain)
                c.link(v.tensor_tensor(g.brl[:, 0:HD], g.brl[:, 0:HD], g.bl[:, :], ALU.add))
                for w_ in (g.wrl, g.brl):
                    c.link(v.tensor_tensor(prod[:, :], w_[:, 0:HD], g.att[:, :], ALU.mult))
                    c.link(v.tensor_reduce(w_[:, HD:HD + H], prod[:, :].rearrange("p (h c) -> p h c", h=H), X, ALU.add))
                    c.link(v.tensor_scalar(w_[:, HD:HD + H], w_[:, HD:HD + H], 0.6, None, ALU.mult))
                c.mark(v.memset(g.att1[:, :, D:D + 1], 1.0))
                c.mark(v.tensor_scalar(g.att1[:, :, 0:D], g.att[:, :].rearrange("p (h c) -> p h c", h=H), 0.4, None, ALU.mult))
                c.link(v.tensor_copy(row[0:1, :], g.brl[0:1, :]))
        split_bias(nc, row[0:1, :], g.brl3, g.ones3)


def gat_loops(nc, g, h, loops):
    with phase(nc) as s:
        hh, z = s.sb("hh", [P, NB, 2 * D]), s.sb("zz", [P, NB, 1, HD])
        chain = s.sem("chain")
        with nc.Block() as block:
            @block.vector
            def _(v):
                c = Chain(v, chain)
                c.mark(v.tensor_copy(hh[:, :, 0:D], h[:, :, :]))
                c.link(v.tensor_copy(hh[:, :, D:2 * D], h[:, :, :]))
        node_linear(nc, g, [hh[:, :, :]], [g.wrl[:, 0:HD]], z)
        with nc.Block() as block:
            @block.vector
            def _(v):
                c = Chain(v, chain)
                c.n = 2
                flat = z[:, :, 0, :]
                over = lambda t: t[:, 0:HD].unsqueeze(1).to_broadcast([P, NB, HD])
                c.link(v.tensor_tensor(flat, flat, over(g.brl), ALU.add))
                c.link(v.scalar_tensor_tensor(flat, flat, 0.2, flat, ALU.mult, ALU.max))
                c.link(v.tensor_tensor(flat, flat, over(g.att), ALU.mult))
                c.link(v.tensor_reduce(loops[:, :, :], flat.rearrange("p b (h c) -> p b h c", h=H), X, ALU.add))


def gat_scores(nc, g):
    G = 2
    NG = K // G
    with phase(nc) as s:
        stage = s.sb("stage_i", [P, 2, K], i32)
        both, starts = s.sb("both", [P, 2, K, 2 * D]), s.sb("starts", [P, 2, K, D])
        bothT, lz = s.sb("bothT", [P, 2, G, P]), s.sb("lz", [P, 4, G, H, D + 1])
        sc, cs = s.sb("sc", [P, 2, K, H]), s.sb("cs", [P, 2, K])
        psB, psZ = s.ps("psB", [P, 2, 512]), s.ps("psZ", [P, 2, G, 512])
        two = lambda name: [s.sem(f"{name}{k}") for k in range(2)]
        loaded_s, used, spread, stored, kept = (two(n) for n in ("starts_in", "slot_used", "spread", "stored", "kept"))
        got = [s.pool_sem(g, k) for k in range(2)]
        dve_c, pool_c, staged, turned, out, made, leaky, prod, scored = (
            s.sem(n) for n in ("dve_c", "pool_c", "staged", "turned", "both_out", "made", "leaky", "prod", "scored"))
        grp = lambda i, n: i * (2 * NG) + (n + 1)
        with nc.Block() as block:
            @block.sync
            def _(sp):
                with sp.Fori(0, NCH // 2) as i:
                    for k in range(2):
                        sp.wait_ge(spread[k], i + 1)
                        sp.dma_start(starts[:, k].rearrange("p j c -> p (j c)"),
                                     g.start_rows[0:EP, :].rearrange("(p j) c -> p (j c)", p=P)[:, bass.ds((i * 2 + k) * (K * D), K * D)]
                                     ).then_inc(loaded_s[k], 16)

            @block.gpsimd
            def _(pool):
                c = Chain(pool, pool_c)
                with pool.Fori(0, NCH // 2) as i:
                    c.begin(i, 2)
                    for k in range(2):
                        pool.wait_ge(used[k], i + 1)
                        pool.wait_ge(kept[k], i + 1)
                        gather_columns(pool, g.table, D, g.srcI, stage, both, c, i, k, got, staged)
                c.end(NCH // 2)

            @block.tensor
            def _(pe):
                for k in range(2):
                    pe.sem_inc(used[k], 1)
                with pe.Fori(0, NCH // 2) as i:
                    for n in range(2 * NG + 1):
                        if n < 2 * NG:
                            k, m = divmod(n, NG)
                            if m == 0:
                                pe.wait_ge(spread[k], i + 2)
                                pe.wait_ge(got[k], i * (16 * K) + 16 * K)
                            for j in range(G):
                                last = pe.transpose(psB[:, n % 2, j * P:(j + 1) * P], both[:, k, m * G + j, :], g.ident[:, :])
                            last.then_inc(turned, 1)
                            if m == NG - 1:
                                pe.wait_ge(turned, grp(i, n))
                                pe.sem_inc(used[k], 1)
                        if n >= 1:
                            q = n - 1
                            pe.wait_ge(out, grp(i, q))
                            if q >= 2:
                                pe.wait_ge(leaky, grp(i, q - 2))
                            for j in range(G):
                                pe.matmul(psZ[:, q % 2, j, 0:HD + H], g.ones3[:, :], g.brl3[:, :], start=True, stop=False)
                                last = pe.matmul(psZ[:, q % 2, j, 0:HD + H], bothT[:, q % 2, j, :], g.wrl[:, :],
                                                 start=False, stop=True)
                            last.then_inc(made, 1)
                    pe.wait_ge(leaky, grp(i, 2 * NG - 1))

            @block.scalar
            def _(act):
                for k in range(2):
                    act.sem_inc(kept[k], 1)
                with act.Fori(0, NCH // 2) as i:
                    for n in range(2 * NG + 1):
                        if n < 2 * NG:
                            k, m = divmod(n, NG)
                            if m == 0:
                                act.wait_ge(got[k], i * (16 * K) + 16 * K)
                                act.dma_start(g.x_src.rearrange("(p j) c -> p j c", p=P)[:, bass.ds((i * 2 + k) * K, K), :],
                                              both[:, k, :, D:2 * D]).then_inc(stored[k], 16)
                            act.wait_ge(turned, grp(i, n))
                            if n >= 2:
                                act.wait_ge(made, grp(i, n - 2))
                            act.activation(bothT[:, n % 2], psB[:, n % 2, 0:G * P].rearrange("p (g e) -> p g e", g=G),
                                           ACT.Copy).then_inc(out, 1)
                            if m == NG - 1:
                                act.wait_ge(stored[k], i * 16 + 16)
                                act.sem_inc(kept[k], 1)
                        if n >= 1:
                            q = n - 1
                            act.wait_ge(made, grp(i, q))
                            if q >= 4:
                                act.wait_ge(scored, grp(i, q - 4))
                            act.activation(lz[:, q % 4, :, :, 0:D], psZ[:, q % 2, :, 0:HD].rearrange("p g (h c) -> p g h c", h=H),
                                           ACT.Abs)
                            act.activation(lz[:, q % 4, :, :, D], psZ[:, q % 2, :, HD:HD + H], ACT.Copy).then_inc(leaky, 1)
                    act.wait_ge(scored, grp(i, 2 * NG - 1))

            @block.vector
            def _(v):
                c = Chain(v, dve_c)
                for k in range(2):
                    v.sem_inc(spread[k], 1)
                c.link(v.tensor_copy(both[:, 1, K - 1, 0:D], g.row_start[:, :]))
                def spread_starts(i, k):
                    c.link(v.tensor_copy(cs[:, k, :], g.cont[:, bass.ds((i * 2 + k) * K, K)]))
                    v.wait_ge(loaded_s[k], i * 16 + 16)
                    v.wait_ge(used[k], i + 1)
                    scan_columns(v, c, both[:, k], starts[:, k], both[:, 1 - k, K - 1, 0:D], cs[:, k, :])
                    v.sem_inc(spread[k], 1)

                with v.Fori(0, NCH // 2) as i:
                    c.begin(i, 6)
                    spread_starts(i, 0)
                    for n in range(2 * NG + 1):
                        if n == NG - 4:
                            spread_starts(i, 1)
                        if n < 2 * NG:
                            v.wait_ge(leaky, grp(i, n))
                            v.tensor_tensor(lz[:, n % 4].rearrange("p g h c -> p g (h c)"),
                                            lz[:, n % 4].rearrange("p g h c -> p g (h c)"),
                                            g.att1[:, :, :].rearrange("p h c -> p (h c)").unsqueeze(1).to_broadcast([P, G, HD + H]),
                                            ALU.mult).then_inc(prod, 1)
                        if n >= 1:
                            q = n - 1
                            k, m = divmod(q, NG)
                            v.wait_ge(prod, grp(i, q))
                            v.tensor_reduce(sc[:, k, m * G:(m + 1) * G, :],
                                            lz[:, q % 4], X, ALU.add).then_inc(scored, 1)
                            if m == NG - 1:
                                v.wait_ge(scored, grp(i, q))
                                c.link(v.tensor_copy(g.score[:, :, bass.ds((i * 2 + k) * K, K)],
                                                     sc[:, k].rearrange("p j h -> p h j")))
                c.end(NCH // 2)


def spread_loops(nc, g, selfs):
    with phase(nc) as s:
        at = s.sb("at_starts", [P, J, H])
        loaded, chain = s.sem("loaded"), s.sem("chain")
        with nc.Block() as block:
            @block.sync
            def _(sp):
                sp.dma_start(at[:, :, :].rearrange("p j h -> p (j h)"),
                             g.start_self[0:EP, :].rearrange("(p j) h -> p (j h)", p=P)).then_inc(loaded, 16)

            @block.vector
            def _(v):
                c = Chain(v, chain)
                v.wait_ge(loaded, 16)
                for h in range(H):
                    c.mark(v.tensor_tensor_scan(selfs[:, h, :], g.cont[:, :], at[:, :, h], g.row_self[:, h:h + 1], ALU.mult, ALU.add))
                c.wait()


def gather_loop_weights(nc, g, selfs, loops):
    with phase(nc) as s:
        at = s.sb("at_edges", [P, J, H])
        turned, kept, got, chain = s.sem("turned"), s.sem("kept"), s.pool_sem(g, 0), s.sem("chain")
        with nc.Block() as block:
            @block.vector
            def _(v):
                v.tensor_copy(at[:, :, :], selfs.rearrange("p h j -> p j h")).then_inc(turned, 1)
                c = Chain(v, chain)
                v.wait_ge(got, 16 * NB)
                for h in range(H):
                    c.mark(v.scalar_tensor_tensor(loops[:, :, h], g.nothas[:, :], 1.0 / H, loops[:, :, h], ALU.mult, ALU.add))
                c.wait()

            @block.sync
            def _(sp):
                sp.wait_ge(turned, 1)
                sp.dma_start(g.self_weight[0:EP, :].rearrange("(p j) h -> p (j h)", p=P),
                             at[:, :, :].rearrange("p j h -> p (j h)")).then_inc(kept, 16)

            @block.gpsimd
            def _(pool):
                pool.wait_ge(kept, 16)
                for b in range(NB):
                    pool.indirect_dma_start(loops[:, b, :], None, g.self_weight,
                                            bass.IndirectOffsetOnAxis(g.idxEnd[:, b:b + 1], 0)).then_inc(got, 16)


def gat_sums(nc, g):
    G = 2
    NG = K // G
    with phase(nc) as s:
        rows, msg, run = s.sb("rows", [P, 2, K, P]), s.sb("msg", [P, 2, K, D]), s.sb("run", [P, 2, K, D])
        rowsT, prod = s.sb("rowsT", [P, 2, G, P]), s.sb("prod", [P, 2, G, HD])
        ws, cs = s.sb("ws", [P, 2, K, H]), s.sb("cs", [P, 2, K])
        psT, psZ = s.ps("psT", [P, 2, 512]), s.ps("psZ", [P, 2, G, 512])
        two = lambda name: [s.sem(f"{name}{k}") for k in range(2)]
        got, used, free = (two(n) for n in ("got", "slot_used", "free"))
        stored = [s.pool_sem(g, k) for k in range(2)]
        padded, dve_c, begun, turned, out, made, weighed, summed, ready = (
            s.sem(n) for n in ("padded", "dve_c", "begun", "turned", "rows_out", "made", "weighed", "summed", "ready"))
        grp = lambda i, n: i * (2 * NG) + (n + 1)
        with nc.Block() as block:
            @block.sync
            def _(sp):
                with sp.Fori(0, NCH // 2) as i:
                    for k in range(2):
                        sp.wait_ge(used[k], i + 1)
                        sp.dma_start(rows[:, k, :, 0:D],
                                     g.x_src.rearrange("(p j) c -> p j c", p=P)[:, bass.ds((i * 2 + k) * K, K), :]
                                     ).then_inc(got[k], 16)

            @block.gpsimd
            def _(pool):
                store_runs(pool, g, run, ready, stored, free)

            @block.tensor
            def _(pe):
                for k in range(2):
                    pe.sem_inc(used[k], 1)
                pe.wait_ge(padded, 2)
                with pe.Fori(0, NCH // 2) as i:
                    for n in range(2 * NG + 1):
                        if n < 2 * NG:
                            k, m = divmod(n, NG)
                            if m == 0:
                                pe.wait_ge(got[k], i * 16 + 16)
                                pe.sem_inc(begun, 1)
                            for j in range(G):
                                last = pe.transpose(psT[:, n % 2, j * P:(j + 1) * P], rows[:, k, m * G + j, :], g.ident[:, :])
                            last.then_inc(turned, 1)
                            if m == NG - 1:
                                pe.wait_ge(turned, grp(i, n))
                                pe.sem_inc(used[k], 1)
                        if n >= 1:
                            q = n - 1
                            pe.wait_ge(out, grp(i, q))
                            if q >= 2:
                                pe.wait_ge(weighed, grp(i, q - 2))
                            for j in range(G):
                                last = pe.matmul(psZ[:, q % 2, j, 0:HD], rowsT[:, q % 2, j, :], g.wlb[:, :],
                                                 start=True, stop=True)
                            last.then_inc(made, 1)
                    pe.wait_ge(weighed, grp(i, 2 * NG - 1))

            @block.scalar
            def _(act):
                with act.Fori(0, NCH // 2) as i:
                    for n in range(2 * NG):
                        act.wait_ge(turned, grp(i, n))
                        if n >= 2:
                            act.wait_ge(made, grp(i, n - 2))
                        act.activation(rowsT[:, n % 2], psT[:, n % 2, 0:G * P].rearrange("p (g e) -> p g e", g=G),
                                       ACT.Copy).then_inc(out, 1)
                    act.wait_ge(made, grp(i, 2 * NG - 1))

            @block.vector
            def _(v):
                c = Chain(v, dve_c)
                v.memset(rows[:, :, :, D:D + 1], 1.0).then_inc(padded, 1)
                v.memset(rows[:, :, :, D + 1:P], 0.0).then_inc(padded, 1)
                c.link(v.memset(run[:, 1, K - 1, :], 0.0))
                with v.Fori(0, NCH // 2) as i:
                    c.begin(i, 6)
                    for k in range(2):
                        c.mark(v.tensor_copy(cs[:, k, :], g.cont[:, bass.ds((i * 2 + k) * K, K)]))
                        c.link(v.tensor_copy(ws[:, k].rearrange("p j h -> p h j"), g.score[:, :, bass.ds((i * 2 + k) * K, K)]))
                    for n in range(2 * NG + 1):
                        if n < 2 * NG:
                            k, m = divmod(n, NG)
                            v.wait_ge(made, grp(i, n))
                            if n >= 2:
                                v.wait_ge(summed, grp(i, n - 2))
                            v.tensor_tensor(prod[:, n % 2].rearrange("p g (h c) -> p g h c", h=H),
                                            psZ[:, n % 2, :, 0:HD].rearrange("p g (h c) -> p g h c", h=H),
                                            ws[:, k, m * G:(m + 1) * G, :].unsqueeze(3).to_broadcast([P, G, H, D]),
                                            ALU.mult).then_inc(weighed, 1)
                        if n >= 1:
                            q = n - 1
                            k, m = divmod(q, NG)
                            v.wait_ge(weighed, grp(i, q))
                            v.tensor_reduce(msg[:, k, m * G:(m + 1) * G, :],
                                            prod[:, q % 2].rearrange("p g (h c) -> p g c h", h=H), X, ALU.add).then_inc(summed, 1)
                            if m == NG - 1:
                                v.wait_ge(summed, grp(i, q))
                                v.wait_ge(free[k], i + 1)
                                scan_columns(v, c, run[:, k], msg[:, k], run[:, 1 - k, K - 1, :], cs[:, k, :])
                                v.sem_inc(ready, 1)
                c.end(NCH // 2)
                c.link(v.tensor_copy(g.tail[:, :], run[:, 1, K - 1, :]))


def gat_layer(nc, g, a, layer, h, out):
    with phase(nc) as s:
        g.layer = s
        gat_weights(nc, g, a, layer)
        loops = s.sb("loops", [P, NB, H])
        gat_loops(nc, g, h, loops)
        with phase(nc) as t:
            g.score = t.sb("score", [P, H, J])
            selfs = t.sb("selfs", [P, H, J])
            put_nodes(nc, g, h, loops)
            gat_scores(nc, g)
            spread_loops(nc, g, selfs)
            softmax(nc, g, H, selfs[:, :, :])
            gather_loop_weights(nc, g, selfs[:, :, :], loops)
            gat_sums(nc, g)
        with phase(nc) as t:
            xl, acc = t.sb("xl", [P, NB, 1, HD]), t.sb("acc", [P, NB, D])
            chain = t.sem("chain")
            node_sums(nc, g, acc)
            node_linear(nc, g, [h[:, :, :]], [g.wl[:, :]], xl)
            with nc.Block() as block:
                @block.vector
                def _(v):
                    c = Chain(v, chain)
                    flat = xl[:, :, 0, :]
                    c.link(v.tensor_tensor(flat, flat, g.bl[:, :].unsqueeze(1).to_broadcast([P, NB, HD]), ALU.add))
                    c.link(v.tensor_tensor(flat.rearrange("p b (h c) -> p b h c", h=H),
                                           flat.rearrange("p b (h c) -> p b h c", h=H),
                                           loops[:, :, :].unsqueeze(3).to_broadcast([P, NB, H, D]), ALU.mult))
                    for n in range(H):
                        c.link(v.tensor_tensor(acc[:, :, :], acc[:, :, :], xl[:, :, 0, n * D:(n + 1) * D], ALU.add))
                    c.link(v.tensor_tensor(acc[:, :, :], acc[:, :, :], g.bias[:, :].unsqueeze(1).to_broadcast([P, NB, D]), ALU.add))
                    c.link(v.tensor_scalar(out[:, :, :], acc[:, :, :], 0.0, None, ALU.max))


def build(nc, a, out):
    Space.used = {}
    g = Space(nc, ExitStack())

    def scratch(name, shape):
        return nc.dram_tensor(name, shape, f32, kind="Internal").ap()

    g.hpx = scratch("hpx", (NR * R, 2 * D))
    g.x_src = scratch("x_src", (EP, D))
    g.scanned = scratch("scanned", (EP + P, D))
    g.carry = scratch("carry", (P, D))
    g.table = scratch("table", (NR, D))
    g.adj = nc.dram_tensor("adj", (NT * P, NB * TC), bf16, kind="Internal").ap()
    g.step_rows, g.step_sums = scratch("step_rows", (S * WD, D)), scratch("step_sums", (S * WD, D))
    g.start_rows = scratch("start_rows", (EP + NR, D))
    g.table_self = scratch("table_self", (NR, H))
    g.start_self = scratch("start_self", (EP + NR, H))
    g.self_weight = scratch("self_weight", (EP + P, H))
    with g.ctx:
        g.pool_sems = [g.sem(f"pool_dma{n}") for n in range(4)]
        setup(nc, g, a)
        g.tail = g.sb("tail", [P, D])
        relation_table(nc, g, a)
        with phase(nc) as s:
            g.score = s.sb("score", [P, 1, J])
            relation_scores(nc, g, a)
            softmax(nc, g, 1)
            weighted_sums(nc, g, "L0")
        with phase(nc) as s:
            nbh = s.sb("nbh", [P, NB, D])
            node_sums(nc, g, nbh)
            relation_output(nc, g, a, nbh)
        with phase(nc) as s:
            y = s.sb("y", [P, NB, D])
            with phase(nc) as t:
                copied = t.sem("copied")
                with nc.Block() as block:
                    @block.vector
                    def _(v):
                        v.tensor_copy(y[:, :, :], g.x[:, :, :]).then_inc(copied, 1)
                        v.wait_ge(copied, 1)
            g.step = s
            adjacency(nc, g, a)
            for _ in range(4):
                propagate(nc, g, y)
            add_norm(nc, g, [y[:, :, :]])
        g.row_start = g.sb("row_start", [P, D])
        g.row_self = g.sb("row_self", [P, H])
        put_nodes(nc, g, g.x)
        gated_convolution(nc, g, a)
        with phase(nc) as s:
            agg = s.sb("agg", [P, NB, D])
            node_sums(nc, g, agg)

            def gated(v, c):
                c.link(v.tensor_tensor(agg[:, :, :], agg[:, :, :], g.x[:, :, :], ALU.add))
                c.link(v.tensor_scalar(agg[:, :, :], agg[:, :, :], 0.0, None, ALU.max))

            add_norm(nc, g, [agg[:, :, :]], gated)
        with phase(nc) as s:
            h1 = s.sb("h1", [P, NB, D])
            gat_layer(nc, g, a, 1, g.x, h1)
            gat_layer(nc, g, a, 2, h1, h1)
            z, fc, bfc = s.sb("z_fc", [P, NB, 1, D]), s.sb("fc", [D, D]), s.sb("bfc", [P, D])
            loaded = s.sem("fc_loaded")
            with nc.Block() as block:
                @block.sync
                def _(sp):
                    sp.dma_start(fc[:, :], a["Wfc"]).then_inc(loaded, 16)
                    sp.dma_start(bfc[:, :], a["bfc"].partition_broadcast(P)).then_inc(loaded, 16)
                    sp.wait_ge(loaded, 32)
            node_linear(nc, g, [h1[:, :, :]], [fc[:, :]], z)
            add_norm(nc, g, [z[:, :, 0, :], bfc[:, :].unsqueeze(1).to_broadcast([P, NB, D])])
            stored = s.sem("out_stored")
            with nc.Block() as block:
                @block.sync
                def _(sp):
                    sp.dma_start(out.rearrange("(p b) d -> p b d", b=NB), g.x[0:N // NB, :, :]).then_inc(stored, 16)
                    sp.wait_ge(stored, 16)


_INS = {"x": "x", "src": "src", "dst": "dst", "et": "edge_type_32", "ea": "edge_attr_128", "ef": "edge_attr_64",
        "relw": "L0_gnn_relation_weight", "rw1": "L0_gnn_res_w1", "rw2": "L0_gnn_res_w2",
        "Wf": "L2_gnn_W_f", "bf": "L2_gnn_b_f", "Ws": "L2_gnn_W_s", "bs": "L2_gnn_b_s",
        "W1l": "L3_gnn_W1l", "b1l": "L3_gnn_b1l", "W1r": "L3_gnn_W1r", "b1r": "L3_gnn_b1r", "att1": "L3_gnn_att1",
        "bias1": "L3_gnn_bias1", "W2l": "L3_gnn_W2l", "b2l": "L3_gnn_b2l", "W2r": "L3_gnn_W2r", "b2r": "L3_gnn_b2r",
        "att2": "L3_gnn_att2", "bias2": "L3_gnn_bias2", "Wfc": "L3_gnn_Wfc", "bfc": "L3_gnn_bfc"}
_EDGES = {"src": 0, "dst": N, "et": 0, "ea": 0, "ef": 0}


def kernel(**inputs):
    import numpy as np
    import concourse.bacc as bacc
    from concourse.bass_utils import run_bass_kernel_spmd as run

    nc = bacc.Bacc("TRN2", target_bir_lowering=False, num_devices=1)
    arrays, args = {}, {}
    for short, name in _INS.items():
        v = np.ascontiguousarray(inputs[name])
        if short in _EDGES:
            pad = np.full((EP - E,) + v.shape[1:], _EDGES[short], v.dtype)
            v = np.concatenate([v, pad])
        arrays[f"in_{short}"] = v
        args[short] = nc.dram_tensor(f"in_{short}", v.shape, mybir.dt.from_np(v.dtype), kind="ExternalInput").ap()
    out = nc.dram_tensor("out_0", (N, D), f32, kind="ExternalOutput").ap()
    build(nc, args, out)
    r = run(nc, [arrays], core_ids=[0])
    return r.results[0]["out_0"]
```

```python
from contextlib import ExitStack, contextmanager

import concourse.bass as bass
from concourse import mybir

P = 128
N, D = 3125, 64
E = 100000
R = 32
H = 5
HD = H * D
DE = 128
NB = N // 125
NR = P * NB
J = 784
EP = P * J
BIG = 1.0e38
WHOLE = 1.5 * 2.0 ** 23
LN_EPS = 1.0e-5
K = 28
NCH = J // K

CE = 128
CH = EP // CE
WD = 5
NW = N // WD
TS = 25
TC = TS * WD
NT = 57
S = NT * TS
SP = 95
SQ = S // SP
assert S >= CH + N // WD + 1 and SP * SQ == S and NB % WD == 0

f32 = mybir.dt.float32
bf16 = mybir.dt.bfloat16
i32 = mybir.dt.int32
ALU = mybir.AluOpType
ACT = mybir.ActivationFunctionType
X = mybir.AxisListType.X


class Chain:

    def __init__(self, eng, sem):
        self.eng, self.sem, self.n, self.turn = eng, sem, 0, None

    def count(self):
        return self.n if self.turn is None else self.turn + self.n

    def mark(self, ins):
        self.n += 1
        ins.then_inc(self.sem, 1)
        return self.count()

    def wait(self, at=None):
        self.eng.wait_ge(self.sem, self.count() if at is None else at)

    def link(self, ins):
        self.mark(ins)
        self.wait()

    def begin(self, i, each):
        self.before, self.each, self.turn = self.n, each, i * each

    def end(self, turns):
        assert self.n - self.before == self.each, (self.n - self.before, self.each)
        self.n = self.before + self.each * turns
        self.turn = None


class Space:

    used = {}

    def __init__(self, nc, ctx):
        self.nc, self.ctx, self.sems = nc, ctx, []

    def sb(self, name, shape, dt=f32):
        return self.ctx.enter_context(self.nc.sbuf_tensor(self.own(name), shape, dt))

    def ps(self, name, shape, dt=f32):
        return self.ctx.enter_context(self.nc.psum_tensor(self.own(name), shape, dt))

    def sem(self, name):
        self.sems.append(self.ctx.enter_context(self.nc.semaphore(self.own(name))))
        return self.sems[-1]

    def pool_sem(self, g, n):
        self.sems.append(g.pool_sems[n])
        return g.pool_sems[n]

    def own(self, name):
        used = Space.used
        used[name] = used.get(name, 0) + 1
        return name if used[name] == 1 else f"{name}_{used[name]}"


@contextmanager
def phase(nc):
    with ExitStack() as ctx:
        s = Space(nc, ctx)
        yield s
        with nc.Block() as block:
            @block.gpsimd
            def _(pool):
                pool.dma_reset()
                for sem in s.sems:
                    pool.sem_clear(sem)


def setup(nc, g, a):
    g.srcI, g.dstI = g.sb("srcI", [P, J], i32), g.sb("dstI", [P, J], i32)
    g.hpS, g.hpD = g.sb("hpS", [P, J], i32), g.sb("hpD", [P, J], i32)
    g.cont, g.isend, g.notend = g.sb("cont", [P, J]), g.sb("isend", [P, J]), g.sb("notend", [P, J])
    g.contz = g.sb("contz", [P, J])
    g.Lm, g.Rm = g.sb("Lm", [P, J]), g.sb("Rm", [P, J])
    g.x = g.sb("x", [P, NB, D])
    g.ident = g.sb("ident", [P, P])
    g.contLrow, g.contRrow = g.sb("contLrow", [P, P]), g.sb("contRrow", [P, P])
    g.dinv, g.has, g.nothas = g.sb("dinv", [P, NB]), g.sb("has", [P, NB]), g.sb("nothas", [P, NB])
    g.idxEnd, g.idxCar = g.sb("idxEnd", [P, NB], i32), g.sb("idxCar", [P, NB], i32)
    g.idxStart, g.row0 = g.sb("idxStart", [P, NB], i32), g.sb("row0", [P, 1], i32)
    with phase(nc) as s:
        etI = s.sb("etI", [P, J], i32)
        edge_rows = s.sb("edge_rows", [P, 2], i32)
        dstF = s.sb("dstF", [P, J])
        dstP = s.sb("dstP", [P, J])
        dstB = s.sb("dstB", [P, J])
        nbr = s.sb("nbr", [P, 2])
        iotaI = s.sb("iotaI", [P, P], i32)
        iotaF = s.sb("iotaF", [P, P])
        nodeI = s.sb("nodeI", [P, NB], i32)
        nodeF = s.sb("nodeF", [P, NB])
        ones = s.sb("ones", [P, P])
        lower = s.sb("lower", [P, P])
        diag = s.sb("diag", [P, 2, P])
        zero = s.sb("zero", [P, P], bf16)
        hotP = s.sb("hotP", [P, 2, K, P], bf16)
        hotB = s.sb("hotB", [P, 2, K, NB], bf16)
        cols = s.sb("cols", [P, 2, 2, K])
        w = s.sb("w", [P, 12, NB])
        psC = s.ps("psC", [P, 512])
        psR = s.ps("psR", [P, 2, 256])
        psE = s.ps("psE", [P, 512])
        loaded = s.sem("loaded")
        cleared = s.sem("cleared")
        made = s.sem("made")
        dve = s.sem("dve")
        hot = [s.sem(f"hot{k}") for k in range(2)]
        counted = [s.sem(f"counted{k}") for k in range(2)]
        split = s.sem("split")
        rows = s.sem("rows")
        total = s.sem("total")
        sq = s.sem("sq")
        sqd = s.sem("sqd")
        zeroed, zeros = s.sem("zeroed"), s.sem("zeros_stored")
        zerof = s.sb("zerof", [P, 3236])
        with nc.Block() as block:
            @block.sync
            def _(sp):
                sp.dma_start(g.srcI[:, :], a["src"].rearrange("(p j) -> p j", p=P)).then_inc(loaded, 16)
                sp.dma_start(g.dstI[:, :], a["dst"].rearrange("(p j) -> p j", p=P)).then_inc(loaded, 16)
                sp.dma_start(etI[:, :], a["et"].rearrange("(p j) -> p j", p=P)).then_inc(loaded, 16)
                d2 = a["dst"].rearrange("(p j) -> p j", p=P)
                sp.wait_ge(cleared, 2)
                sp.dma_start(edge_rows[1:P, 0:1], d2[0:P - 1, J - 1:J],
                             allow_slow_non_contiguous=True).then_inc(loaded, 16)
                sp.dma_start(edge_rows[0:P - 1, 1:2], d2[1:P, 0:1],
                             allow_slow_non_contiguous=True).then_inc(loaded, 16)
                sp.dma_start(g.x[0:N // NB], a["x"].rearrange("(p b) d -> p b d", b=NB)).then_inc(loaded, 16)
                sp.wait_ge(loaded, 6 * 16)

            @block.gpsimd
            def _(pool):
                pool.memset(edge_rows[:, :], -1).then_inc(cleared, 1)
                pool.memset(zerof[:, :], 0.0).then_inc(zeroed, 1)
                pool.memset(g.x[:, :, :], 0.0).then_inc(cleared, 1)
                pool.memset(ones[:, :], 1.0).then_inc(made, 1)
                pool.memset(g.ident[:, :], 0.0).then_inc(made, 1)
                pool.wait_ge(made, 2)
                pool.affine_select(out=g.ident[:, :], in_=g.ident[:, :], compare_op=ALU.not_equal, fill=1.0,
                                   base=0, pattern=[[-1, P]], channel_multiplier=1).then_inc(made, 1)
                pool.affine_select(out=lower[:, :], in_=ones[:, :], compare_op=ALU.is_gt, fill=0.0,
                                   base=0, pattern=[[1, P]], channel_multiplier=-1).then_inc(made, 1)
                pool.iota(iotaI[:, :], pattern=[[1, P]], base=0, channel_multiplier=0).then_inc(made, 1)
                pool.iota(nodeI[:, :], pattern=[[1, NB]], base=0, channel_multiplier=NB).then_inc(made, 1)
                pool.memset(zero[:, :], 0.0).then_inc(made, 1)
                pool.wait_ge(made, 7)

            @block.vector
            def _(v):
                c = Chain(v, dve)
                v.wait_ge(loaded, 6 * 16)
                v.wait_ge(made, 7)
                v.tensor_copy(iotaF[:, :], iotaI[:, :]).then_inc(dve, 1)
                v.tensor_copy(nodeF[:, :], nodeI[:, :]).then_inc(dve, 1)
                c.n = 2
                c.mark(v.tensor_copy(nbr[:, :], edge_rows[:, :]))
                c.link(v.tensor_copy(dstF[:, :], g.dstI[:, :]))
                c.mark(v.tensor_scalar(g.Lm[:, :], dstF[:, :], nbr[:, 0:1], None, ALU.is_equal))
                c.mark(v.tensor_scalar(g.Rm[:, :], dstF[:, :], nbr[:, 1:2], None, ALU.is_equal))
                c.mark(v.tensor_tensor(g.cont[:, 1:J], dstF[:, 1:J], dstF[:, 0:J - 1], ALU.is_equal))
                c.mark(v.tensor_tensor(g.cont[:, 0:1], dstF[:, 0:1], nbr[:, 0:1], ALU.is_equal))
                c.mark(v.tensor_tensor(g.isend[:, 0:J - 1], dstF[:, 1:J], dstF[:, 0:J - 1], ALU.not_equal))
                c.mark(v.memset(g.isend[:, J - 1:J], 1.0))
                c.mark(v.scalar_tensor_tensor(g.hpS[:, :], g.srcI[:, :], float(R), etI[:, :], ALU.mult, ALU.add))
                c.mark(v.scalar_tensor_tensor(g.hpD[:, :], g.dstI[:, :], float(R), etI[:, :], ALU.mult, ALU.add))
                c.mark(v.tensor_copy(g.row0[:, :], g.dstI[:, 0:1]))
                c.link(v.tensor_scalar(dstP[:, :], dstF[:, :], 1.0 / NB, -0.48, ALU.mult, ALU.add))
                c.link(v.tensor_copy(g.contz[:, :], g.cont[:, :]))
                c.link(v.memset(g.contz[:, :].rearrange("p (n k) -> p n k", k=K)[:, :, 0:1], 0.0))
                c.mark(v.tensor_scalar(g.notend[:, :], g.isend[:, :], -1.0, 1.0, ALU.mult, ALU.add))
                c.link(v.tensor_scalar(dstP[:, :], dstP[:, :], WHOLE, -WHOLE, ALU.add, ALU.add))
                c.link(v.scalar_tensor_tensor(dstB[:, :], dstP[:, :], -float(NB), dstF[:, :], ALU.mult, ALU.add))
                c.mark(v.tensor_scalar(diag[:, 0, :], g.ident[:, :], g.Lm[:, J - 1:J], None, ALU.mult))
                c.link(v.tensor_scalar(diag[:, 1, :], g.ident[:, :], g.Rm[:, 0:1], None, ALU.mult))
                v.sem_inc(split, 1)
                with v.Fori(0, NCH // 2) as i:
                    c.begin(i, 4)
                    for k in range(2):
                        v.wait_ge(counted[k], i + 1)
                        c.mark(v.tensor_copy(cols[:, k, 0, :], dstP[:, bass.ds((i * 2 + k) * K, K)]))
                        c.link(v.tensor_copy(cols[:, k, 1, :], dstB[:, bass.ds((i * 2 + k) * K, K)]))
                        v.tensor_tensor(hotP[:, k], cols[:, k, 0, :].unsqueeze(2).to_broadcast([P, K, P]),
                                        iotaF[:, :].unsqueeze(1).to_broadcast([P, K, P]), ALU.is_equal).then_inc(hot[k], 1)
                        v.tensor_tensor(hotB[:, k], cols[:, k, 1, :].unsqueeze(2).to_broadcast([P, K, NB]),
                                        iotaF[:, 0:NB].unsqueeze(1).to_broadcast([P, K, NB]), ALU.is_equal).then_inc(hot[k], 1)
                c.end(NCH // 2)
                deg, cum, tot, start, has = (w[:, n, :] for n in range(5))
                t1, q, cross, end, t2 = (w[:, n, :] for n in range(5, 10))
                v.wait_ge(rows, 1)
                c.mark(v.tensor_copy(g.contLrow[:, :], psR[:, 0, 0:P]))
                c.mark(v.tensor_copy(g.contRrow[:, :], psR[:, 1, 0:P]))
                v.wait_ge(rows, 2)
                c.link(v.tensor_copy(deg, psC[:, 0:NB]))
                c.link(v.tensor_tensor_scan(cum, ones[:, 0:NB], deg, 0.0, ALU.mult, ALU.add))
                c.link(v.tensor_copy(tot[:, 0:1], cum[:, NB - 1:NB]))
                v.sem_inc(total, 1)
                v.wait_ge(rows, 3)
                c.link(v.tensor_copy(tot[:, 1:2], psE[:, 0:1]))
                c.link(v.tensor_scalar(end, cum, tot[:, 1:2], -1.0, ALU.add, ALU.add))
                c.link(v.scalar_tensor_tensor(start, deg, -1.0, end, ALU.mult, ALU.add))
                c.link(v.tensor_scalar(start, start, 1.0, None, ALU.add))
                c.link(v.tensor_scalar(has, deg, 0.0, None, ALU.is_gt))
                c.mark(v.tensor_copy(g.has[:, :], has))
                c.mark(v.tensor_scalar(g.nothas[:, :], has, -1.0, 1.0, ALU.mult, ALU.add))
                c.link(v.tensor_scalar(t1, deg, 1.0, None, ALU.max))
                v.sem_inc(sq, 1)
                c.link(v.tensor_scalar(q, end, 1.0 / J, -(0.5 - 0.5 / J), ALU.mult, ALU.add))
                c.link(v.tensor_scalar(q, q, WHOLE, -WHOLE, ALU.add, ALU.add))
                c.link(v.scalar_tensor_tensor(cross, q, float(J), start, ALU.mult, ALU.is_gt))
                c.link(v.tensor_tensor(cross, cross, has, ALU.mult))
                c.link(v.tensor_tensor(cross, cross, q, ALU.mult))
                c.mark(v.tensor_copy(g.idxCar[:, :], cross))
                c.link(v.tensor_scalar(t2, end, -float(EP), None, ALU.add))
                c.link(v.tensor_tensor(t2, t2, has, ALU.mult))
                c.link(v.tensor_scalar(t2, t2, float(EP), None, ALU.add))
                c.link(v.tensor_copy(g.idxEnd[:, :], t2))
                c.link(v.tensor_scalar(nodeF[:, :], nodeF[:, :], float(EP), None, ALU.add))
                c.link(v.tensor_tensor(t2, start, nodeF[:, :], ALU.subtract))
                c.link(v.tensor_tensor(t2, t2, has, ALU.mult))
                c.link(v.tensor_tensor(t2, t2, nodeF[:, :], ALU.add))
                c.link(v.tensor_copy(g.idxStart[:, :], t2))
                v.wait_ge(sqd, 1)
                c.link(v.reciprocal(g.dinv[:, :], g.dinv[:, :]))
                c.link(v.tensor_tensor(g.dinv[:, :], g.dinv[:, :], has, ALU.mult))

            @block.scalar
            def _(act):
                act.wait_ge(zeroed, 1)
                z = zerof.shape[1]
                for n in range(16):
                    act.dma_start(g.start_rows.rearrange("(p j) c -> p (j c)", p=P)[:, n * z:(n + 1) * z],
                                  zerof[:, :]).then_inc(zeros, 16)
                act.dma_start(g.start_self.rearrange("(p j) c -> p (j c)", p=P)[:, 0:2048],
                              zerof[:, 0:2048]).then_inc(zeros, 16)
                act.dma_start(g.start_self.rearrange("(p j) c -> p (j c)", p=P)[:, 2048:4045],
                              zerof[:, 0:1997]).then_inc(zeros, 16)
                act.dma_start(g.scanned[EP:EP + P, :], zerof[:, 0:D]).then_inc(zeros, 16)
                act.dma_start(g.self_weight[EP:EP + P, :], zerof[:, 0:H]).then_inc(zeros, 16)
                act.wait_ge(sq, 1)
                act.activation(g.dinv[:, :], w[:, 5, :], ACT.Sqrt).then_inc(sqd, 1)
                act.wait_ge(zeros, 16 * 20)

            @block.tensor
            def _(pe):
                pe.sem_inc(counted[0], 1)
                pe.sem_inc(counted[1], 1)
                pe.wait_ge(made, 7)
                pe.wait_ge(split, 1)
                pe.matmul(psR[:, 0, 0:P], ones[:, :], diag[:, 0, :], start=True, stop=True)
                pe.matmul(psR[:, 1, 0:P], ones[:, :], diag[:, 1, :], start=True, stop=True).then_inc(rows, 1)
                pe.matmul(psC[:, 0:NB], zero[:, :], zero[:, 0:NB], start=True, stop=False, skip_group_check=True)
                with pe.Fori(0, NCH // 2) as i:
                    for k in range(2):
                        pe.wait_ge(hot[k], i * 2 + 2)
                        for j in range(K):
                            last = pe.matmul(psC[:, 0:NB], hotP[:, k, j, :], hotB[:, k, j, :], start=False,
                                             stop=False, skip_group_check=True)
                        last.then_inc(counted[k], 1)
                pe.matmul(psC[:, 0:NB], zero[:, :], zero[:, 0:NB], start=False, stop=True,
                          skip_group_check=True).then_inc(rows, 1)
                pe.wait_ge(total, 1)
                pe.matmul(psE[:, 0:1], lower[:, :], w[:, 2, 0:1], start=True, stop=True).then_inc(rows, 1)


def relation_table(nc, g, a):
    with phase(nc) as s:
        w = s.sb("relw", [P, R * D])
        xT = s.sb("xT", [P, 2, P])
        stage = s.sb("stage", [P, 2, R, 2 * D])
        psT = s.ps("psT", [D, 2, 512])
        psH = s.ps("psH", [P, 2, 1024])
        loaded, padded = s.sem("w_loaded"), s.sem("padded")
        turned, xT_ready, x_put = s.sem("turned"), s.sem("xT_ready"), s.sem("x_put")
        made = [s.sem(f"half_made{h}") for h in range(2)]
        evac = [s.sem(f"half_out{h}") for h in range(2)]
        stored = [s.sem(f"hpx_stored{k}") for k in range(2)]
        with nc.Block() as block:
            @block.sync
            def _(sp):
                sp.dma_start(w[0:D, :].rearrange("d (r e) -> d r e", r=R),
                             a["relw"].rearrange("r d e -> d r e")).then_inc(loaded, 16)
                for b in range(NB):
                    sp.wait_ge(evac[0], b + 1)
                    sp.wait_ge(evac[1], b + 1)
                    sp.wait_ge(x_put, b + 1)
                    sp.dma_start(g.hpx[0:NR * R, :].rearrange("(p b r) c -> p b (r c)", b=NB, r=R)[:, b, :],
                                 stage[:, b % 2].rearrange("p r c -> p (r c)")).then_inc(stored[b % 2], 16)
                for k in range(2):
                    sp.wait_ge(stored[k], 16 * ((NB + 1 - k) // 2))

            @block.gpsimd
            def _(pool):
                pool.memset(w[D:P, :], 0.0).then_inc(padded, 1)
                pool.memset(xT[D:P, :, :], 0.0).then_inc(padded, 1)

            @block.tensor
            def _(pe):
                for b in range(NB):
                    pe.transpose(psT[:, b % 2, 0:P], g.x[:, b, :], g.ident[:, :]).then_inc(turned, 1)
                    pe.wait_ge(xT_ready, b + 1)
                    if b == 0:
                        pe.wait_ge(loaded, 16)
                        pe.wait_ge(padded, 2)
                    for h in range(2):
                        if b >= 1:
                            pe.wait_ge(evac[h], b)
                        for q in range(2):
                            last = pe.matmul(psH[:, h, q * 512:(q + 1) * 512], xT[:, b % 2, :],
                                             w[:, (2 * h + q) * 512:(2 * h + q + 1) * 512], start=True, stop=True)
                        last.then_inc(made[h], 1)

            @block.scalar
            def _(act):
                for b in range(NB):
                    act.wait_ge(turned, b + 1)
                    if b >= 2:
                        act.wait_ge(made[1], b - 1)
                    act.activation(xT[0:D, b % 2, :], psT[:, b % 2, 0:P], ACT.Copy).then_inc(xT_ready, 1)
                    act.wait_ge(made[0], b + 1)
                    if b >= 2:
                        act.wait_ge(stored[b % 2], 16 * (b // 2))
                    act.activation(stage[:, b % 2, 0:R // 2, 0:D],
                                   psH[:, 0, :].rearrange("p (r e) -> p r e", e=D), ACT.Copy).then_inc(evac[0], 1)

            @block.vector
            def _(v):
                for b in range(NB):
                    if b >= 2:
                        v.wait_ge(stored[b % 2], 16 * (b // 2))
                    v.tensor_copy(stage[:, b % 2, :, D:2 * D],
                                  g.x[:, b, :].unsqueeze(1).to_broadcast([P, R, D])).then_inc(x_put, 1)
                    v.wait_ge(made[1], b + 1)
                    v.tensor_copy(stage[:, b % 2, R // 2:R, 0:D],
                                  psH[:, 1, :].rearrange("p (r e) -> p r e", e=D)).then_inc(evac[1], 1)


def gather_columns(pool, table, width, index, stage, buf, c, i, k, done, staged):
    c.link(pool.tensor_copy(stage[:, k, :], index[:, bass.ds((i * 2 + k) * K, K)]))
    pool.sem_inc(staged, 1)
    for j in range(K):
        pool.indirect_dma_start(buf[:, k, j, 0:width] if width == buf.shape[3] else buf[:, k, j, D:2 * D], None,
                                table, bass.IndirectOffsetOnAxis(stage[:, k, j:j + 1], 0)).then_inc(done[k], 16)


class Tiles:

    GS = 4
    NG = (TS + GS - 1) // GS

    def __init__(self, nc, g, s):
        self.nc, self.g = nc, g
        self.cols = s.sb("cols", [P, 2, 2, TS], bf16)
        self.hot = s.sb("hot", [P, 2, 2 * TS, P], bf16)
        self.tile = s.sb("tile", [P, 2, NB, TC], bf16)
        self.ps = s.ps("psA", [P, self.NG, 512])
        self.hot_made, self.hot_used, self.stored = (
            [s.sem(f"{n}{k}") for k in range(2)] for n in ("hot_made", "hot_used", "tile_stored"))
        self.counted, self.moved = s.sem("counted"), s.sem("moved")

    def one_hots(self, c, v, tile, k, turn):
        v.wait_ge(self.hot_used[k], turn + 1)
        at = bass.ds(tile * TS, TS) if not isinstance(tile, int) else slice(tile * TS, (tile + 1) * TS)
        c.link(v.tensor_copy(self.cols[:, k], self.g.colsT[:, :, at]))
        v.tensor_tensor(self.hot[:, k], self.cols[:, k].rearrange("p n s -> p (n s)").unsqueeze(2).to_broadcast([P, 2 * TS, P]),
                        self.g.iotaB[:, :].unsqueeze(1).to_broadcast([P, 2 * TS, P]), ALU.is_equal).then_inc(self.hot_made[k], 1)

    def pe_begin(self, pe):
        for k in range(2):
            pe.sem_inc(self.hot_used[k], 1)

    def products(self, pe, before, k, turn):
        NG, GS = self.NG, self.GS
        pe.wait_ge(self.hot_made[k], turn + 1)
        for n in range(NG):
            pe.wait_ge(self.moved, before * NG + n + 1)
            for j in range(min(GS, TS - n * GS)):
                st = n * GS + j
                last = pe.matmul(self.ps[:, n, j * TC:(j + 1) * TC], self.hot[:, k, st, :], self.hot[:, k, TS + st, 0:TC],
                                 start=True, stop=True)
            last.then_inc(self.counted, 1)
        pe.wait_ge(self.counted, before * NG + NG)
        pe.sem_inc(self.hot_used[k], 1)

    def act_begin(self, act):
        act.sem_inc(self.moved, self.NG)
        for k in range(2):
            act.sem_inc(self.stored[k], 16)

    def move(self, act, before, k, turn):
        act.wait_ge(self.stored[k], turn * 16 + 16)
        for n in range(self.NG):
            m = min(self.GS, TS - n * self.GS)
            act.wait_ge(self.counted, before * self.NG + n + 1)
            act.activation(self.tile[:, k, :, n * self.GS * WD:(n * self.GS + m) * WD],
                           self.ps[:, n, 0:m * TC].rearrange("p (s a) -> p a s", a=NB), ACT.Copy).then_inc(self.moved, 1)

    def store(self, sp, before, k):
        sp.wait_ge(self.moved, before * self.NG + 2 * self.NG)
        at = bass.ds(before * P, P) if not isinstance(before, int) else slice(before * P, (before + 1) * P)
        sp.dma_start(self.g.adj[at, :], self.tile[:, k].rearrange("p a c -> p (a c)")).then_inc(self.stored[k], 16)

    def sp_end(self, sp):
        sp.wait_ge(self.stored[0], ((NT + 1) // 2 + 1) * 16)
        sp.wait_ge(self.stored[1], (NT // 2 + 1) * 16)


def relation_scores(nc, g, a):
    TB = NT // (NCH // 2)
    assert TB % 2 == 0 and TB * (NCH // 2) == NT - 1
    with phase(nc) as s:
        stS, stD = s.sb("stS", [P, 2, K], i32), s.sb("stD", [P, 2, K], i32)
        rows_s, rows_d = s.sb("rows_s", [P, 2, K, 2 * D]), s.sb("rows_d", [P, 2, K, 2 * D])
        ef = s.sb("ef", [P, 2, K, D])
        sc = s.sb("sc", [P, 2, K])
        got_s = [s.pool_sem(g, k) for k in range(2)]
        got_d = [s.pool_sem(g, 2 + k) for k in range(2)]
        edge = [s.sem(f"edge{k}") for k in range(2)]
        stored = [s.sem(f"x_src_stored{k}") for k in range(2)]
        used, kept = [s.sem(f"used{k}") for k in range(2)], [s.sem(f"kept{k}") for k in range(2)]
        summed, tanh, pool_c, dve_c, staged = s.sem("summed"), s.sem("tanh"), s.sem("pool_c"), s.sem("dve_c"), s.sem("staged")
        tiles = Tiles(nc, g, s)
        with nc.Block() as block:
            @block.sync
            def _(sp):
                with sp.Fori(0, NCH // 2) as i:
                    for k in range(2):
                        sp.wait_ge(used[k], i + 1)
                        sp.dma_start(ef[:, k].rearrange("p j c -> p (j c)"),
                                     a["ef"].rearrange("(p j) c -> p (j c)", p=P)[:, bass.ds((i * 2 + k) * (K * D), K * D)]
                                     ).then_inc(edge[k], 16)
                        for r in range(k * TB // 2, (k + 1) * TB // 2):
                            tiles.store(sp, i * TB + r, r % 2)
                tiles.store(sp, NT - 1, 0)
                tiles.sp_end(sp)

            @block.gpsimd
            def _(pool):
                c = Chain(pool, pool_c)
                with pool.Fori(0, NCH // 2) as i:
                    c.begin(i, 4)
                    for k in range(2):
                        pool.wait_ge(used[k], i + 1)
                        pool.wait_ge(kept[k], i + 1)
                        gather_columns(pool, g.hpx, 2 * D, g.hpS, stS, rows_s, c, i, k, got_s, staged)
                        gather_columns(pool, g.hpx, 2 * D, g.hpD, stD, rows_d, c, i, k, got_d, staged)
                c.end(NCH // 2)

            @block.vector
            def _(v):
                c = Chain(v, dve_c)
                for k in range(2):
                    v.sem_inc(used[k], 1)
                with v.Fori(0, NCH // 2) as i:
                    c.begin(i, 4 + TB)
                    for k in range(2):
                        for r in range(k * TB // 2, (k + 1) * TB // 2):
                            tiles.one_hots(c, v, i * TB + r, r % 2, i * (TB // 2) + r // 2)
                        v.wait_ge(edge[k], i * 16 + 16)
                        v.wait_ge(got_d[k], i * (16 * K) + 16 * K)
                        v.tensor_tensor(ef[:, k], ef[:, k], rows_d[:, k, :, 0:D], ALU.add).then_inc(summed, 1)
                        v.wait_ge(tanh, i * 2 + k + 1)
                        v.wait_ge(got_s[k], i * (16 * K) + 16 * K)
                        c.link(v.tensor_tensor(ef[:, k], ef[:, k], rows_s[:, k, :, 0:D], ALU.mult))
                        c.link(v.tensor_reduce(sc[:, k, :], ef[:, k], X, ALU.add))
                        v.tensor_copy(g.score[:, 0, bass.ds((i * 2 + k) * K, K)], sc[:, k, :]).then_inc(used[k], 1)
                c.end(NCH // 2)
                tiles.one_hots(c, v, NT - 1, 0, NT // 2)

            @block.tensor
            def _(pe):
                tiles.pe_begin(pe)
                with pe.Fori(0, NCH // 2) as i:
                    for r in range(TB):
                        tiles.products(pe, i * TB + r, r % 2, i * (TB // 2) + r // 2)
                tiles.products(pe, NT - 1, 0, NT // 2)

            @block.scalar
            def _(act):
                for k in range(2):
                    act.sem_inc(kept[k], 1)
                tiles.act_begin(act)
                with act.Fori(0, NCH // 2) as i:
                    for k in range(2):
                        act.wait_ge(got_s[k], i * (16 * K) + 16 * K)
                        act.dma_start(g.x_src.rearrange("(p j) c -> p j c", p=P)[:, bass.ds((i * 2 + k) * K, K), :],
                                      rows_s[:, k, :, D:2 * D]).then_inc(stored[k], 16)
                        act.wait_ge(summed, i * 2 + k + 1)
                        act.activation(ef[:, k], ef[:, k], ACT.Tanh).then_inc(tanh, 1)
                        for r in range(k * TB // 2, (k + 1) * TB // 2):
                            tiles.move(act, i * TB + r, r % 2, i * (TB // 2) + r // 2)
                        act.wait_ge(stored[k], i * 16 + 16)
                        act.sem_inc(kept[k], 1)
                tiles.move(act, NT - 1, 0, NT // 2)


def carry_over(nc, g, s, heads, first, last, out, combine):
    big = combine == ALU.max
    neutral = -BIG if big else 0.0
    flag = s.sb("flag", [P, 2, P])
    left, right = s.sb("left", [D, P + 1]), s.sb("right", [D, P + 1])
    ps = s.ps("ps_carry", [P, 2, P])
    pt = s.ps("ps_carried", [P, 2, D])
    ready, turned, scanned, back, chain = (s.sem(f"carry_{n}") for n in ("ready", "turned", "scanned", "back", "chain"))
    with nc.Block() as block:
        @block.vector
        def _(v):
            c = Chain(v, chain)
            for n, row in enumerate((g.contLrow, g.contRrow)):
                if big:
                    c.mark(v.tensor_scalar(flag[:, n, :], row[:, :], BIG, -BIG, ALU.mult, ALU.add))
                else:
                    c.mark(v.tensor_copy(flag[:, n, :], row[:, :]))
            c.mark(v.memset(left[:, 0:1], neutral))
            c.link(v.memset(right[:, P:P + 1], neutral))
            op = ALU.add if big else ALU.mult
            v.wait_ge(turned, 1)
            v.tensor_tensor_scan(left[0:heads, 1:P + 1], flag[0:heads, 0, :], ps[0:heads, 0, :], neutral, op, combine)
            v.tensor_tensor_scan(right[0:heads, 0:P][:, ::-1], flag[0:heads, 1, ::-1], ps[0:heads, 1, ::-1], neutral,
                                 op, combine).then_inc(scanned, 1)
            v.wait_ge(back, 1)
            c.link(v.tensor_copy(out, pt[:, :, 0:heads]))

        @block.tensor
        def _(pe):
            pe.transpose(ps[0:heads, 0, :], last, g.ident[:, :])
            pe.transpose(ps[0:heads, 1, :], first, g.ident[:, :]).then_inc(turned, 1)
            pe.wait_ge(scanned, 1)
            pe.transpose(pt[:, 0, 0:heads], left[0:heads, 0:P], g.ident[0:heads, 0:heads])
            pe.transpose(pt[:, 1, 0:heads], right[0:heads, 1:P + 1], g.ident[0:heads, 0:heads]).then_inc(back, 1)


def softmax(nc, g, heads, selfs=None):
    for stage, combine in (("max", ALU.max), ("sum", ALU.add)):
        with phase(nc) as s:
            run = s.sb("run", [P, 2, J])
            total = s.sb("total", [P, heads, J])
            ends = s.sb("ends", [P, 2, heads])
            carried = s.sb("carried", [P, 2, heads])
            pen = s.sb("pen", [P, 3, J])
            chain, shifted, exped = s.sem("chain"), s.sem("shifted"), s.sem("exped")
            with nc.Block() as block:
                @block.vector
                def _(v):
                    c = Chain(v, chain)
                    if stage == "max":
                        for n, m in enumerate((g.cont, g.Lm, g.Rm)):
                            c.link(v.tensor_scalar(pen[:, n, :], m[:, :], BIG, -BIG, ALU.mult, ALU.add))
                    for h in range(heads):
                        if stage == "max":
                            c.link(v.tensor_tensor_scan(run[:, 0, :], pen[:, 0, :], g.score[:, h, :], -BIG, ALU.add, ALU.max))
                        else:
                            c.link(v.tensor_tensor_scan(run[:, 0, :], g.cont[:, :], g.score[:, h, :], 0.0, ALU.mult, ALU.add))
                        c.link(v.tensor_tensor(run[:, 1, :], run[:, 0, :], g.isend[:, :], ALU.mult))
                        c.link(v.tensor_tensor_scan(total[:, h, ::-1], g.notend[:, ::-1], run[:, 1, ::-1], 0.0, ALU.mult, ALU.add))
                        c.mark(v.tensor_copy(ends[:, 0, h:h + 1], total[:, h, 0:1]))
                        c.link(v.tensor_copy(ends[:, 1, h:h + 1], total[:, h, J - 1:J]))
            carry_over(nc, g, s, heads, ends[:, 0, :], ends[:, 1, :], carried[:, :, :], combine)
            with nc.Block() as block:
                @block.vector
                def _(v):
                    c = Chain(v, chain)
                    c.n = (3 if stage == "max" else 0) + 5 * heads
                    if stage == "max":
                        for h in range(heads):
                            for n in range(2):
                                c.link(v.scalar_tensor_tensor(total[:, h, :], pen[:, 1 + n, :], carried[:, n, h:h + 1],
                                                              total[:, h, :], ALU.add, ALU.max))
                        if selfs is not None:
                            c.link(v.tensor_tensor(total[:, :, :], total[:, :, :], selfs, ALU.max))
                            c.mark(v.tensor_tensor(selfs, selfs, total[:, :, :], ALU.subtract))
                        c.link(v.tensor_tensor(g.score[:, 0:heads, :], g.score[:, 0:heads, :], total[:, :, :], ALU.subtract))
                        v.sem_inc(shifted, 1)
                    else:
                        for h in range(heads):
                            for n, m in enumerate((g.Lm, g.Rm)):
                                c.link(v.scalar_tensor_tensor(total[:, h, :], m[:, :], carried[:, n, h:h + 1],
                                                              total[:, h, :], ALU.mult, ALU.add))
                        if selfs is not None:
                            c.link(v.tensor_tensor(total[:, :, :], total[:, :, :], selfs, ALU.add))
                            c.link(v.tensor_scalar(total[:, :, :], total[:, :, :], 1.0e-16, float(H), ALU.add, ALU.mult))
                        c.link(v.reciprocal(total[:, :, :], total[:, :, :]))
                        if selfs is not None:
                            c.mark(v.tensor_tensor(selfs, selfs, total[:, :, :], ALU.mult))
                        c.link(v.tensor_tensor(g.score[:, 0:heads, :], g.score[:, 0:heads, :], total[:, :, :], ALU.mult))

                if stage == "max":
                    @block.scalar
                    def _(act):
                        act.wait_ge(shifted, 1)
                        if selfs is not None:
                            act.activation(selfs, selfs, ACT.Exp).then_inc(exped, 1)
                        act.activation(g.score[:, 0:heads, :], g.score[:, 0:heads, :], ACT.Exp).then_inc(exped, 1)


def scan_columns(v, c, out, data, prev, cont):
    for f in range(D):
        last = v.tensor_tensor_scan(out[:, :, f], cont, data[:, :, f], prev[:, f:f + 1], ALU.mult, ALU.add)
    c.link(last)


class Sums:

    def __init__(self, g, s, queue_sems):
        self.g = g
        self.flags, self.msg, self.sums = (s.sb(n, [P, 2, D, K]) for n in ("flags", "msg", "sums"))
        self.run, self.cs = s.sb("run", [P, 2, K, D]), s.sb("cs", [P, 2, 1])
        self.flagged = [s.sem(f"flagged{k}") for k in range(2)]
        self.scanned, self.ready = s.sem("scanned"), s.sem("ready")
        self.free, self.stored = [s.sem(f"free{k}") for k in range(2)], queue_sems

    def dve_begin(self, c, v):
        v.sem_inc(self.scanned, 2)
        c.link(v.memset(self.sums[:, 1, :, K - 1], 0.0))

    def first_flag(self, c, v, i, k):
        c.link(v.tensor_copy(self.cs[:, k, :], self.g.cont[:, bass.ds((i * 2 + k) * K, 1)]))

    def scan(self, c, v, i, k):
        msg, sums = self.msg, self.sums
        c.link(v.scalar_tensor_tensor(msg[:, k, :, 0], sums[:, 1 - k, :, K - 1], self.cs[:, k, :], msg[:, k, :, 0], ALU.mult, ALU.add))
        v.wait_ge(self.flagged[k], i + 1)
        v.wait_ge(self.ready, i * 2 + k + 1)
        flat = lambda t: t[:, k].rearrange("p c j -> p (c j)")
        c.link(v.tensor_tensor_scan(flat(sums), flat(self.flags), flat(msg), 0.0, ALU.mult, ALU.add))
        v.sem_inc(self.scanned, 1)

    def dve_end(self, c, v):
        c.link(v.tensor_copy(self.g.tail[:, :], self.sums[:, 1, :, K - 1]))

    def act_begin(self, act):
        act.sem_inc(self.ready, 2)

    def flag(self, act, i, k):
        act.wait_ge(self.scanned, i * 2 + k + 1)
        act.activation(self.flags[:, k], self.g.contz[:, bass.ds((i * 2 + k) * K, K)].unsqueeze(1).to_broadcast([P, D, K]),
                       ACT.Copy).then_inc(self.flagged[k], 1)

    def turn(self, act, i, k):
        act.wait_ge(self.scanned, i * 2 + k + 3)
        act.wait_ge(self.free[k], i + 1)
        act.activation(self.run[:, k], self.sums[:, k].rearrange("p c j -> p j c"), ACT.Copy).then_inc(self.ready, 1)

    def store(self, eng, i, k):
        eng.wait_ge(self.ready, i * 2 + k + 3)
        eng.dma_start(self.g.scanned[0:EP, :].rearrange("(p j) c -> p (j c)", p=P)[:, bass.ds((i * 2 + k) * (K * D), K * D)],
                      self.run[:, k].rearrange("p j c -> p (j c)")).then_inc(self.stored[k], 16)

    def store_all(self, eng):
        for k in range(2):
            eng.sem_inc(self.free[k], 1)
        with eng.Fori(0, NCH // 2) as i:
            for k in range(2):
                self.store(eng, i, k)
                eng.wait_ge(self.stored[k], i * 16 + 16)
                eng.sem_inc(self.free[k], 1)


def weighted_sums(nc, g):
    with phase(nc) as s:
        rows, ws = s.sb("rows", [P, 2, K, D]), s.sb("ws", [P, 2, K])
        sums = Sums(g, s, [s.pool_sem(g, k) for k in range(2)])
        got = [s.sem(f"got{k}") for k in range(2)]
        used = [s.sem(f"used{k}") for k in range(2)]
        dve_c = s.sem("dve_c")
        with nc.Block() as block:
            @block.sync
            def _(sp):
                with sp.Fori(0, NCH // 2) as i:
                    for k in range(2):
                        sp.wait_ge(used[k], i + 1)
                        sp.dma_start(rows[:, k].rearrange("p j c -> p (j c)"),
                                     g.x_src.rearrange("(p j) c -> p (j c)", p=P)[:, bass.ds((i * 2 + k) * (K * D), K * D)]
                                     ).then_inc(got[k], 16)

            @block.vector
            def _(v):
                c = Chain(v, dve_c)
                for k in range(2):
                    v.sem_inc(used[k], 1)
                sums.dve_begin(c, v)
                with v.Fori(0, NCH // 2) as i:
                    c.begin(i, 10)
                    for k in range(2):
                        sums.first_flag(c, v, i, k)
                        c.link(v.tensor_copy(ws[:, k, :], g.score[:, 0, bass.ds((i * 2 + k) * K, K)]))
                        v.wait_ge(got[k], i * 16 + 16)
                        c.link(v.tensor_tensor(sums.msg[:, k], rows[:, k].rearrange("p j c -> p c j"),
                                               ws[:, k, :].unsqueeze(1).to_broadcast([P, D, K]), ALU.mult))
                        v.sem_inc(used[k], 1)
                        sums.scan(c, v, i, k)
                c.end(NCH // 2)
                sums.dve_end(c, v)

            @block.scalar
            def _(act):
                sums.act_begin(act)
                with act.Fori(0, NCH // 2) as i:
                    for k in range(2):
                        sums.flag(act, i, k)
                        sums.turn(act, i, k)

            @block.gpsimd
            def _(pool):
                sums.store_all(pool)


def node_sums(nc, g, out):
    with phase(nc) as s:
        part = s.sb("part", [P, NB, D])
        carried = s.sb("carried", [P, 2, D])
        carry_over(nc, g, s, D, g.tail[:, :], g.tail[:, :], carried[:, :, :], ALU.add)
        kept, got_e, got_c, chain = s.sem("kept"), s.pool_sem(g, 0), s.pool_sem(g, 1), s.sem("chain")
        with nc.Block() as block:
            @block.sync
            def _(sp):
                sp.dma_start(g.carry, carried[:, 0, :]).then_inc(kept, 16)
                sp.wait_ge(kept, 16)

            @block.gpsimd
            def _(pool):
                for b in range(NB):
                    pool.indirect_dma_start(out[:, b, :], None, g.scanned,
                                            bass.IndirectOffsetOnAxis(g.idxEnd[:, b:b + 1], 0)).then_inc(got_e, 16)
                pool.wait_ge(kept, 16)
                for b in range(NB):
                    pool.indirect_dma_start(part[:, b, :], None, g.carry,
                                            bass.IndirectOffsetOnAxis(g.idxCar[:, b:b + 1], 0)).then_inc(got_c, 16)

            @block.vector
            def _(v):
                v.wait_ge(got_e, 16 * NB)
                v.wait_ge(got_c, 16 * NB)
                v.tensor_tensor(out[:, :, :], out[:, :, :], part[:, :, :], ALU.add).then_inc(chain, 1)
                v.wait_ge(chain, 1)


def node_linear(nc, g, srcs, weights, out):
    with phase(nc) as s:
        S, nout = len(srcs), out.shape[3]
        kin = srcs[0].shape[2]
        xT = s.sb("xT", [kin, 2, S, P])
        psT = s.ps("psT", [kin, 2, 512])
        psZ = s.ps("psZ", [P, 2, 512])
        turned, ready, made, evac = (s.sem(n) for n in ("turned", "ready", "made", "evac"))
        with nc.Block() as block:
            @block.tensor
            def _(pe):
                for b in range(NB):
                    for n in range(S):
                        last = pe.transpose(psT[:, b % 2, n * P:(n + 1) * P], srcs[n][:, b, :], g.ident[:, :])
                    last.then_inc(turned, 1)
                    pe.wait_ge(ready, b + 1)
                    if b >= 2:
                        pe.wait_ge(evac, b - 1)
                    for n in range(S):
                        last = pe.matmul(psZ[:, b % 2, n * nout:(n + 1) * nout], xT[:, b % 2, n, :], weights[n],
                                         start=True, stop=True)
                    last.then_inc(made, 1)

            @block.scalar
            def _(act):
                for b in range(NB):
                    act.wait_ge(turned, b + 1)
                    if b >= 2:
                        act.wait_ge(made, b - 1)
                    act.activation(xT[:, b % 2], psT[:, b % 2, 0:S * P].rearrange("k (s e) -> k s e", s=S),
                                   ACT.Copy).then_inc(ready, 1)

            @block.vector
            def _(v):
                for b in range(NB):
                    v.wait_ge(made, b + 1)
                    v.tensor_copy(out[:, b], psZ[:, b % 2, 0:S * nout].rearrange("p (s n) -> p s n", s=S)).then_inc(evac, 1)
                v.wait_ge(evac, NB)


def layernorm(v, c, data, tmp, stat, var_ready, std_ready, at=1):
    over = lambda t: t.unsqueeze(2).to_broadcast([P, NB, D])
    c.link(v.tensor_reduce(stat[:, 0, :], data, X, ALU.add))
    c.link(v.tensor_scalar(stat[:, 0, :], stat[:, 0, :], 1.0 / D, None, ALU.mult))
    c.link(v.tensor_tensor(data, data, over(stat[:, 0, :]), ALU.subtract))
    c.link(v.tensor_tensor(tmp, data, data, ALU.mult))
    c.link(v.tensor_reduce(stat[:, 1, :], tmp, X, ALU.add))
    v.tensor_scalar(stat[:, 1, :], stat[:, 1, :], 1.0 / D, LN_EPS, ALU.mult, ALU.add).then_inc(var_ready, 1)
    v.wait_ge(std_ready, at)
    c.link(v.reciprocal(stat[:, 2, :], stat[:, 2, :]))
    c.link(v.tensor_tensor(data, data, over(stat[:, 2, :]), ALU.mult))


def root(act, stat, var_ready, std_ready, at=1):
    act.wait_ge(var_ready, at)
    act.activation(stat[:, 2, :], stat[:, 1, :], ACT.Sqrt).then_inc(std_ready, 1)


def relation_output(nc, g, a, nbh):
    with phase(nc) as s:
        ab = s.sb("ab", [P, 2, NB, D])
        wr, wT = s.sb("wr", [D, 2, D]), s.sb("wT", [D, 2, D])
        z = s.sb("z", [P, NB, 2, D])
        stat = s.sb("stat", [P, 3, NB])
        ps = s.ps("psw", [D, 2, D])
        loaded, turned, chain, var_ready, std_ready = (s.sem(n) for n in ("loaded", "wturned", "chain", "var", "std"))
        with nc.Block() as block:
            @block.sync
            def _(sp):
                sp.dma_start(wr[:, 0, :], a["rw1"]).then_inc(loaded, 16)
                sp.dma_start(wr[:, 1, :], a["rw2"]).then_inc(loaded, 16)

            @block.tensor
            def _(pe):
                pe.wait_ge(loaded, 32)
                for n in range(2):
                    last = pe.transpose(ps[:, n, :], wr[:, n, :], g.ident[0:D, 0:D])
                last.then_inc(turned, 1)

            @block.vector
            def _(v):
                c = Chain(v, chain)
                c.mark(v.tensor_tensor(ab[:, 0], g.x[:, :, :], nbh[:, :, :], ALU.add))
                c.mark(v.tensor_tensor(ab[:, 1], g.x[:, :, :], nbh[:, :, :], ALU.mult))
                v.wait_ge(turned, 1)
                c.link(v.tensor_copy(wT[:, :, :], ps[:, :, :]))
        node_linear(nc, g, [ab[:, 0], ab[:, 1]], [wT[:, 0, :], wT[:, 1, :]], z)
        with nc.Block() as block:
            @block.vector
            def _(v):
                c = Chain(v, chain)
                c.n = 3
                c.link(v.scalar_tensor_tensor(z[:, :, :, :].rearrange("p b s d -> p (b s d)"),
                                              z[:, :, :, :].rearrange("p b s d -> p (b s d)"), 0.01,
                                              z[:, :, :, :].rearrange("p b s d -> p (b s d)"), ALU.mult, ALU.max))
                c.link(v.tensor_tensor(g.x[:, :, :], g.x[:, :, :], z[:, :, 0, :], ALU.add))
                c.link(v.tensor_tensor(g.x[:, :, :], g.x[:, :, :], z[:, :, 1, :], ALU.add))
                layernorm(v, c, g.x[:, :, :], ab[:, 0], stat, var_ready, std_ready)

            @block.scalar
            def _(act):
                root(act, stat, var_ready, std_ready)


def adjacency(nc, g, a):
    g.colsT, g.iotaB = g.hot.sb("colsT", [P, 2, S], bf16), g.hot.sb("iotaB", [P, P], bf16)
    with phase(nc) as t:
        first_i, first = t.sb("first_i", [CH // 7, 7], i32), t.sb("first", [CH // 7, 7])
        ones, iotaI = t.sb("ones", [P, P]), t.sb("iotaI", [P, P], i32)
        diag = t.sb("diag", [CH // 7, 7, CH // 7])
        win, begin = t.sb("win", [P, CH]), t.sb("begin", [P, CH])
        chunk_i, stepG_i, stepR_i, win_i = (t.sb("chunk_i", [P, 7, CH // 7], i32), t.sb("stepG_i", [SP, SQ], i32),
                                            t.sb("stepR_i", [SP, SQ + 1], i32), t.sb("win_i", [NW // WD, WD], i32))
        stepG, stepR, winF = t.sb("stepG", [SP, SQ]), t.sb("stepR", [SP, SQ + 1]), t.sb("winF", [NW // WD, WD])
        before = t.sb("before", [P, SQ + 1, CH], bf16)
        chG, chR, chW = t.sb("chG", [SP, SQ]), t.sb("chR", [SP, SQ + 1]), t.sb("chW", [NW // WD, WD])
        chG_i = t.sb("chG_i", [SP, SQ], i32)
        raw = t.sb("raw", [SP, 2, SQ, CE], i32)
        srcF, dstF, quo = t.sb("srcF_c", [SP, SQ, CE]), t.sb("dstF_c", [SP, SQ, CE]), t.sb("quo", [SP, SQ, CE])
        shift, band, diag2 = t.sb("shift", [SP, SP]), t.sb("band", [SP, SP]), t.sb("diag2", [SP, SP])
        psW, psS, psT = t.ps("psW", [P, 2, 512]), t.ps("psS", [P, 512]), t.ps("psT", [P, 2, 512])
        loaded, made, dve, cols, wide, flags, spread, turned, taken = (
            t.sem(n) for n in ("loaded", "made", "dve", "cols", "wide", "flags", "spread", "turned", "taken"))
        got, rows_in = t.pool_sem(g, 0), t.sem("rows_in")
        with nc.Block() as block:
            @block.sync
            def _(sp):
                sp.dma_start(first_i[:, :].unsqueeze(2), a["dst"].rearrange("(p q e) -> p q e", q=7, e=CE)[:, :, 0:1],
                             allow_slow_non_contiguous=True).then_inc(loaded, 16)
                sp.wait_ge(loaded, 16)

            @block.gpsimd
            def _(pool):
                pool.memset(ones[:, :], 1.0).then_inc(made, 1)
                pool.iota(iotaI[:, :], pattern=[[1, P]], base=0, channel_multiplier=0).then_inc(made, 1)
                pool.iota(chunk_i[:, :, :], pattern=[[1, 7], [7, CH // 7]], base=0, channel_multiplier=0).then_inc(made, 1)
                pool.iota(stepG_i[:, :], pattern=[[SP, SQ]], base=0, channel_multiplier=1).then_inc(made, 1)
                pool.iota(stepR_i[:, :], pattern=[[1, SQ + 1]], base=-1, channel_multiplier=SQ).then_inc(made, 1)
                pool.iota(win_i[:, :], pattern=[[1, WD]], base=0, channel_multiplier=WD).then_inc(made, 1)
                pool.wait_ge(made, 6)
                pool.memset(band[:, :], 0.0).then_inc(made, 1)
                pool.wait_ge(made, 7)
                pool.affine_select(out=band[:, :], in_=band[:, :], compare_op=ALU.not_equal, fill=1.0,
                                   base=1, pattern=[[-1, SP]], channel_multiplier=1).then_inc(made, 1)
                pool.wait_ge(made, 8)
                pool.wait_ge(cols, 1)
                for q in range(SQ):
                    for n, name in enumerate(("src", "dst")):
                        pool.indirect_dma_start(raw[:, n, q, :], None, a[name].rearrange("(c e) -> c e", e=CE),
                                                bass.IndirectOffsetOnAxis(chG_i[:, q:q + 1], 0)).then_inc(got, 16)
                pool.wait_ge(got, 2 * SQ * 16)
                pool.sem_inc(rows_in, 1)

            @block.tensor
            def _(pe):
                pe.wait_ge(wide, 1)
                for q in range(7):
                    at = (q % 4) * (CH // 7)
                    last = pe.matmul(psW[:, q // 4, at:at + CH // 7], ones[0:CH // 7, :], diag[:, q, :], start=True, stop=True)
                last.then_inc(spread, 1)
                pe.wait_ge(flags, 1)
                pe.matmul(psS[0:SP, 0:SP], ones[0:SP, 0:SP], diag2[:, :], start=True, stop=True).then_inc(spread, 1)
                pe.wait_ge(wide, 2)
                for q in range(SQ):
                    if q >= 2:
                        pe.wait_ge(taken, q - 1)
                    pe.transpose(psT[:, q % 2, 0:SP], quo[:, q, :], g.ident[0:SP, 0:SP])
                    pe.transpose(psT[:, q % 2, P:P + SP], dstF[:, q, :], g.ident[0:SP, 0:SP]).then_inc(turned, 1)

            @block.vector
            def _(v):
                c = Chain(v, dve)
                v.wait_ge(loaded, 16)
                v.wait_ge(made, 8)
                c.mark(v.tensor_copy(g.iotaB[:, :], iotaI[:, :]))
                c.mark(v.tensor_copy(stepG[:, :], stepG_i[:, :]))
                c.mark(v.tensor_copy(stepR[:, :], stepR_i[:, :]))
                c.mark(v.tensor_copy(winF[:, :], win_i[:, :]))
                c.mark(v.tensor_copy(begin[:, :], chunk_i[:, :, :].rearrange("p q c -> p (q c)")))
                c.link(v.tensor_copy(first[:, :], first_i[:, :]))
                c.link(v.tensor_scalar(first[:, :], first[:, :], 1.0 / WD, -0.4, ALU.mult, ALU.add))
                c.link(v.tensor_scalar(first[:, :], first[:, :], WHOLE, -WHOLE, ALU.add, ALU.add))
                c.link(v.tensor_tensor(diag[:, :, :], first[:, :].unsqueeze(2).to_broadcast([CH // 7, 7, CH // 7]),
                                       g.ident[0:CH // 7, 0:CH // 7].unsqueeze(1).to_broadcast([CH // 7, 7, CH // 7]), ALU.mult))
                v.sem_inc(wide, 1)
                v.wait_ge(spread, 1)
                half = 4 * (CH // 7)
                c.mark(v.tensor_copy(win[:, 0:half], psW[:, 0, 0:half]))
                c.link(v.tensor_copy(win[:, half:CH], psW[:, 1, 0:CH - half]))
                c.link(v.tensor_tensor(begin[:, :], begin[:, :], win[:, :], ALU.add))

                def chunks(out, bounds, at, rows, n):
                    c.link(v.tensor_tensor(before[0:rows, 0:n, :], bounds[0:rows, :].unsqueeze(1).to_broadcast([rows, n, CH]),
                                           at[:, :].unsqueeze(2).to_broadcast([rows, n, CH]), ALU.is_le))
                    c.link(v.tensor_reduce(out[:, :], before[0:rows, 0:n, :], X, ALU.add))
                    c.link(v.tensor_scalar(out[:, :], out[:, :], -1.0, None, ALU.add))

                chunks(chG, begin, stepG, SP, SQ)
                c.link(v.tensor_scalar(chG[:, :], chG[:, :], 0.0, None, ALU.max))
                c.link(v.tensor_copy(chG_i[:, :], chG[:, :]))
                v.sem_inc(cols, 1)
                chunks(chR, begin, stepR, SP, SQ + 1)
                c.link(v.tensor_tensor(g.same[:, :], chR[:, 1:SQ + 1], chR[:, 0:SQ], ALU.subtract))
                c.link(v.tensor_tensor_scan(g.prefix[:, :], g.same[:, :], g.same[:, :], 1.0, ALU.mult, ALU.min))
                c.link(v.tensor_scalar(diag2[:, :], g.ident[0:SP, 0:SP], g.prefix[:, SQ - 1:SQ], None, ALU.mult))
                v.sem_inc(flags, 1)
                chunks(chW, win, winF, NW // WD, WD)
                c.link(v.tensor_scalar(chW[:, :], chW[:, :], 0.0, None, ALU.max))
                c.link(v.tensor_tensor(chW[:, :], chW[:, :], winF[:, :], ALU.add))
                c.link(v.tensor_copy(g.last_step[:, :], chW[:, :]))
                v.wait_ge(spread, 2)
                c.mark(v.memset(shift[:, 0:1], 0.0))
                c.link(v.tensor_copy(shift[:, 1:SP], psS[0:SP, 0:SP - 1]))
                c.link(v.tensor_tensor_scan(g.hand[:, :], shift[:, :], band[:, :], 0.0, ALU.mult, ALU.add))
                c.link(v.tensor_tensor(stepG[:, :], stepG[:, :], chG[:, :], ALU.subtract))
                c.link(v.tensor_scalar(stepG[:, :], stepG[:, :], float(WD * NB), None, ALU.mult))
                v.wait_ge(rows_in, 1)
                c.mark(v.tensor_copy(srcF[:, :, :], raw[:, 0]))
                c.link(v.tensor_copy(dstF[:, :, :], raw[:, 1]))
                c.link(v.tensor_scalar(quo[:, :, :], srcF[:, :, :], 1.0 / NB, -0.48, ALU.mult, ALU.add))
                c.link(v.tensor_scalar(quo[:, :, :], quo[:, :, :], WHOLE, -WHOLE, ALU.add, ALU.add))
                c.link(v.scalar_tensor_tensor(srcF[:, :, :], quo[:, :, :], -float(NB), srcF[:, :, :], ALU.mult, ALU.add))
                c.link(v.scalar_tensor_tensor(dstF[:, :, :], dstF[:, :, :], float(NB), srcF[:, :, :], ALU.mult, ALU.add))
                c.link(v.tensor_tensor(dstF[:, :, :], dstF[:, :, :], stepG[:, :].unsqueeze(2).to_broadcast([SP, SQ, CE]),
                                       ALU.subtract))
                c.link(v.tensor_scalar(dstF[:, :, :], dstF[:, :, :], -1.0, 255.0, ALU.max, ALU.min))
                v.sem_inc(wide, 1)
                for q in range(SQ):
                    v.wait_ge(turned, q + 1)
                    v.tensor_copy(g.colsT[:, 0, q * SP:(q + 1) * SP], psT[:, q % 2, 0:SP])
                    v.tensor_copy(g.colsT[:, 1, q * SP:(q + 1) * SP], psT[:, q % 2, P:P + SP]).then_inc(taken, 1)
                v.wait_ge(taken, SQ)


def propagate(nc, g, y):
    with phase(nc) as s:
        parts = s.sb("parts", [P, NB, 3, D], bf16)
        with phase(nc) as t:
            rest = t.sb("rest", [P, NB, D])
            chain = t.sem("chain")
            with nc.Block() as block:
                @block.vector
                def _(v):
                    c = Chain(v, chain)
                    c.link(v.tensor_tensor(rest[:, :, :], y[:, :, :], g.dinv[:, :].unsqueeze(2).to_broadcast([P, NB, D]), ALU.mult))
                    for n in range(3):
                        c.link(v.tensor_copy(parts[:, :, n, :], rest[:, :, :]))
                        if n < 2:
                            c.link(v.tensor_tensor(rest[:, :, :], rest[:, :, :], parts[:, :, n, :], ALU.subtract))
        B = 3
        tile, z = s.sb("tile", [P, B, NB, TC], bf16), s.sb("z", [TC, B, D])
        psY = s.ps("psY", [P, B, 512])
        three = lambda name: [s.sem(f"{name}{k}") for k in range(B)]
        tile_in, used, product, summed, stored = (three(n) for n in ("tile_in", "used", "product", "summed", "stored"))
        with nc.Block() as block:
            @block.sync
            def _(sp):
                with sp.Fori(0, NT // B) as i:
                    for k in range(B):
                        sp.wait_ge(used[k], i + 1)
                        sp.dma_start(tile[:, k].rearrange("p a c -> p (a c)"),
                                     g.adj[bass.ds((i * B + k) * P, P), :]).then_inc(tile_in[k], 16)

            @block.tensor
            def _(pe):
                for k in range(B):
                    pe.sem_inc(used[k], 1)
                with pe.Fori(0, NT // B) as i:
                    for k in range(B):
                        pe.wait_ge(tile_in[k], i * 16 + 16)
                        pe.wait_ge(summed[k], i + 1)
                        for b in range(NB):
                            last = pe.matmul(psY[0:TC, k, 0:3 * D], tile[:, k, b, :], parts[:, b].rearrange("p n c -> p (n c)"),
                                             start=b == 0, stop=b == NB - 1)
                        last.then_inc(product[k], 1)
                        pe.wait_ge(product[k], i + 1)
                        pe.sem_inc(used[k], 1)

            @block.vector
            def _(v):
                for k in range(B):
                    v.sem_inc(summed[k], 1)
                with v.Fori(0, NT // B) as i:
                    for k in range(B):
                        v.wait_ge(product[k], i + 1)
                        v.wait_ge(stored[k], i * 16 + 16)
                        v.tensor_reduce(z[:, k, :], psY[0:TC, k, 0:3 * D].rearrange("p (n c) -> p c n", n=3), X, ALU.add
                                        ).then_inc(summed[k], 1)

            @block.scalar
            def _(act):
                for k in range(B):
                    act.sem_inc(stored[k], 16)
                with act.Fori(0, NT // B) as i:
                    for k in range(B):
                        act.wait_ge(summed[k], i + 2)
                        act.dma_start(g.step_rows[bass.ds((i * B + k) * TC, TC), :], z[:, k, :]).then_inc(stored[k], 16)
                for k in range(B):
                    act.wait_ge(stored[k], (NT // B + 1) * 16)
    with phase(nc) as s:
        acc, back = s.sb("acc", [SP, SQ, WD * D]), s.sb("back", [SP, WD * D])
        psH = s.ps("psH", [P, 512])
        loaded, chain, tails, handed, ready, put, got = (
            s.sem("loaded"), s.sem("chain"), s.sem("tails"), s.sem("handed"), s.sem("ready"), s.sem("put"), s.pool_sem(g, 0))
        with nc.Block() as block:
            @block.sync
            def _(sp):
                rows = lambda ap: ap.rearrange("(p q d) c -> p q (d c)", p=SP, d=WD)
                sp.dma_start(acc[:, :, :], rows(g.step_rows)).then_inc(loaded, 16)
                sp.wait_ge(ready, 1)
                sp.dma_start(rows(g.step_sums), acc[:, :, :]).then_inc(put, 16)

            @block.vector
            def _(v):
                c = Chain(v, chain)
                v.wait_ge(loaded, 16)
                for q in range(1, SQ):
                    c.link(v.scalar_tensor_tensor(acc[:, q, :], acc[:, q - 1, :], g.same[:, q:q + 1], acc[:, q, :], ALU.mult, ALU.add))
                v.sem_inc(tails, 1)
                v.wait_ge(handed, 1)
                c.link(v.tensor_copy(back[:, :], psH[0:SP, 0:WD * D]))
                for q in range(SQ):
                    c.mark(v.scalar_tensor_tensor(acc[:, q, :], back[:, :], g.prefix[:, q:q + 1], acc[:, q, :], ALU.mult, ALU.add))
                c.wait()
                v.sem_inc(ready, 1)

            @block.tensor
            def _(pe):
                pe.wait_ge(tails, 1)
                pe.matmul(psH[0:SP, 0:WD * D], g.hand[:, :], acc[:, SQ - 1, :], start=True, stop=True).then_inc(handed, 1)

            @block.gpsimd
            def _(pool):
                pool.wait_ge(put, 16)
                for q in range(WD):
                    pool.indirect_dma_start(y[0:NW // WD, q * WD:(q + 1) * WD, :].rearrange("p b c -> p (b c)"), None,
                                            g.step_sums.rearrange("(s d) c -> s (d c)", d=WD),
                                            bass.IndirectOffsetOnAxis(g.last_step[:, q:q + 1], 0)).then_inc(got, 16)
                pool.wait_ge(got, WD * 16)
    with phase(nc) as s:
        chain = s.sem("chain")
        with nc.Block() as block:
            @block.vector
            def _(v):
                c = Chain(v, chain)
                c.link(v.tensor_tensor(y[:, :, :], y[:, :, :], g.dinv[:, :].unsqueeze(2).to_broadcast([P, NB, D]), ALU.mult))


def add_norm(nc, g, terms, first=None):
    with phase(nc) as s:
        tmp, stat = s.sb("tmp", [P, NB, D]), s.sb("stat", [P, 3, NB])
        chain, var_ready, std_ready = s.sem("chain"), s.sem("var"), s.sem("std")
        with nc.Block() as block:
            @block.vector
            def _(v):
                c = Chain(v, chain)
                if first is not None:
                    first(v, c)
                for t in terms:
                    c.link(v.tensor_tensor(g.x[:, :, :], g.x[:, :, :], t, ALU.add))
                layernorm(v, c, g.x[:, :, :], tmp[:, :, :], stat, var_ready, std_ready)

            @block.scalar
            def _(act):
                root(act, stat, var_ready, std_ready)


def put_nodes(nc, g, h, loops=None):
    with phase(nc) as s:
        put, sent, got = s.sem("put"), s.pool_sem(g, 0), s.pool_sem(g, 1)
        with nc.Block() as block:
            @block.sync
            def _(sp):
                sp.dma_start(g.table.rearrange("(p b) d -> p b d", b=NB), h[:, :, :]).then_inc(put, 16)
                if loops is not None:
                    sp.dma_start(g.table_self.rearrange("(p b) d -> p b d", b=NB), loops[:, :, :]).then_inc(put, 16)

            @block.gpsimd
            def _(pool):
                for b in range(NB):
                    at = bass.IndirectOffsetOnAxis(g.idxStart[:, b:b + 1], 0)
                    pool.indirect_dma_start(g.start_rows, at, h[:, b, :], None).then_inc(sent, 16)
                    if loops is not None:
                        pool.indirect_dma_start(g.start_self, at, loops[:, b, :], None).then_inc(sent, 16)
                at = bass.IndirectOffsetOnAxis(g.row0[:, 0:1], 0)
                pool.wait_ge(put, 16 if loops is None else 32)
                pool.indirect_dma_start(g.row_start[:, :], None, g.table, at).then_inc(got, 16)
                if loops is not None:
                    pool.indirect_dma_start(g.row_self[:, :], None, g.table_self, at).then_inc(got, 16)
                pool.wait_ge(got, 16 if loops is None else 32)
                pool.wait_ge(sent, 16 * NB if loops is None else 32 * NB)


def split_bias(nc, row, b3, ones3):
    n = b3.shape[1]
    with phase(nc) as s:
        low = s.sb("low", [1, 3, n], bf16)
        moved, chain, split = s.sem("b_moved"), s.sem("b_chain"), s.sem("b_split")
        with nc.Block() as block:
            @block.sync
            def _(sp):
                sp.wait_ge(split, 1)
                for q in range(3):
                    sp.dma_start(b3[q:q + 1, :], low[0:1, q, :]).then_inc(moved, 16)
                sp.wait_ge(moved, 48)

            @block.vector
            def _(v):
                c = Chain(v, chain)
                c.mark(v.memset(ones3[:, :], 1.0))
                c.link(v.memset(b3[:, :], 0.0))
                for q in range(3):
                    c.link(v.tensor_copy(low[0:1, q, :], row))
                    if q < 2:
                        c.link(v.tensor_tensor(row, row, low[0:1, q, :], ALU.subtract))
                v.sem_inc(split, 1)


def gated_convolution(nc, g, a):
    G = 4
    NG = K // G
    with phase(nc) as s:
        w1, w2 = s.sb("w1", [2 * D, 2 * D]), s.sb("w2", [DE, 2 * D])
        b3, ones3 = s.sb("b3", [P, 2 * D], bf16), s.sb("ones3", [P, P], bf16)
        row = s.sb("bias_row", [1, 2 * D])
        b_in = s.sem("b_in")
        with nc.Block() as block:
            @block.sync
            def _(sp):
                sp.dma_start(row[0:1, 0:D], a["bf"].rearrange("(o n) -> o n", o=1)).then_inc(b_in, 16)
                sp.dma_start(row[0:1, D:2 * D], a["bs"].rearrange("(o n) -> o n", o=1)).then_inc(b_in, 16)
                sp.wait_ge(b_in, 32)
        split_bias(nc, row[0:1, :], b3, ones3)
        stage = s.sb("stage_i", [P, 2, K], i32)
        both = s.sb("both", [P, 2, K, 2 * D])
        starts = s.sb("starts", [P, 2, K, D])
        ea = s.sb("ea", [P, 2, K, DE])
        bothT, eaT = s.sb("bothT", [P, 2, G, P]), s.sb("eaT", [P, 2, G, P])
        la = s.sb("la", [P, 4, G, 2 * D])
        gate, core = s.sb("gate", [P, 4, G, D]), s.sb("core", [P, 4, G, D])
        sums = Sums(g, s, [s.sem(f"stored{k}") for k in range(2)])
        cs = s.sb("cs_k", [P, 2, K])
        sums.cs = cs[:, :, 0:1]
        psB, psE, psZ = s.ps("psB", [P, 2, G, P]), s.ps("psE", [P, 2, G, P]), s.ps("psZ", [P, 4, G, P])
        two = lambda name: [s.sem(f"{name}{k}") for k in range(2)]
        loaded_s, loaded_e, used, spread = (
            two(n) for n in ("starts_in", "ea_in", "slot_used", "spread"))
        got = [s.pool_sem(g, k) for k in range(2)]
        dve_c, pool_c, staged, w_in = s.sem("dve_c"), s.sem("pool_c"), s.sem("staged"), s.sem("w_in")
        turned, both_out, ea_out, made, logs, low, sig, chained, multiplied = (
            s.sem(n) for n in ("turned", "both_out", "ea_out", "made", "logs", "low", "sig", "chained", "multiplied"))
        grp = lambda i, k, n: i * (2 * NG) + (k * NG + n + 1)
        with nc.Block() as block:
            @block.sync
            def _(sp):
                sp.dma_start(w1[:, 0:D], a["Wf"][0:2 * D, :]).then_inc(w_in, 16)
                sp.dma_start(w1[:, D:2 * D], a["Ws"][0:2 * D, :]).then_inc(w_in, 16)
                sp.dma_start(w2[:, 0:D], a["Wf"][2 * D:2 * D + DE, :]).then_inc(w_in, 16)
                sp.dma_start(w2[:, D:2 * D], a["Ws"][2 * D:2 * D + DE, :]).then_inc(w_in, 16)
                sp.sem_inc(sums.free[0], 1)
                with sp.Fori(0, NCH // 2) as i:
                    for k in range(2):
                        sp.wait_ge(spread[k], i + 1)
                        sp.dma_start(starts[:, k].rearrange("p j c -> p (j c)"),
                                     g.start_rows[0:EP, :].rearrange("(p j) c -> p (j c)", p=P)[:, bass.ds((i * 2 + k) * (K * D), K * D)]
                                     ).then_inc(loaded_s[k], 16)
                        sp.wait_ge(used[k], i + 1)
                        sp.dma_start(ea[:, k].rearrange("p j c -> p (j c)"),
                                     a["ea"].rearrange("(p j) c -> p (j c)", p=P)[:, bass.ds((i * 2 + k) * (K * DE), K * DE)]
                                     ).then_inc(loaded_e[k], 16)
                    sums.store(sp, i, 0)
                    sp.wait_ge(sums.stored[0], i * 16 + 16)
                    sp.sem_inc(sums.free[0], 1)

            @block.gpsimd
            def _(pool):
                c = Chain(pool, pool_c)
                with pool.Fori(0, NCH // 2) as i:
                    c.begin(i, 2)
                    for k in range(2):
                        pool.wait_ge(used[k], i + 1)
                        gather_columns(pool, g.table, D, g.srcI, stage, both, c, i, k, got, staged)
                c.end(NCH // 2)

            @block.tensor
            def _(pe):
                for k in range(2):
                    pe.sem_inc(used[k], 1)
                pe.wait_ge(w_in, 64)
                with pe.Fori(0, NCH // 2) as i:
                    for n in range(2 * NG + 1):
                        if n < 2 * NG:
                            k, m = divmod(n, NG)
                            if m == 0:
                                pe.wait_ge(spread[k], i + 2)
                                pe.wait_ge(got[k], i * (16 * K) + 16 * K)
                                pe.wait_ge(loaded_e[k], i * 16 + 16)
                            for j in range(G):
                                pe.transpose(psB[:, n % 2, j, :], both[:, k, m * G + j, :], g.ident[:, :])
                            for j in range(G):
                                last = pe.transpose(psE[:, n % 2, j, :], ea[:, k, m * G + j, :], g.ident[:, :])
                            last.then_inc(turned, 1)
                            if m == NG - 1:
                                pe.wait_ge(turned, grp(i, 0, n))
                                pe.sem_inc(used[k], 1)
                        if n >= 1:
                            q = n - 1
                            pe.wait_ge(both_out, grp(i, 0, q))
                            pe.wait_ge(ea_out, grp(i, 0, q))
                            pe.wait_ge(logs, grp(i, 0, max(q - 4, -1)) + 1)
                            pe.wait_ge(low, grp(i, 0, max(q - 4, -1)) + 1)
                            for j in range(G):
                                pe.matmul(psZ[:, q % 4, j, :], ones3[:, :], b3[:, :], start=True, stop=False)
                                pe.matmul(psZ[:, q % 4, j, :], bothT[:, q % 2, j, :], w1[:, :], start=False, stop=False)
                                last = pe.matmul(psZ[:, q % 4, j, :], eaT[:, q % 2, j, :], w2[:, :], start=False, stop=True)
                            last.then_inc(made, 1)

            @block.scalar
            def _(act):
                act.preload_act_table_set("natural_log_exp_and_others")
                act.sem_inc(logs, 1)
                sums.act_begin(act)
                act.sem_inc(sums.stored[1], 16)

                def turn(i, first):
                    for n in range(2 * NG + 2):
                        if n % NG == 0 and n < 2 * NG:
                            sums.flag(act, i, n // NG)
                        if n == 4 and not first:
                            sums.turn(act, i - 1, 1)
                            sums.store(act, i - 1, 1)
                        if n == NG + 5:
                            sums.turn(act, i, 0)
                            act.wait_ge(sums.stored[1], i * 16 + 16)
                            act.sem_inc(sums.free[1], 1)
                        if n < 2 * NG:
                            act.wait_ge(turned, grp(i, 0, n))
                            if n >= 2:
                                act.wait_ge(made, grp(i, 0, n - 2))
                            act.activation(bothT[:, n % 2], psB[:, n % 2], ACT.Copy).then_inc(both_out, 1)
                            act.activation(eaT[:, n % 2], psE[:, n % 2], ACT.Copy).then_inc(ea_out, 1)
                        if 1 <= n <= 2 * NG:
                            q = n - 1
                            act.wait_ge(made, grp(i, 0, q))
                            if q >= 4:
                                act.wait_ge(low, grp(i, 0, q - 4) + 1)
                            act.activation(la[:, q % 4], psZ[:, q % 4], ACT.Abs).then_inc(chained, 1)
                            act.wait_ge(chained, i * (4 * NG) + 2 * q + 1)
                            act.activation(la[:, q % 4], la[:, q % 4], ACT.Exp, scale=-1.0).then_inc(chained, 1)
                            act.wait_ge(chained, i * (4 * NG) + 2 * q + 2)
                            act.activation(la[:, q % 4], la[:, q % 4], ACT.Ln, bias=1.0).then_inc(logs, 1)
                        if n >= 2:
                            q = n - 2
                            act.wait_ge(low, grp(i, 0, q) + 1)
                            act.activation(gate[:, q % 4], gate[:, q % 4], ACT.Exp).then_inc(sig, 1)

                turn(0, True)
                with act.Fori(1, NCH // 2) as i:
                    turn(i, False)
                sums.turn(act, NCH // 2 - 1, 1)
                sums.store(act, NCH // 2 - 1, 1)
                act.wait_ge(sums.stored[1], (NCH // 2 + 1) * 16)

            @block.vector
            def _(v):
                c = Chain(v, dve_c)
                for k in range(2):
                    v.sem_inc(spread[k], 1)
                c.mark(v.tensor_copy(both[:, 1, K - 1, 0:D], g.row_start[:, :]))
                sums.dve_begin(c, v)
                v.sem_inc(low, 1)

                def spread_starts(i, k):
                    c.link(v.tensor_copy(cs[:, k, :], g.cont[:, bass.ds((i * 2 + k) * K, K)]))
                    v.wait_ge(loaded_s[k], i * 16 + 16)
                    v.wait_ge(used[k], i + 1)
                    scan_columns(v, c, both[:, k], starts[:, k], both[:, 1 - k, K - 1, 0:D], cs[:, k, :])
                    v.sem_inc(spread[k], 1)

                def turn(i, last):
                    for n in range(2 * NG + 3):
                        if n == NG - 2:
                            spread_starts(i, 1)
                        if n == 2 * NG - 1 and not last:
                            spread_starts(i + 1, 0)
                        if 1 <= n <= 2 * NG:
                            q = n - 1
                            v.wait_ge(logs, grp(i, 0, q) + 1)
                            if q >= 4:
                                v.wait_ge(multiplied, grp(i, 0, q - 4))
                            v.scalar_tensor_tensor(gate[:, q % 4], psZ[:, q % 4, :, 0:D], 0.0, la[:, q % 4, :, 0:D],
                                                   ALU.min, ALU.subtract)
                            v.scalar_tensor_tensor(core[:, q % 4], psZ[:, q % 4, :, D:2 * D], 0.0, la[:, q % 4, :, D:2 * D],
                                                   ALU.max, ALU.add).then_inc(low, 1)
                        if n >= 3:
                            q = n - 3
                            k, m = divmod(q, NG)
                            v.wait_ge(sig, grp(i, 0, q))
                            v.wait_ge(low, grp(i, 0, q) + 1)
                            v.tensor_tensor(sums.msg[:, k, :, m * G:(m + 1) * G].rearrange("p c g -> p g c"), gate[:, q % 4], core[:, q % 4],
                                            ALU.mult).then_inc(multiplied, 1)
                            if m == NG - 1:
                                v.wait_ge(multiplied, grp(i, 0, q))
                                sums.scan(c, v, i, k)

                spread_starts(0, 0)
                with v.Fori(0, NCH // 2 - 1) as i:
                    c.begin(i, 8)
                    turn(i, False)
                c.end(NCH // 2 - 1)
                turn(NCH // 2 - 1, True)
                sums.dve_end(c, v)


def gat_weights(nc, g, a, layer):
    s = g.layer
    w = lambda name: a[name.format(layer)]
    g.wrl, g.wl = s.sb("wrl", [2 * D, HD + H]), s.sb("wl", [D, HD])
    g.bl, g.brl, g.att, g.bias = s.sb("bl", [P, HD]), s.sb("brl", [P, HD + H]), s.sb("att", [P, HD]), s.sb("bias", [P, D])
    g.brl3, g.ones3 = s.sb("brl3", [P, HD + H], bf16), s.sb("ones3", [P, P], bf16)
    g.wlb = s.sb("wlb", [P, HD])
    g.att1 = s.sb("att1", [P, H, D + 1])
    with phase(nc) as t:
        loaded, zeroed, chain = t.sem("loaded"), t.sem("zeroed"), t.sem("chain")
        prod, row = t.sb("prod_w", [P, HD]), t.sb("row", [1, HD + H])
        with nc.Block() as block:
            @block.sync
            def _(sp):
                sp.dma_start(g.wrl[0:D, 0:HD], w("W{}r")).then_inc(loaded, 16)
                sp.dma_start(g.wrl[D:2 * D, 0:HD], w("W{}l")).then_inc(loaded, 16)
                sp.dma_start(g.wl[:, :], w("W{}l")).then_inc(loaded, 16)
                sp.dma_start(g.bl[:, :], w("b{}l").partition_broadcast(P)).then_inc(loaded, 16)
                sp.dma_start(g.brl[:, 0:HD], w("b{}r").partition_broadcast(P)).then_inc(loaded, 16)
                sp.dma_start(g.att[:, :], w("att{}").rearrange("h c -> (h c)").partition_broadcast(P)).then_inc(loaded, 16)
                sp.dma_start(g.bias[:, :], w("bias{}").partition_broadcast(P)).then_inc(loaded, 16)
                sp.wait_ge(zeroed, 1)
                sp.dma_start(g.wlb[0:D, :], w("W{}l")).then_inc(loaded, 16)
                sp.dma_start(g.wlb[D:D + 1, :], w("b{}l").rearrange("(o n) -> o n", o=1)).then_inc(loaded, 16)
                sp.wait_ge(loaded, 9 * 16)

            @block.gpsimd
            def _(pool):
                pool.memset(g.wlb[:, :], 0.0).then_inc(zeroed, 1)

            @block.vector
            def _(v):
                v.wait_ge(loaded, 9 * 16)
                c = Chain(v, chain)
                c.link(v.tensor_tensor(g.brl[:, 0:HD], g.brl[:, 0:HD], g.bl[:, :], ALU.add))
                for w_ in (g.wrl, g.brl):
                    c.link(v.tensor_tensor(prod[:, :], w_[:, 0:HD], g.att[:, :], ALU.mult))
                    c.link(v.tensor_reduce(w_[:, HD:HD + H], prod[:, :].rearrange("p (h c) -> p h c", h=H), X, ALU.add))
                    c.link(v.tensor_scalar(w_[:, HD:HD + H], w_[:, HD:HD + H], 0.6, None, ALU.mult))
                c.mark(v.memset(g.att1[:, :, D:D + 1], 1.0))
                c.mark(v.tensor_scalar(g.att1[:, :, 0:D], g.att[:, :].rearrange("p (h c) -> p h c", h=H), 0.4, None, ALU.mult))
                c.link(v.tensor_copy(row[0:1, :], g.brl[0:1, :]))
        split_bias(nc, row[0:1, :], g.brl3, g.ones3)


def gat_loops(nc, g, h, loops):
    with phase(nc) as s:
        hh, z = s.sb("hh", [P, NB, 2 * D]), s.sb("zz", [P, NB, 1, HD])
        chain = s.sem("chain")
        with nc.Block() as block:
            @block.vector
            def _(v):
                c = Chain(v, chain)
                c.mark(v.tensor_copy(hh[:, :, 0:D], h[:, :, :]))
                c.link(v.tensor_copy(hh[:, :, D:2 * D], h[:, :, :]))
        node_linear(nc, g, [hh[:, :, :]], [g.wrl[:, 0:HD]], z)
        with nc.Block() as block:
            @block.vector
            def _(v):
                c = Chain(v, chain)
                c.n = 2
                flat = z[:, :, 0, :]
                over = lambda t: t[:, 0:HD].unsqueeze(1).to_broadcast([P, NB, HD])
                c.link(v.tensor_tensor(flat, flat, over(g.brl), ALU.add))
                c.link(v.scalar_tensor_tensor(flat, flat, 0.2, flat, ALU.mult, ALU.max))
                c.link(v.tensor_tensor(flat, flat, over(g.att), ALU.mult))
                c.link(v.tensor_reduce(loops[:, :, :], flat.rearrange("p b (h c) -> p b h c", h=H), X, ALU.add))


class Spread:

    def __init__(self, g, s, starts, loaded, both, used, spread):
        self.g, self.starts, self.loaded, self.both, self.used, self.spread = g, starts, loaded, both, used, spread
        self.flags, self.data, self.vals = (s.sb(n, [P, 2, D, K]) for n in ("flags", "data", "vals"))
        self.cs = s.sb("cs", [P, 2, 1])
        self.laid, self.scanned = [s.sem(f"laid{k}") for k in range(2)], s.sem("scanned")

    def lay(self, act, i, k):
        act.wait_ge(self.scanned, i * 2 + k + 1)
        act.wait_ge(self.loaded[k], i * 16 + 16)
        act.activation(self.data[:, k], self.starts[:, k].rearrange("p j c -> p c j"), ACT.Copy)
        act.activation(self.flags[:, k], self.g.contz[:, bass.ds((i * 2 + k) * K, K)].unsqueeze(1).to_broadcast([P, D, K]),
                       ACT.Copy).then_inc(self.laid[k], 1)

    def hand(self, act, i, k):
        act.wait_ge(self.scanned, i * 2 + k + 3)
        act.wait_ge(self.used[k], i + 1)
        act.activation(self.both[:, k, :, 0:D], self.vals[:, k].rearrange("p c j -> p j c"), ACT.Copy).then_inc(self.spread[k], 1)

    def dve_begin(self, c, v):
        v.sem_inc(self.scanned, 2)
        for k in range(2):
            v.sem_inc(self.spread[k], 1)
        c.link(v.tensor_copy(self.vals[:, 1, :, K - 1], self.g.row_start[:, :]))

    def scan(self, c, v, i, k):
        data, vals = self.data, self.vals
        c.link(v.tensor_copy(self.cs[:, k, :], self.g.cont[:, bass.ds((i * 2 + k) * K, 1)]))
        v.wait_ge(self.laid[k], i + 1)
        c.link(v.scalar_tensor_tensor(data[:, k, :, 0], vals[:, 1 - k, :, K - 1], self.cs[:, k, :], data[:, k, :, 0], ALU.mult, ALU.add))
        v.wait_ge(self.spread[k], i + 1)
        flat = lambda t: t[:, k].rearrange("p c j -> p (c j)")
        c.link(v.tensor_tensor_scan(flat(vals), flat(self.flags), flat(data), 0.0, ALU.mult, ALU.add))
        v.sem_inc(self.scanned, 1)


def gat_scores(nc, g):
    G = 2
    NG = K // G
    with phase(nc) as s:
        stage = s.sb("stage_i", [P, 2, K], i32)
        both, starts = s.sb("both", [P, 2, K, 2 * D]), s.sb("starts", [P, 2, K, D])
        bothT, lz = s.sb("bothT", [P, 2, G, P]), s.sb("lz", [P, 4, G, H, D + 1])
        sc = s.sb("sc", [P, 2, K, H])
        psB, psZ = s.ps("psB", [P, 2, 512]), s.ps("psZ", [P, 2, G, 512])
        two = lambda name: [s.sem(f"{name}{k}") for k in range(2)]
        loaded_s, used, spread, stored, kept = (two(n) for n in ("starts_in", "slot_used", "spread", "stored", "kept"))
        got = [s.pool_sem(g, k) for k in range(2)]
        dve_c, pool_c, staged, turned, out, made, leaky, prod, scored = (
            s.sem(n) for n in ("dve_c", "pool_c", "staged", "turned", "both_out", "made", "leaky", "prod", "scored"))
        over = Spread(g, s, starts, loaded_s, both, used, spread)
        grp = lambda i, n: i * (2 * NG) + (n + 1)
        with nc.Block() as block:
            @block.sync
            def _(sp):
                with sp.Fori(0, NCH // 2) as i:
                    for k in range(2):
                        sp.wait_ge(spread[k], i + 1)
                        sp.dma_start(starts[:, k].rearrange("p j c -> p (j c)"),
                                     g.start_rows[0:EP, :].rearrange("(p j) c -> p (j c)", p=P)[:, bass.ds((i * 2 + k) * (K * D), K * D)]
                                     ).then_inc(loaded_s[k], 16)

            @block.gpsimd
            def _(pool):
                c = Chain(pool, pool_c)
                with pool.Fori(0, NCH // 2) as i:
                    c.begin(i, 2)
                    for k in range(2):
                        pool.wait_ge(used[k], i + 1)
                        pool.wait_ge(kept[k], i + 1)
                        gather_columns(pool, g.table, D, g.srcI, stage, both, c, i, k, got, staged)
                c.end(NCH // 2)

            @block.tensor
            def _(pe):
                pe.sem_inc(made, 2)
                for k in range(2):
                    pe.sem_inc(used[k], 1)
                with pe.Fori(0, NCH // 2) as i:
                    for n in range(2 * NG + 1):
                        if n < 2 * NG:
                            k, m = divmod(n, NG)
                            if m == 0:
                                pe.wait_ge(spread[k], i + 2)
                                pe.wait_ge(got[k], i * (16 * K) + 16 * K)
                            for j in range(G):
                                last = pe.transpose(psB[:, n % 2, j * P:(j + 1) * P], both[:, k, m * G + j, :], g.ident[:, :])
                            last.then_inc(turned, 1)
                            if m == NG - 1:
                                pe.wait_ge(turned, grp(i, n))
                                pe.sem_inc(used[k], 1)
                        if n >= 1:
                            q = n - 1
                            pe.wait_ge(out, grp(i, q))
                            pe.wait_ge(leaky, grp(i, q))
                            for j in range(G):
                                pe.matmul(psZ[:, q % 2, j, 0:HD + H], g.ones3[:, :], g.brl3[:, :], start=True, stop=False)
                                last = pe.matmul(psZ[:, q % 2, j, 0:HD + H], bothT[:, q % 2, j, :], g.wrl[:, :],
                                                 start=False, stop=True)
                            last.then_inc(made, 1)

            @block.scalar
            def _(act):
                act.sem_inc(leaky, 2)
                for k in range(2):
                    act.sem_inc(kept[k], 1)

                def turn(i, last):
                    for n in range(2 * NG + 1):
                        if n == NG - 10:
                            over.lay(act, i, 1)
                        if n == NG - 2:
                            over.hand(act, i, 1)
                        if n == NG + 1 and not last:
                            over.lay(act, i + 1, 0)
                        if n == 2 * NG - 5 and not last:
                            over.hand(act, i + 1, 0)
                        if n < 2 * NG:
                            k, m = divmod(n, NG)
                            if m == 0:
                                act.wait_ge(got[k], i * (16 * K) + 16 * K)
                                act.dma_start(g.x_src.rearrange("(p j) c -> p j c", p=P)[:, bass.ds((i * 2 + k) * K, K), :],
                                              both[:, k, :, D:2 * D]).then_inc(stored[k], 16)
                            act.wait_ge(turned, grp(i, n))
                            act.wait_ge(made, grp(i, n))
                            act.activation(bothT[:, n % 2], psB[:, n % 2, 0:G * P].rearrange("p (g e) -> p g e", g=G),
                                           ACT.Copy).then_inc(out, 1)
                            if m == NG - 1:
                                act.wait_ge(stored[k], i * 16 + 16)
                                act.sem_inc(kept[k], 1)
                        if n >= 1:
                            q = n - 1
                            act.wait_ge(made, grp(i, q) + 2)
                            act.wait_ge(scored, grp(i, q))
                            act.activation(lz[:, q % 4, :, :, 0:D], psZ[:, q % 2, :, 0:HD].rearrange("p g (h c) -> p g h c", h=H),
                                           ACT.Abs)
                            act.activation(lz[:, q % 4, :, :, D], psZ[:, q % 2, :, HD:HD + H], ACT.Copy).then_inc(leaky, 1)

                over.lay(act, 0, 0)
                over.hand(act, 0, 0)
                with act.Fori(0, NCH // 2 - 1) as i:
                    turn(i, False)
                turn(NCH // 2 - 1, True)

            @block.vector
            def _(v):
                c = Chain(v, dve_c)
                over.dve_begin(c, v)

                def turn(i, last):
                    for n in range(2 * NG + 1):
                        if n == NG - 4:
                            over.scan(c, v, i, 1)
                        if n == 2 * NG - 8 and not last:
                            over.scan(c, v, i + 1, 0)
                        if n < 2 * NG:
                            v.wait_ge(leaky, grp(i, n) + 2)
                            v.tensor_tensor(lz[:, n % 4].rearrange("p g h c -> p g (h c)"),
                                            lz[:, n % 4].rearrange("p g h c -> p g (h c)"),
                                            g.att1[:, :, :].rearrange("p h c -> p (h c)").unsqueeze(1).to_broadcast([P, G, HD + H]),
                                            ALU.mult).then_inc(prod, 1)
                        if n >= 1:
                            q = n - 1
                            k, m = divmod(q, NG)
                            v.wait_ge(prod, grp(i, q))
                            v.tensor_reduce(sc[:, k, m * G:(m + 1) * G, :],
                                            lz[:, q % 4], X, ALU.add).then_inc(scored, 1)
                            if m == NG - 1:
                                v.wait_ge(scored, grp(i, q) + 4)
                                c.link(v.tensor_copy(g.score[:, :, bass.ds((i * 2 + k) * K, K)],
                                                     sc[:, k].rearrange("p j h -> p h j")))

                v.sem_inc(scored, 4)
                over.scan(c, v, 0, 0)
                with v.Fori(0, NCH // 2 - 1) as i:
                    c.begin(i, 8)
                    turn(i, False)
                c.end(NCH // 2 - 1)
                turn(NCH // 2 - 1, True)


def spread_loops(nc, g, selfs):
    with phase(nc) as s:
        at = s.sb("at_starts", [P, J, H])
        loaded, chain = s.sem("loaded"), s.sem("chain")
        with nc.Block() as block:
            @block.sync
            def _(sp):
                sp.dma_start(at[:, :, :].rearrange("p j h -> p (j h)"),
                             g.start_self[0:EP, :].rearrange("(p j) h -> p (j h)", p=P)).then_inc(loaded, 16)

            @block.vector
            def _(v):
                c = Chain(v, chain)
                v.wait_ge(loaded, 16)
                for h in range(H):
                    c.mark(v.tensor_tensor_scan(selfs[:, h, :], g.cont[:, :], at[:, :, h], g.row_self[:, h:h + 1], ALU.mult, ALU.add))
                c.wait()


def gather_loop_weights(nc, g, selfs, loops):
    with phase(nc) as s:
        at = s.sb("at_edges", [P, J, H])
        turned, kept, got, chain = s.sem("turned"), s.sem("kept"), s.pool_sem(g, 0), s.sem("chain")
        with nc.Block() as block:
            @block.vector
            def _(v):
                v.tensor_copy(at[:, :, :], selfs.rearrange("p h j -> p j h")).then_inc(turned, 1)
                c = Chain(v, chain)
                v.wait_ge(got, 16 * NB)
                for h in range(H):
                    c.mark(v.scalar_tensor_tensor(loops[:, :, h], g.nothas[:, :], 1.0 / H, loops[:, :, h], ALU.mult, ALU.add))
                c.wait()

            @block.sync
            def _(sp):
                sp.wait_ge(turned, 1)
                sp.dma_start(g.self_weight[0:EP, :].rearrange("(p j) h -> p (j h)", p=P),
                             at[:, :, :].rearrange("p j h -> p (j h)")).then_inc(kept, 16)

            @block.gpsimd
            def _(pool):
                pool.wait_ge(kept, 16)
                for b in range(NB):
                    pool.indirect_dma_start(loops[:, b, :], None, g.self_weight,
                                            bass.IndirectOffsetOnAxis(g.idxEnd[:, b:b + 1], 0)).then_inc(got, 16)


def gat_sums(nc, g):
    G = 2
    NG = K // G
    with phase(nc) as s:
        rows = s.sb("rows", [P, 2, K, P])
        sums = Sums(g, s, [s.pool_sem(g, k) for k in range(2)])
        rowsT, prod = s.sb("rowsT", [P, 2, G, P]), s.sb("prod", [P, 2, G, HD])
        ws = s.sb("ws", [P, 2, K, H])
        psT, psZ = s.ps("psT", [P, 2, 512]), s.ps("psZ", [P, 2, G, 512])
        two = lambda name: [s.sem(f"{name}{k}") for k in range(2)]
        got, used = (two(n) for n in ("got", "slot_used"))
        padded, dve_c, begun, turned, out, made, weighed, summed = (
            s.sem(n) for n in ("padded", "dve_c", "begun", "turned", "rows_out", "made", "weighed", "summed"))
        grp = lambda i, n: i * (2 * NG) + (n + 1)
        with nc.Block() as block:
            @block.sync
            def _(sp):
                with sp.Fori(0, NCH // 2) as i:
                    for k in range(2):
                        sp.wait_ge(used[k], i + 1)
                        sp.dma_start(rows[:, k, :, 0:D],
                                     g.x_src.rearrange("(p j) c -> p j c", p=P)[:, bass.ds((i * 2 + k) * K, K), :]
                                     ).then_inc(got[k], 16)

            @block.gpsimd
            def _(pool):
                sums.store_all(pool)

            @block.tensor
            def _(pe):
                for k in range(2):
                    pe.sem_inc(used[k], 1)
                pe.wait_ge(padded, 2)
                pe.sem_inc(made, 2)
                with pe.Fori(0, NCH // 2) as i:
                    for n in range(2 * NG + 1):
                        if n < 2 * NG:
                            k, m = divmod(n, NG)
                            if m == 0:
                                pe.wait_ge(got[k], i * 16 + 16)
                                pe.sem_inc(begun, 1)
                            for j in range(G):
                                last = pe.transpose(psT[:, n % 2, j * P:(j + 1) * P], rows[:, k, m * G + j, :], g.ident[:, :])
                            last.then_inc(turned, 1)
                            if m == NG - 1:
                                pe.wait_ge(turned, grp(i, n))
                                pe.sem_inc(used[k], 1)
                        if n >= 1:
                            q = n - 1
                            pe.wait_ge(out, grp(i, q))
                            pe.wait_ge(weighed, grp(i, q))
                            for j in range(G):
                                last = pe.matmul(psZ[:, q % 2, j, 0:HD], rowsT[:, q % 2, j, :], g.wlb[:, :],
                                                 start=True, stop=True)
                            last.then_inc(made, 1)

            @block.scalar
            def _(act):
                sums.act_begin(act)

                def turn(i, first):
                    for n in range(2 * NG):
                        if n == 4 and not first:
                            sums.turn(act, i - 1, 1)
                        if n % NG == 6:
                            sums.flag(act, i, n // NG)
                        if n == NG + 3:
                            sums.turn(act, i, 0)
                        act.wait_ge(turned, grp(i, n))
                        act.wait_ge(made, grp(i, n))
                        act.activation(rowsT[:, n % 2], psT[:, n % 2, 0:G * P].rearrange("p (g e) -> p g e", g=G),
                                       ACT.Copy).then_inc(out, 1)

                turn(0, True)
                with act.Fori(1, NCH // 2) as i:
                    turn(i, False)
                sums.turn(act, NCH // 2 - 1, 1)

            @block.vector
            def _(v):
                c = Chain(v, dve_c)
                v.memset(rows[:, :, :, D:D + 1], 1.0).then_inc(padded, 1)
                v.memset(rows[:, :, :, D + 1:P], 0.0).then_inc(padded, 1)
                sums.dve_begin(c, v)
                v.sem_inc(weighed, 2)
                v.sem_inc(summed, 2)

                def weights(i, k):
                    sums.first_flag(c, v, i, k)
                    c.link(v.tensor_copy(ws[:, k].rearrange("p j h -> p h j"), g.score[:, :, bass.ds((i * 2 + k) * K, K)]))

                with v.Fori(0, NCH // 2) as i:
                    c.begin(i, 8)
                    weights(i, 0)
                    for n in range(2 * NG + 1):
                        if n == NG - 2:
                            weights(i, 1)
                        if n < 2 * NG:
                            k, m = divmod(n, NG)
                            v.wait_ge(made, grp(i, n) + 2)
                            v.wait_ge(summed, grp(i, n))
                            v.tensor_tensor(prod[:, n % 2].rearrange("p g (h c) -> p g h c", h=H),
                                            psZ[:, n % 2, :, 0:HD].rearrange("p g (h c) -> p g h c", h=H),
                                            ws[:, k, m * G:(m + 1) * G, :].unsqueeze(3).to_broadcast([P, G, H, D]),
                                            ALU.mult).then_inc(weighed, 1)
                        if n >= 1:
                            q = n - 1
                            k, m = divmod(q, NG)
                            v.wait_ge(weighed, grp(i, q) + 2)
                            v.tensor_reduce(sums.msg[:, k, :, m * G:(m + 1) * G].rearrange("p c g -> p g c"),
                                            prod[:, q % 2].rearrange("p g (h c) -> p g c h", h=H), X, ALU.add).then_inc(summed, 1)
                            if m == NG - 1:
                                v.wait_ge(summed, grp(i, q) + 2)
                                sums.scan(c, v, i, k)
                c.end(NCH // 2)
                sums.dve_end(c, v)


def gat_layer(nc, g, a, layer, h, out):
    with phase(nc) as s:
        g.layer = s
        gat_weights(nc, g, a, layer)
        loops = s.sb("loops", [P, NB, H])
        gat_loops(nc, g, h, loops)
        with phase(nc) as t:
            g.score = t.sb("score", [P, H, J])
            selfs = t.sb("selfs", [P, H, J])
            put_nodes(nc, g, h, loops)
            gat_scores(nc, g)
            spread_loops(nc, g, selfs)
            softmax(nc, g, H, selfs[:, :, :])
            gather_loop_weights(nc, g, selfs[:, :, :], loops)
            gat_sums(nc, g)
        with phase(nc) as t:
            xl, acc = t.sb("xl", [P, NB, 1, HD]), t.sb("acc", [P, NB, D])
            chain = t.sem("chain")
            node_sums(nc, g, acc)
            node_linear(nc, g, [h[:, :, :]], [g.wl[:, :]], xl)
            with nc.Block() as block:
                @block.vector
                def _(v):
                    c = Chain(v, chain)
                    flat = xl[:, :, 0, :]
                    c.link(v.tensor_tensor(flat, flat, g.bl[:, :].unsqueeze(1).to_broadcast([P, NB, HD]), ALU.add))
                    c.link(v.tensor_tensor(flat.rearrange("p b (h c) -> p b h c", h=H),
                                           flat.rearrange("p b (h c) -> p b h c", h=H),
                                           loops[:, :, :].unsqueeze(3).to_broadcast([P, NB, H, D]), ALU.mult))
                    for n in range(H):
                        c.link(v.tensor_tensor(acc[:, :, :], acc[:, :, :], xl[:, :, 0, n * D:(n + 1) * D], ALU.add))
                    c.link(v.tensor_tensor(acc[:, :, :], acc[:, :, :], g.bias[:, :].unsqueeze(1).to_broadcast([P, NB, D]), ALU.add))
                    c.link(v.tensor_scalar(out[:, :, :], acc[:, :, :], 0.0, None, ALU.max))


def build(nc, a, out):
    Space.used = {}
    g = Space(nc, ExitStack())

    def scratch(name, shape):
        return nc.dram_tensor(name, shape, f32, kind="Internal").ap()

    g.hpx = scratch("hpx", (NR * R, 2 * D))
    g.x_src = scratch("x_src", (EP, D))
    g.scanned = scratch("scanned", (EP + P, D))
    g.carry = scratch("carry", (P, D))
    g.table = scratch("table", (NR, D))
    g.adj = nc.dram_tensor("adj", (NT * P, NB * TC), bf16, kind="Internal").ap()
    g.step_rows, g.step_sums = scratch("step_rows", (S * WD, D)), scratch("step_sums", (S * WD, D))
    g.start_rows = scratch("start_rows", (EP + NR, D))
    g.table_self = scratch("table_self", (NR, H))
    g.start_self = scratch("start_self", (EP + NR, H))
    g.self_weight = scratch("self_weight", (EP + P, H))
    with g.ctx:
        g.pool_sems = [g.sem(f"pool_dma{n}") for n in range(4)]
        setup(nc, g, a)
        g.tail = g.sb("tail", [P, D])
        g.same, g.prefix = g.sb("same", [SP, SQ]), g.sb("prefix", [SP, SQ])
        g.hand = g.sb("hand", [SP, SP])
        g.last_step = g.sb("last_step", [NW // WD, NB // WD], i32)
        relation_table(nc, g, a)
        with phase(nc) as s:
            g.score = s.sb("score", [P, 1, J])
            with phase(nc) as t:
                g.hot = t
                adjacency(nc, g, a)
                relation_scores(nc, g, a)
            softmax(nc, g, 1)
            weighted_sums(nc, g)
        with phase(nc) as s:
            nbh = s.sb("nbh", [P, NB, D])
            node_sums(nc, g, nbh)
            relation_output(nc, g, a, nbh)
        with phase(nc) as s:
            y = s.sb("y", [P, NB, D])
            with phase(nc) as t:
                copied = t.sem("copied")
                with nc.Block() as block:
                    @block.vector
                    def _(v):
                        v.tensor_copy(y[:, :, :], g.x[:, :, :]).then_inc(copied, 1)
                        v.wait_ge(copied, 1)
            for _ in range(4):
                propagate(nc, g, y)
            add_norm(nc, g, [y[:, :, :]])
        g.row_start = g.sb("row_start", [P, D])
        g.row_self = g.sb("row_self", [P, H])
        put_nodes(nc, g, g.x)
        gated_convolution(nc, g, a)
        with phase(nc) as s:
            agg = s.sb("agg", [P, NB, D])
            node_sums(nc, g, agg)

            def gated(v, c):
                c.link(v.tensor_tensor(agg[:, :, :], agg[:, :, :], g.x[:, :, :], ALU.add))
                c.link(v.tensor_scalar(agg[:, :, :], agg[:, :, :], 0.0, None, ALU.max))

            add_norm(nc, g, [agg[:, :, :]], gated)
        with phase(nc) as s:
            h1 = s.sb("h1", [P, NB, D])
            gat_layer(nc, g, a, 1, g.x, h1)
            gat_layer(nc, g, a, 2, h1, h1)
            z, fc, bfc = s.sb("z_fc", [P, NB, 1, D]), s.sb("fc", [D, D]), s.sb("bfc", [P, D])
            loaded = s.sem("fc_loaded")
            with nc.Block() as block:
                @block.sync
                def _(sp):
                    sp.dma_start(fc[:, :], a["Wfc"]).then_inc(loaded, 16)
                    sp.dma_start(bfc[:, :], a["bfc"].partition_broadcast(P)).then_inc(loaded, 16)
                    sp.wait_ge(loaded, 32)
            node_linear(nc, g, [h1[:, :, :]], [fc[:, :]], z)
            add_norm(nc, g, [z[:, :, 0, :], bfc[:, :].unsqueeze(1).to_broadcast([P, NB, D])])
            stored = s.sem("out_stored")
            with nc.Block() as block:
                @block.sync
                def _(sp):
                    sp.dma_start(out.rearrange("(p b) d -> p b d", b=NB), g.x[0:N // NB, :, :]).then_inc(stored, 16)
                    sp.wait_ge(stored, 16)


_INS = {"x": "x", "src": "src", "dst": "dst", "et": "edge_type_32", "ea": "edge_attr_128", "ef": "edge_attr_64",
        "relw": "L0_gnn_relation_weight", "rw1": "L0_gnn_res_w1", "rw2": "L0_gnn_res_w2",
        "Wf": "L2_gnn_W_f", "bf": "L2_gnn_b_f", "Ws": "L2_gnn_W_s", "bs": "L2_gnn_b_s",
        "W1l": "L3_gnn_W1l", "b1l": "L3_gnn_b1l", "W1r": "L3_gnn_W1r", "b1r": "L3_gnn_b1r", "att1": "L3_gnn_att1",
        "bias1": "L3_gnn_bias1", "W2l": "L3_gnn_W2l", "b2l": "L3_gnn_b2l", "W2r": "L3_gnn_W2r", "b2r": "L3_gnn_b2r",
        "att2": "L3_gnn_att2", "bias2": "L3_gnn_bias2", "Wfc": "L3_gnn_Wfc", "bfc": "L3_gnn_bfc"}
_EDGES = {"src": 0, "dst": N, "et": 0, "ea": 0, "ef": 0}


def kernel(**inputs):
    import numpy as np
    import concourse.bacc as bacc
    from concourse.bass_utils import run_bass_kernel_spmd as run

    nc = bacc.Bacc("TRN2", target_bir_lowering=False, num_devices=1)
    arrays, args = {}, {}
    for short, name in _INS.items():
        v = np.ascontiguousarray(inputs[name])
        if short in _EDGES:
            pad = np.full((EP - E,) + v.shape[1:], _EDGES[short], v.dtype)
            v = np.concatenate([v, pad])
        arrays[f"in_{short}"] = v
        args[short] = nc.dram_tensor(f"in_{short}", v.shape, mybir.dt.from_np(v.dtype), kind="ExternalInput").ap()
    out = nc.dram_tensor("out_0", (N, D), f32, kind="ExternalOutput").ap()
    build(nc, args, out)
    r = run(nc, [arrays], core_ids=[0])
    return r.results[0]["out_0"]
```
